# Optimizing a Trainium2 kernel written in Bass

```python
import numpy as np
import jax
import jax.numpy as jnp

def _softmax(x, axis=-1):
    return jax.nn.softmax(x, axis=axis)

def _gelu(x):
    return jax.nn.gelu(x, approximate=True)

def _silu(x):
    return jax.nn.silu(x)

def _sigmoid(x):
    return jax.nn.sigmoid(x)

def _layernorm(x, axis=-1, eps=1e-05):
    m = jnp.mean(x, axis=axis, keepdims=True)
    v = jnp.var(x, axis=axis, keepdims=True)
    return (x - m) / jnp.sqrt(v + eps)

def _scatter_add(tgt, idx, src, axis=0):
    return tgt.at[idx].add(src)

def _segment_sum(src, seg, n):
    return jax.ops.segment_sum(src, seg, n)
kernel_name = 'mk_flamingo_gated_d2_seqx_r4_6a0ac6'

def setup_inputs(seed: int=0):
    np.random.seed(seed)
    _w = jnp.asarray

    def _rec_inputs():
        import jax
        import jax.numpy as jnp
        _rk = jax.random.key(seed)
        x = -0.0002928 + 1 * jax.random.normal(jax.random.fold_in(_rk, 1), (8, 512, 256), jnp.float32)
        _lenS = 512 - jax.random.randint(jax.random.fold_in(_rk, 7), (8,), 0, max(1, 512 // 4) + 1, jnp.int32)
        _lenS2 = 512 - jax.random.randint(jax.random.fold_in(_rk, 8), (8,), 0, max(1, 512 // 4) + 1, jnp.int32)
        _ctx_1024P = jax.random.normal(jax.random.fold_in(_rk, 11), (8, 16, 256), jnp.float32)
        _ctx_1024c = jax.random.dirichlet(jax.random.fold_in(_rk, 511), 0.3 * jnp.ones((16,), jnp.float32), (8, 512))
        _ctx_1024t = jnp.einsum('bsk,bkd->bsd', _ctx_1024c, _ctx_1024P)
        _ctx_1024t = _ctx_1024t * jax.lax.rsqrt(jnp.mean(jnp.square(_ctx_1024t)) + 1e-12) * 0.953939
        ctx_1024 = -1.39393e-06 + 0.999914 * (_ctx_1024t + 0.3 * jax.random.normal(jax.random.fold_in(_rk, 611), (8, 512, 256), jnp.float32))
        _validS = jnp.arange(512)[None, :] < _lenS[:, None]
        _validS2 = jnp.arange(512)[None, :] < _lenS2[:, None]
        _causal = jnp.tril(jnp.ones((512, 512), dtype=bool))
        mask_Bx1xS2_if1 = jnp.where(jnp.ones((8, 1, 512), dtype=bool), 1, 0).astype(jnp.int32)
        _g = jax.random.normal(jax.random.fold_in(_rk, 9001), (2, 2), jnp.float32)
        _g = jnp.sign(_g) * jnp.maximum(jnp.abs(_g), 1.0) + (_g == 0) * 1.0
        g_xattn = _g[0]
        g_ffn = _g[1]
        return (x, ctx_1024, mask_Bx1xS2_if1, g_xattn, g_ffn)
    x, ctx_1024, mask_Bx1xS2_if1, g_xattn, g_ffn = _rec_inputs()

    def _L0_xattn_setup():
        import jax, jax.numpy as jnp
        import numpy as np
        import math
        H = 16
        D_MODEL = 256
        D_K = D_MODEL // H

        def _split_heads(x, B, S):
            return x.reshape(B, S, H, D_K).transpose(0, 2, 1, 3)
        key = jax.random.key(seed)
        ks = jax.random.split(key, 12)
        B, S, D = (2, 512, D_MODEL)
        s = 1.0 / math.sqrt(D)
        inp = {'query': jax.random.normal(ks[0], (B, S, D), jnp.float32), 'key': jax.random.normal(ks[1], (B, S, D), jnp.float32), 'value': jax.random.normal(ks[2], (B, S, D), jnp.float32), 'mask': jnp.ones((B, 1, S), jnp.int32), 'wq': jax.random.normal(ks[3], (D, D), jnp.float32) * s, 'bq': jnp.zeros((D,), jnp.float32), 'wk': jax.random.normal(ks[4], (D, D), jnp.float32) * s, 'bk': jnp.zeros((D,), jnp.float32), 'wv': jax.random.normal(ks[5], (D, D), jnp.float32) * s, 'bv': jnp.zeros((D,), jnp.float32), 'wo': jax.random.normal(ks[6], (D, D), jnp.float32) * s, 'bo': jnp.zeros((D,), jnp.float32)}
        return inp
    _L0_xattn_all = _L0_xattn_setup()
    _L0_xattn_in = {k: v for k, v in _L0_xattn_all.items() if k in ('wq', 'bq', 'wk', 'bk', 'wv', 'bv', 'wo', 'bo')}
    del _L0_xattn_all

    def _L0_ffn_setup():
        import jax, jax.numpy as jnp
        import numpy as np
        TOP_K = 2
        CAP_FACTOR = 1.25
        EPS = 1.1920929e-07
        key = jax.random.key(seed)
        ks = jax.random.split(key, 6)
        B, S, D, E, H = (8, 512, 256, 8, 1024)
        return {'hidden_states': jax.random.normal(ks[0], (B, S, D), jnp.float32), 'wg': jax.random.normal(ks[1], (D, E), jnp.float32) * 0.02, 'fc1_w': jax.random.normal(ks[2], (E, H, D), jnp.float32) * 0.02, 'fc1_b': jnp.zeros((E, H), jnp.float32), 'fc2_w': jax.random.normal(ks[3], (E, H, D), jnp.float32) * 0.02, 'fc2_b': jnp.zeros((E, D), jnp.float32), 'ln_gamma': jnp.ones((D,), jnp.float32), 'ln_beta': jnp.zeros((D,), jnp.float32)}
    _L0_ffn_all = _L0_ffn_setup()
    _L0_ffn_in = {k: v for k, v in _L0_ffn_all.items() if k in ('wg', 'fc1_w', 'fc1_b', 'fc2_w', 'fc2_b', 'ln_gamma', 'ln_beta')}
    del _L0_ffn_all

    def _L1_xattn_setup():
        import jax, jax.numpy as jnp
        import numpy as np
        R = 16

        def _split_heads(x, r):
            B, T, D = x.shape
            return x.reshape(B, T, r, D // r).transpose(0, 2, 1, 3)
        key = jax.random.key(seed)
        ks = jax.random.split(key, 6)
        B, T, D = (2, 512, 256)
        s = 1.0 / np.sqrt(D)
        return {'q': jax.random.normal(ks[0], (B, T, D), jnp.float32), 'k': jax.random.normal(ks[1], (B, T, D), jnp.float32), 'q_map': jax.random.normal(ks[2], (D, D), jnp.float32) * s, 'k_map': jax.random.normal(ks[3], (D, D), jnp.float32) * s, 'v_map': jax.random.normal(ks[4], (D, D), jnp.float32) * s, 'output_map': jax.random.normal(ks[5], (D, D), jnp.float32) * s}
    _L1_xattn_all = _L1_xattn_setup()
    _L1_xattn_in = {k: v for k, v in _L1_xattn_all.items() if k in ('q_map', 'k_map', 'v_map', 'output_map')}
    del _L1_xattn_all

    def _L1_ffn_setup():
        import jax, jax.numpy as jnp
        import numpy as np
        FP8_E4M3_MAX = 448.0

        def fake_quant_fp8(t):
            amax = jnp.max(jnp.abs(t))
            scale = FP8_E4M3_MAX / jnp.maximum(amax, 1e-12)
            q = (t * scale).astype(jnp.float8_e4m3fn).astype(jnp.float32)
            return q / scale
        key = jax.random.key(seed)
        k1, k2, k3 = jax.random.split(key, 3)
        d_in, d_out = (256, 256)
        x = jax.random.normal(k1, (4, 2048, d_in), dtype=jnp.float32)
        weight = jax.random.normal(k2, (d_out, d_in), dtype=jnp.float32) * (1.0 / np.sqrt(d_in))
        bias = jax.random.normal(k3, (d_out,), dtype=jnp.float32) * 0.01
        return {'x': x, 'weight': weight, 'bias': bias}
    _L1_ffn_all = _L1_ffn_setup()
    _L1_ffn_in = {k: v for k, v in _L1_ffn_all.items() if k in ('weight', 'bias')}
    del _L1_ffn_all
    return {'x': x, 'ctx_1024': ctx_1024, 'mask_Bx1xS2_if1': mask_Bx1xS2_if1, 'g_xattn': g_xattn, 'g_ffn': g_ffn, 'L0_xattn_wq': _L0_xattn_in['wq'], 'L0_xattn_bq': _L0_xattn_in['bq'], 'L0_xattn_wk': _L0_xattn_in['wk'], 'L0_xattn_bk': _L0_xattn_in['bk'], 'L0_xattn_wv': _L0_xattn_in['wv'], 'L0_xattn_bv': _L0_xattn_in['bv'], 'L0_xattn_wo': _L0_xattn_in['wo'], 'L0_xattn_bo': _L0_xattn_in['bo'], 'L0_ffn_wg': _L0_ffn_in['wg'], 'L0_ffn_fc1_w': _L0_ffn_in['fc1_w'], 'L0_ffn_fc1_b': _L0_ffn_in['fc1_b'], 'L0_ffn_fc2_w': _L0_ffn_in['fc2_w'], 'L0_ffn_fc2_b': _L0_ffn_in['fc2_b'], 'L0_ffn_ln_gamma': _L0_ffn_in['ln_gamma'], 'L0_ffn_ln_beta': _L0_ffn_in['ln_beta'], 'L1_xattn_q_map': _L1_xattn_in['q_map'], 'L1_xattn_k_map': _L1_xattn_in['k_map'], 'L1_xattn_v_map': _L1_xattn_in['v_map'], 'L1_xattn_output_map': _L1_xattn_in['output_map'], 'L1_ffn_weight': _L1_ffn_in['weight'], 'L1_ffn_bias': _L1_ffn_in['bias']}

def reference(x, ctx_1024, mask_Bx1xS2_if1, g_xattn, g_ffn, L0_xattn_wq, L0_xattn_bq, L0_xattn_wk, L0_xattn_bk, L0_xattn_wv, L0_xattn_bv, L0_xattn_wo, L0_xattn_bo, L0_ffn_wg, L0_ffn_fc1_w, L0_ffn_fc1_b, L0_ffn_fc2_w, L0_ffn_fc2_b, L0_ffn_ln_gamma, L0_ffn_ln_beta, L1_xattn_q_map, L1_xattn_k_map, L1_xattn_v_map, L1_xattn_output_map, L1_ffn_weight, L1_ffn_bias):
    import jax
    import jax.numpy as jnp

    def _L0_xattn_ref(query, key, value, mask, wq, bq, wk, bk, wv, bv, wo, bo):
        import jax, jax.numpy as jnp
        import numpy as np
        import math
        H = 16
        D_MODEL = 256
        D_K = D_MODEL // H

        def _split_heads(x, B, S):
            return x.reshape(B, S, H, D_K).transpose(0, 2, 1, 3)
        B, S, D = query.shape
        q = _split_heads(query @ wq.T + bq, B, S)
        k = _split_heads(key @ wk.T + bk, B, S)
        v = _split_heads(value @ wv.T + bv, B, S)
        scores = jnp.einsum('bhqd,bhkd->bhqk', q, k) / math.sqrt(D_K)
        m = mask[:, None, :, :]
        scores = jnp.where(m == 0, jnp.float32(-1000000000.0), scores)
        p_attn = jax.nn.softmax(scores, axis=-1)
        x = jnp.einsum('bhqk,bhkd->bhqd', p_attn, v)
        x = x.transpose(0, 2, 1, 3).reshape(B, S, D)
        return x @ wo.T + bo

    def _L0_ffn_ref(hidden_states, wg, fc1_w, fc1_b, fc2_w, fc2_b, ln_gamma, ln_beta):
        import jax, jax.numpy as jnp
        import numpy as np
        TOP_K = 2
        CAP_FACTOR = 1.25
        EPS = 1.1920929e-07
        B, S, D = hidden_states.shape
        E = wg.shape[1]
        N = B * S
        k = TOP_K
        C = k * int(CAP_FACTOR * ((N + E - 1) // E))
        x = hidden_states.reshape(N, D)
        scores = jax.nn.softmax(x @ wg, axis=-1)
        gates, idx = jax.lax.top_k(scores, k)
        gates = gates / jnp.clip(jnp.sum(gates, -1, keepdims=True), EPS)
        masks = jax.nn.one_hot(idx, E, dtype=jnp.int32)
        counts = masks.sum(0)
        offsets = jnp.concatenate([jnp.zeros((1, E), jnp.int32), jnp.cumsum(counts, 0)[:-1]], 0)
        loc = jnp.cumsum(masks, 0) - 1 + offsets[None]
        loc_sel = (loc * masks).sum(-1)
        keep = loc_sel < C
        gates = gates * keep.astype(gates.dtype)
        pos = jnp.where(keep, idx * C + loc_sel, E * C)
        xk = jnp.broadcast_to(x[:, None, :], (N, k, D)).reshape(N * k, D)
        buf = jnp.zeros((E * C + 1, D), x.dtype).at[pos.reshape(-1)].set(xk)
        disp = buf[:E * C].reshape(E, C, D)
        h = jax.nn.silu(jnp.einsum('ecd,ehd->ech', disp, fc1_w) + fc1_b[:, None, :])
        y = jnp.einsum('ech,ehd->ecd', h, fc2_w) + fc2_b[:, None, :]
        ybuf = jnp.concatenate([y.reshape(E * C, D), jnp.zeros((1, D), y.dtype)], 0)
        combined = jnp.sum(gates[..., None] * ybuf[pos], axis=1)
        res = hidden_states + combined.reshape(B, S, D)
        mu = jnp.mean(res, -1, keepdims=True)
        var = jnp.var(res, -1, keepdims=True)
        return (res - mu) * jax.lax.rsqrt(var + 1e-05) * ln_gamma + ln_beta

    def _L1_xattn_ref(q, k, q_map, k_map, v_map, output_map):
        import jax, jax.numpy as jnp
        import numpy as np
        R = 16

        def _split_heads(x, r):
            B, T, D = x.shape
            return x.reshape(B, T, r, D // r).transpose(0, 2, 1, 3)
        B, Tq, D = q.shape
        dh = D // R
        qh = _split_heads(q @ q_map, R)
        kh = _split_heads(k @ k_map, R)
        vh = _split_heads(k @ v_map, R)
        scale = 1.0 / jnp.sqrt(jnp.asarray(dh, qh.dtype))
        scores = jnp.einsum('brqd,brkd->brqk', qh, kh) * scale
        weights = jax.nn.softmax(scores, axis=-1)
        out = jnp.einsum('brqk,brkd->brqd', weights, vh)
        merged = out.transpose(0, 2, 1, 3).reshape(B, Tq, D)
        return merged @ output_map

    def _L1_ffn_ref(x, weight, bias):
        import jax, jax.numpy as jnp
        import numpy as np
        FP8_E4M3_MAX = 448.0

        def fake_quant_fp8(t):
            amax = jnp.max(jnp.abs(t))
            scale = FP8_E4M3_MAX / jnp.maximum(amax, 1e-12)
            q = (t * scale).astype(jnp.float8_e4m3fn).astype(jnp.float32)
            return q / scale
        xq = fake_quant_fp8(x)
        wq = fake_quant_fp8(weight)
        return jnp.einsum('bsd,od->bso', xq, wq) + bias
    x = x + jnp.tanh(g_xattn[0]) * _L0_xattn_ref(_layernorm(x, axis=-1), ctx_1024, ctx_1024, mask_Bx1xS2_if1, L0_xattn_wq, L0_xattn_bq, L0_xattn_wk, L0_xattn_bk, L0_xattn_wv, L0_xattn_bv, L0_xattn_wo, L0_xattn_bo)
    x = x + jnp.tanh(g_ffn[0]) * _L0_ffn_ref(_layernorm(x, axis=-1), L0_ffn_wg, L0_ffn_fc1_w, L0_ffn_fc1_b, L0_ffn_fc2_w, L0_ffn_fc2_b, L0_ffn_ln_gamma, L0_ffn_ln_beta)
    x = x + jnp.tanh(g_xattn[1]) * _L1_xattn_ref(_layernorm(x, axis=-1), ctx_1024, L1_xattn_q_map, L1_xattn_k_map, L1_xattn_v_map, L1_xattn_output_map)
    x = x + jnp.tanh(g_ffn[1]) * _L1_ffn_ref(_layernorm(x, axis=-1), L1_ffn_weight, L1_ffn_bias)
    return x

_drawn_inputs = setup_inputs


def setup_inputs(seed=0):
    import zlib

    import numpy as np

    out = dict(_drawn_inputs(seed))
    spreads = {'g_ffn': (-1.0, 0.2),
     'L0_xattn_bq': (0.0, 0.274),
     'L0_xattn_bk': (0.0, 0.8),
     'L0_xattn_bv': (0.0, 0.1),
     'L0_xattn_bo': (0.0, 0.1),
     'L0_ffn_fc1_b': (0.0, 0.1),
     'L0_ffn_fc2_b': (0.0, 0.1),
     'L0_ffn_ln_gamma': (1.0, 0.2),
     'L0_ffn_ln_beta': (0.0, 0.1)}
    factors = {'L1_ffn_bias': 7.086}
    for name, (base, spread) in spreads.items():
        noise = np.random.default_rng([zlib.crc32(name.encode()), seed]).standard_normal(out[name].shape)
        drawn = base * np.exp(spread * noise) if base else spread * noise
        out[name] = jnp.asarray(drawn.astype(out[name].dtype))
    for name, factor in factors.items():
        out[name] = (out[name] * factor).astype(out[name].dtype)
    return out
```

```python
from contextlib import ExitStack

import concourse.bass as bass
from concourse import mybir

F32 = mybir.dt.float32
BF16 = mybir.dt.bfloat16
I32 = mybir.dt.int32
U32 = mybir.dt.uint32
ACT = mybir.ActivationFunctionType
ALU = mybir.AluOpType
AX = mybir.AxisListType
ds = bass.ds

P = 128
B, SEQ, D = 8, 512, 256
TPB = SEQ // P
NT = B * TPB
N = B * SEQ
KD = D // P
H, DH = 16, 16
G, HG = 4, 4
E, FF = 8, 1024
KF = FF // P
CAP = 2 * int(1.25 * ((N + E - 1) // E))
CHUNK = 256
NCH = CAP // CHUNK
VW = DH + 1
Q_PARTS = (0, 1, 2, 0, 1, 0)
K_PARTS = (0, 0, 0, 1, 1, 2)
PARTS_ROWS = 6 * DH
MAX_ROWS = PARTS_ROWS + 3
ALL_ROWS = MAX_ROWS + 3
FP8_MAX = 448.0


class Shared:
    pass


class NormBuffers:
    def __init__(self, sb, n=""):
        self.stats, self.mv = sb(f"stats{n}", [P, TPB, 6]), sb(f"mv{n}", [P, TPB, 2])
        self.var, self.rstd = sb(f"var{n}", [P, TPB]), sb(f"rstd{n}", [P, TPB])


def need(e, sem, value):
    if not isinstance(value, int) or value > 0:
        e.wait_ge(sem, value)


def loop(e, n):
    def run(body):
        body(0)
        with e.Fori(1, n) as i:
            body(i)
    return run


class Chain:

    def __init__(self, sem, per=0):
        self.sem, self.per, self.base, self.k = sem, per, 0, 0

    def begin(self, i):
        self.i, self.k = i, 0

    def end(self):
        assert self.k == self.per, (self.sem, self.k, self.per)

    def did(self, ins):
        ins.then_inc(self.sem, 1)
        self.k += 1
        return self.k

    def wait(self, eng, k=None):
        k = self.k if k is None else k
        need(eng, self.sem, self.i * self.per + k)


def build(nc, a, out, stop=99):
    ctx = ExitStack()
    with ctx:
        S = Shared()
        S.nc, S.a, S.out, S.w = nc, a, out, {}
        S.sem = lambda name: ctx.enter_context(nc.semaphore(name))
        S.stage_sems, S.sems_ctx = [], ExitStack()

        S.gates = S.sem("gates")

        def sb(name, shape, dt=F32):
            return ctx.enter_context(nc.sbuf_tensor(name, shape, dt))

        def dram(name, shape, dt=F32):
            return nc.dram_tensor(name, shape, dt).ap()

        ctx.enter_context(nc.allow_non_contiguous_dma(reason="small vectors, head-wise rows"))
        S.X = sb("X", [P, NT, D])
        S.BIG = sb("BIG", [P, NT, D])
        S.ident = sb("ident", [P, P])
        S.identb = sb("identb", [P, P], BF16)
        S.onesb = sb("onesb", [P, P], BF16)
        S.triu = sb("triu", [P, P], BF16)
        S.onesrow = sb("onesrow", [1, P])
        S.iota8 = sb("iota8", [P, 2 * E])
        S.half = sb("half", [P, TPB])
        S.tg = sb("tg", [P, 4])
        for w in ("wq0", "wk0", "wv0", "wo0", "wq1", "wk1", "wv1", "wo1"):
            S.w[w] = sb(w, [P, KD, D])
        S.w["wg"] = sb("wg", [P, KD, E])
        S.w["bq"] = sb("bq", [P, KD])
        S.w["bk"] = sb("bk", [P, KD])
        for w in ("bv_b", "bo_b", "gamma_b", "beta_b", "fb_b"):
            S.w[w] = sb(w, [P, D])
        S.b1T = sb("b1T", [P, E * KF])
        S.idx = sb("idx", [P, 2, NT])
        S.gate = sb("gate", [P, 2, NT])
        S.onehot = sb("onehot", [P, 2 * E, NT], BF16)
        S.row_put = sb("row_put", [P, 2, NT], I32)
        S.row_get = sb("row_get", [P, 2, NT], I32)
        S.amax = sb("amax", [P, B])
        S.qs = [dram(f"qs{l}", (3, D, N), BF16) for l in range(2)]
        S.ks = [dram(f"ks{l}", (3, D, N), BF16) for l in range(2)]
        S.vs = [dram(f"vs{l}", (N, H * VW)) for l in range(2)]
        S.mrows = [dram(f"mrows{l}", (3, N), BF16) for l in range(2)]
        S.disp = dram("disp", (E * CAP + 2 * N, D))
        S.ybuf = dram("ybuf", (E * CAP + P, D))

        stages = [setup, project, lambda S: attention(S, 0), route, place, recycle, experts, combine,
                  lambda S: attention(S, 1), merge, quantise]
        for n, stage in enumerate(stages):
            if n < stop:
                stage(S)
        S.sems_ctx.close()


def scope(S, n):
    ctx = ExitStack()
    nc = S.nc
    return (ctx, lambda name, shape, dt=F32: ctx.enter_context(nc.sbuf_tensor(f"{n}_{name}", shape, dt)),
            lambda name, shape, dt=F32: ctx.enter_context(nc.psum_tensor(f"{n}_{name}", shape, dt)),
            lambda name, keep=False: S.sem(f"{n}_{name}") if keep else stage_sem(S, f"{n}_{name}"))


def stage_sem(S, name):
    S.stage_sems.append(S.sems_ctx.enter_context(S.nc.semaphore(name)))
    return S.stage_sems[-1]


def recycle(S):
    with S.nc.Block() as block:
        @block.gpsimd
        def _(e):
            for sem in S.stage_sems:
                e.sem_clear(sem)
    S.sems_ctx.close()
    S.stage_sems, S.sems_ctx = [], ExitStack()


def setup(S):
    nc, a = S.nc, S.a
    ctx, sb, ps, sem = scope(S, "s")
    with ctx:
        raw = [sb(f"raw{j}", [P, KD, D]) for j in range(4)]
        b1raw = sb("b1raw", [E * KF, P])
        mi = sb("mi", [B, SEQ], I32)
        mf = sb("mf", [B, 3, SEQ])
        mparts = sb("mparts", [B, 3, SEQ], BF16)
        mzero = sb("mzero", [B, 3, SEQ], BF16)
        zrow = sb("zrow", [P, 4096])
        gl = sb("gl", [P, 4])
        pw = [ps(f"pw{j}", [P, KD, KD, P]) for j in range(4)]
        pb = ps("pb", [P, E * KF])
        ld_raw, ld, ld_mask, ld_g = sem("ld_raw"), sem("ld"), sem("ld_mask"), sem("ld_g")
        id0, idd, tr, ev, vc, st = sem("id0"), sem("idd"), sem("tr"), sem("ev"), sem("vc"), sem("st")
        zs, zst = sem("zs"), sem("zst", keep=True)

        with nc.Block() as block:
            @block.sync
            def _(e):
                for j, w in enumerate(("L0_xattn_wq", "L0_xattn_wk", "L0_xattn_wv", "L0_xattn_wo")):
                    e.dma_start(raw[j][:, :, :], a[w].rearrange("(t p) c -> p t c", p=P)).then_inc(ld_raw, 16)
                e.dma_start(b1raw[:, :], a["L0_ffn_fc1_b"].rearrange("e (j p) -> (e j) p", p=P)).then_inc(ld_raw, 16)
                e.dma_start(mi[:, :], a["mask_Bx1xS2_if1"][:, 0, :]).then_inc(ld_mask, 16)
                e.dma_start(gl[:, 0:2], a["g_xattn"].rearrange("(o n) -> o n", o=1).broadcast_to([P, 2])).then_inc(ld_g, 16)
                e.dma_start(gl[:, 2:4], a["g_ffn"].rearrange("(o n) -> o n", o=1).broadcast_to([P, 2])).then_inc(ld_g, 16)
                n = 0
                for w, src in (("wq1", "L1_xattn_q_map"), ("wk1", "L1_xattn_k_map"),
                               ("wv1", "L1_xattn_v_map"), ("wo1", "L1_xattn_output_map"), ("wg", "L0_ffn_wg")):
                    e.dma_start(S.w[w][:, :, :], a[src].rearrange("(k p) o -> p k o", p=P)).then_inc(ld, 16)
                    n += 1
                for w, src in (("bq", "L0_xattn_bq"), ("bk", "L0_xattn_bk")):
                    e.dma_start(S.w[w][:, :], a[src].rearrange("(k p) -> p k", p=P)).then_inc(ld, 16)
                    n += 1
                for w, src in (("bv_b", "L0_xattn_bv"), ("bo_b", "L0_xattn_bo"), ("gamma_b", "L0_ffn_ln_gamma"),
                               ("beta_b", "L0_ffn_ln_beta"), ("fb_b", "L1_ffn_bias")):
                    e.dma_start(S.w[w][:, :],
                                a[src].rearrange("(o n) -> o n", o=1).broadcast_to([P, D])).then_inc(ld, 16)
                    n += 1
                need(e, vc, 8)
                e.dma_start(S.mrows[0].rearrange("s (b t) -> b s t", b=B), mparts[:, :, :]).then_inc(st, 16)
                e.dma_start(S.mrows[1].rearrange("s (b t) -> b s t", b=B), mzero[:, :, :]).then_inc(st, 16)
                need(e, ld, 16 * n)
                need(e, st, 32)

            @block.gpsimd
            def _(e):
                e.memset(S.ident[:, :], 0.0).then_inc(id0, 1)
                e.memset(S.onesb[:, :], 1.0).then_inc(id0, 1)
                e.memset(S.half[:, :], -0.5).then_inc(idd, 1)
                e.memset(S.onesrow[:, :], 1.0).then_inc(idd, 1)
                e.memset(zrow[:, :], 0.0).then_inc(zs, 1)
                need(e, id0, 2)
                e.affine_select(out=S.ident[:, :], in_=S.ident[:, :], compare_op=ALU.not_equal, fill=1.0,
                                base=0, pattern=[[-1, P]], channel_multiplier=1).then_inc(idd, 1)
                e.affine_select(out=S.triu[:, :], in_=S.onesb[:, :], compare_op=ALU.is_ge, fill=0.0,
                                base=0, pattern=[[1, P]], channel_multiplier=-1).then_inc(idd, 1)
                e.iota(S.iota8[:, :], pattern=[[0, 2], [1, E]], base=0, channel_multiplier=0,
                       allow_small_or_imprecise_dtypes=True).then_inc(idd, 1)
                need(e, zs, 1)
                rows = E * CAP // P
                for j in range(rows // 16):
                    e.dma_start(S.disp[j * 16 * P:(j + 1) * 16 * P, :].rearrange("(p r) d -> p (r d)", p=P),
                                zrow[:, :]).then_inc(zst, 16)
                e.dma_start(S.ybuf[E * CAP:E * CAP + P, :], zrow[:, 0:D]).then_inc(zst, 16)
                S.cleared = (zst, 16 * (rows // 16 + 1))

            @block.tensor
            def _(e):
                need(e, idd, 5)
                need(e, ld_raw, 80)
                for j in range(4):
                    for k in range(KD):
                        for t in range(KD):
                            e.transpose(pw[j][:, k, t, :], raw[j][:, t, k * P:(k + 1) * P], S.ident[:, :]).then_inc(tr, 1)
                e.transpose(pb[:, :], b1raw[:, :], S.ident[0:E * KF, 0:E * KF]).then_inc(tr, 1)

            @block.scalar
            def _(e):
                need(e, ld_g, 32)
                e.activation(S.tg[:, :], gl[:, :], ACT.Tanh).then_inc(ev, 1)
                for j, w in enumerate(("wq0", "wk0", "wv0", "wo0")):
                    need(e, tr, 4 * j + 4)
                    e.activation(S.w[w][:, :, :], pw[j][:, :, :, :], ACT.Copy).then_inc(ev, 1)
                need(e, tr, 17)
                e.activation(S.b1T[:, :], pb[:, :], ACT.Copy).then_inc(ev, 1)

            @block.vector
            def _(e):
                c = Chain(vc)
                c.begin(0)
                c.did(e.memset(mzero[:, :, :], 0.0))
                need(e, ld_mask, 16)
                c.did(e.tensor_scalar(mf[:, 0, :], mi[:, :], 0.0, -1.0, ALU.not_equal, ALU.add))
                c.wait(e)
                c.did(e.tensor_scalar(mf[:, 1, :], mf[:, 0, :], 1.0e9, None, ALU.mult))
                c.wait(e)
                split3(e, c, mf[:, 1, :], mf[:, 2, :], mparts[:, 0, :], mparts[:, 1, :], mparts[:, 2, :])
                need(e, idd, 5)
                c.did(e.tensor_copy(S.identb[:, :], S.ident[:, :]))


def split3(e, c, src, rest, p0, p1, p2):
    c.did(e.tensor_copy(p0, src))
    c.wait(e)
    c.did(e.tensor_tensor(rest, src, p0, ALU.subtract))
    c.wait(e)
    c.did(e.tensor_copy(p1, rest))
    c.wait(e)
    c.did(e.tensor_tensor(p2, rest, p1, ALU.subtract))


def norm_vector(S, e, c, nb, src, dst, ready, rstd_ready, i):
    gate(S, e)
    for t in range(TPB):
        c.did(e.bn_stats(nb.stats[:, t, :], src[:, t, :]))
    c.wait(e)
    gate(S, e)
    for t in range(TPB):
        ins = e.bn_aggr(nb.mv[:, t, :], nb.stats[:, t, :])
        if t < TPB - 1:
            c.did(ins)
    ins.then_inc(ready, 1)
    need(e, rstd_ready, i + 1)
    need(e, ready, i + 1)
    c.wait(e)
    for t in range(TPB):
        c.did(e.tensor_scalar(dst[:, t, :], src[:, t, :], nb.mv[:, t, 0:1], nb.rstd[:, t:t + 1],
                              ALU.subtract, ALU.mult))


NORM_STEPS = 3 * TPB - 1


def norm_gpsimd(S, e, nb, ready, own, rstd_ready, i):
    need(e, ready, i + 1)
    gate(S, e)
    e.tensor_scalar(nb.var[:, :], nb.mv[:, :, 1], 1e-5, None, ALU.add).then_inc(own, 1)
    need(e, own, i + 1)
    e.tensor_tensor(nb.rstd[:, :], nb.var[:, :], S.half[:, :], ALU.pow).then_inc(rstd_ready, 1)


def gate(S, e):
    e.sem_inc(S.gates, 1)


def project(S):
    nc, a = S.nc, S.a
    ctx, sb, ps, sem = scope(S, "p")
    with ctx:
        cin = sb("cin", [P, TPB, D])
        cT = sb("cT", [P, KD, SEQ])
        hn = sb("hn", [P, TPB, D])
        hT = sb("hT", [P, KD, SEQ])
        mi = sb("mi", [P, SEQ], I32)
        mb = sb("mb", [P, SEQ])
        bq4 = sb("bq4", [P, KD])
        nb = NormBuffers(sb)
        jobs = ("k0", "k1", "q0")
        full = {j: sb(f"full_{j}", [P, KD, SEQ]) for j in jobs}
        rest = {j: sb(f"rest_{j}", [P, KD, SEQ]) for j in jobs}
        parts = {j: sb(f"parts_{j}", [P, 3, KD, SEQ], BF16) for j in jobs}
        va = [sb(f"va{l}", [P, TPB, H, VW]) for l in range(2)]
        pT = [ps(f"pT{j}", [P, KD, SEQ]) for j in range(2)]
        pJ = [ps(f"pJ{j}", [P, KD, SEQ]) for j in range(2)]
        pV = pJ[1][:, :, :].rearrange("p k (t o) -> p (k t) o", o=D)
        one, ld_x, ld_c, ld_m = sem("one"), sem("ld_x"), sem("ld_c"), sem("ld_m")
        trc, trh, cte, hte, mke, norm = (sem(x) for x in ("trc", "trh", "cte", "hte", "mke", "norm"))
        mvr, pown, rsr, vc = sem("mvr"), sem("pown"), sem("rsr"), sem("vc")
        pj = {j: sem(f"pj_{j}") for j in ("k0", "k1", "q0", "v0", "v1")}
        stp = {j: sem(f"stp_{j}") for j in jobs}
        vev = [sem(f"vev{l}") for l in range(2)]
        kst = {j: sem(f"kst_{j}") for j in ("k0", "k1", "q0", "v0", "v1")}
        FULL, P0, REST, P1, P2 = KD, KD + 1, KD + 2, KD + 3, KD + 4
        dst = {"k0": S.ks[0], "k1": S.ks[1], "q0": S.qs[0]}
        w = {"k0": S.w["wk0"], "k1": S.w["wk1"], "q0": S.w["wq0"], "v0": S.w["wv0"], "v1": S.w["wv1"]}

        def load(e, b):
            need(e, trc, b)
            e.dma_start(cin[:, :, :], a["ctx_1024"][ds(b, 1), :, :].rearrange("o (t p) c -> p (o t) c", p=P)).then_inc(ld_c, 16)
            need(e, mke, b)
            e.dma_start(mi[:, :], a["mask_Bx1xS2_if1"][ds(b, 1), 0, :].broadcast_to([P, SEQ])).then_inc(ld_m, 16)
            need(e, ld_x, 16 * b)
            e.dma_start(S.X[:, ds(b * TPB, TPB), :], a["x"][ds(b, 1), :, :].rearrange("o (t p) c -> p (o t) c", p=P)).then_inc(ld_x, 16)

        def store(e, b):
            for j in ("k0", "v0", "k1", "v1", "q0"):
                if j[0] == "v":
                    l = int(j[1])
                    need(e, vev[l], b + 1)
                    e.dma_start(S.vs[l][ds(b * SEQ, SEQ), :].rearrange("(t p) c -> p t c", p=P),
                                va[l][:, :, :, :].rearrange("p t h c -> p t (h c)")).then_inc(kst[j], 16)
                else:
                    need(e, stp[j], b * P2 + P2)
                    for s in range(3):
                        e.dma_start(dst[j][s, :, ds(b * SEQ, SEQ)].rearrange("(t p) c -> p t c", p=P),
                                    parts[j][:, s, :, :]).then_inc(kst[j], 16)

        with nc.Block() as block:
            @block.sync
            def _(e):
                load(e, 0)
                @loop(e, B - 1)
                def _(b):
                    load(e, b + 1)
                    store(e, b)
                store(e, B - 1)
                for j in ("k0", "k1", "q0"):
                    need(e, kst[j], 48 * B)
                for j in ("v0", "v1"):
                    need(e, kst[j], 16 * B)

            @block.tensor
            def _(e):
                def product(j, b, src, out):
                    for t in range(KD):
                        for k in range(KD):
                            last = e.matmul(out[:, t, :], w[j][:, k, t * P:(t + 1) * P], src[:, k, :],
                                            start=(k == 0), stop=(k == KD - 1))
                    last.then_inc(pj[j], 1)

                def values(j, b, src):
                    for t in range(TPB):
                        for k in range(KD):
                            last = e.matmul(pV[:, t, :], src[:, k, t * P:(t + 1) * P], w[j][:, k, :],
                                            start=(k == 0), stop=(k == KD - 1))
                    last.then_inc(pj[j], 1)

                @loop(e, B)
                def _(b):
                    need(e, ld_c, 16 * b + 16)
                    need(e, cte, b)
                    for k in range(KD):
                        for t in range(TPB):
                            last = e.transpose(pT[0][:, k, t * P:(t + 1) * P], cin[:, t, k * P:(k + 1) * P], S.ident[:, :])
                    last.then_inc(trc, 1)
                    need(e, cte, b + 1)
                    need(e, stp["q0"], b * P2)
                    product("k0", b, cT, pJ[0])
                    need(e, vev[1], b)
                    values("v0", b, cT)
                    need(e, stp["k0"], b * P2 + FULL)
                    product("k1", b, cT, pJ[0])
                    need(e, vev[0], b + 1)
                    values("v1", b, cT)
                    need(e, norm, (b + 1) * NORM_STEPS)
                    need(e, hte, b)
                    for k in range(KD):
                        for t in range(TPB):
                            last = e.transpose(pT[1][:, k, t * P:(t + 1) * P], hn[:, t, k * P:(k + 1) * P], S.ident[:, :])
                    last.then_inc(trh, 1)
                    need(e, hte, b + 1)
                    need(e, stp["k1"], b * P2 + FULL)
                    product("q0", b, hT, pJ[0])

            @block.gpsimd
            def _(e):
                @loop(e, B)
                def _(b):
                    norm_gpsimd(S, e, nb, mvr, pown, rsr, b)

            @block.scalar
            def _(e):
                e.activation(bq4[:, :], S.w["bq"][:, :], ACT.Copy, scale=0.25).then_inc(one, 1)
                need(e, one, 2)
                @loop(e, B)
                def _(b):
                    need(e, trc, b + 1)
                    need(e, pj["v1"], b)
                    e.activation(cT[:, :, :], pT[0][:, :, :], ACT.Copy).then_inc(cte, 1)

                    def casts(j):
                        need(e, stp[j], b * P2 + FULL)
                        need(e, kst[j], 48 * b)
                        e.activation(parts[j][:, 0, :, :], full[j][:, :, :], ACT.Copy).then_inc(stp[j], 1)
                        need(e, stp[j], b * P2 + REST)
                        e.activation(parts[j][:, 1, :, :], rest[j][:, :, :], ACT.Copy).then_inc(stp[j], 1)

                    casts("k0")
                    need(e, pj["k1"], b + 1)
                    need(e, stp["k1"], b * P2)
                    for t in range(KD):
                        e.activation(full["k1"][:, t, :], pJ[0][:, t, :], ACT.Copy).then_inc(stp["k1"], 1)
                    casts("k1")
                    need(e, pj["v1"], b + 1)
                    need(e, kst["v1"], 16 * b)
                    e.activation(va[1][:, :, :, 0:DH], pV.rearrange("p t (h c) -> p t h c", h=H), ACT.Copy).then_inc(vev[1], 1)
                    need(e, pj["q0"], b + 1)
                    need(e, stp["q0"], b * P2)
                    for t in range(KD):
                        e.activation(full["q0"][:, t, :], pJ[0][:, t, :], ACT.Identity, bias=bq4[:, t:t + 1],
                                     scale=0.25).then_inc(stp["q0"], 1)
                    casts("q0")

            @block.vector
            def _(e):
                e.memset(va[0][:, :, :, DH:VW], 1.0).then_inc(vc, 1)
                e.memset(va[1][:, :, :, DH:VW], 1.0).then_inc(vc, 1)
                need(e, vc, 2)
                e.memset(mb[:, :], 0.0).then_inc(one, 1)
                need(e, one, 2)
                c = Chain(norm, NORM_STEPS)
                @loop(e, B)
                def _(b):
                    c.begin(b)

                    def remainders(j):
                        need(e, stp[j], b * P2 + P0)
                        e.tensor_tensor(rest[j][:, :, :], full[j][:, :, :], parts[j][:, 0, :, :], ALU.subtract).then_inc(stp[j], 1)
                        need(e, stp[j], b * P2 + P1)
                        e.tensor_tensor(parts[j][:, 2, :, :], rest[j][:, :, :], parts[j][:, 1, :, :], ALU.subtract).then_inc(stp[j], 1)

                    need(e, ld_m, 16 * b + 16)
                    need(e, stp["k0"], b * P2)
                    e.tensor_scalar(mb[:, :], mi[:, :], 0.0, None, ALU.not_equal).then_inc(mke, 1)
                    need(e, ld_x, 16 * b + 16)
                    need(e, trh, b)
                    norm_vector(S, e, c, nb, S.X[:, ds(b * TPB, TPB), :], hn, mvr, rsr, b)
                    c.wait(e)
                    need(e, mke, b + 1)
                    need(e, pj["k0"], b + 1)
                    for t in range(KD):
                        ins = e.scalar_tensor_tensor(out=full["k0"][:, t, :], in0=pJ[0][:, t, :], scalar=S.w["bk"][:, t:t + 1],
                                                     in1=mb[:, :], op0=ALU.add, op1=ALU.mult)
                        ins.then_inc(stp["k0"], 1)
                    need(e, pj["v0"], b + 1)
                    need(e, kst["v0"], 16 * b)
                    e.tensor_tensor(va[0][:, :, :, 0:DH], pV.rearrange("p t (h c) -> p t h c", h=H),
                                    S.w["bv_b"][:, :].rearrange("p (o h c) -> p o h c", o=1, h=H).broadcast_to([P, TPB, H, DH]),
                                    ALU.add).then_inc(vev[0], 1)
                    remainders("k0")
                    need(e, trh, b + 1)
                    need(e, pj["q0"], b)
                    e.tensor_copy(hT[:, :, :], pT[1][:, :, :]).then_inc(hte, 1)
                    remainders("k1")
                    remainders("q0")
                    c.end()


def attention(S, l):
    nc = S.nc
    ctx, sb, ps, sem = scope(S, f"a{l}")
    SLOTS = 2 * TPB
    NMAX = HG * TPB
    LOADS = 16 * 13
    CLEARED = 2 * G + 1
    with ctx:
        q = [sb(f"q{g}", [P, HG, SEQ], BF16) for g in range(G)]
        k = [sb(f"k{g}", [P, HG, SEQ], BF16) for g in range(G)]
        v = [sb(f"v{g}", [P, TPB, HG, VW]) for g in range(G)]
        pexp = [sb(f"pexp{t}", [P, HG, SEQ]) for t in range(TPB)]
        nmax = [sb(f"nmax{g}", [P, NMAX]) for g in range(G)]
        nrest = sb("nrest", [P, NMAX])
        nparts = sb("nparts", [P, P], BF16)
        nT = sb("nT", [3 * NMAX, P], BF16)
        osb = sb("osb", [P, SEQ])
        rden = sb("rden", [P, TPB, HG])
        pmax = [ps(f"pmax{j}", [P, SEQ]) for j in range(2)]
        pscore = [ps(f"pscore{j}", [P, 2, SEQ]) for j in range(2)]
        pout = ps("pout", [P, SEQ])
        pturn = ps("pturn", [P, TPB, P])
        pturn_n = pturn[:, 0, 0:P // 2].bitcast(BF16)[0:P, :]
        ones_up, ld_v = sem("ones_up"), [sem(f"ld_v{g}", keep=True) for g in range(G)]
        ld = [sem(f"ld{g}") for g in range(G)]
        mrow = [sem(f"mrow{g}") for g in range(G)]
        maxed, reduced, cut, nturned, nout = (sem(x) for x in ("maxed", "reduced", "cut", "nturned", "nout"))
        scored, exped, summed, oout, turned, rec, normed = (
            sem(x) for x in ("scored", "exped", "summed", "oout", "turned", "rec", "normed"))

        def groups(body):
            def run(e):
                for g in range(G):
                    body(e, 0, g, g == 0, False)
                with e.Fori(1, B - 1) as b:
                    for g in range(G):
                        body(e, b, g, False, False)
                for g in range(G):
                    body(e, B - 1, g, False, True)
            return run

        def ahead(b, g, by):
            return (b, g + by) if g + by < G else (b + 1, g + by - G)

        with nc.Block() as block:
            @block.sync
            def _(e):
                def load(b, g):
                    at = ds(b * SEQ, SEQ)
                    for j in range(6):
                        for buf, src, part in ((q, S.qs[l], Q_PARTS[j]), (k, S.ks[l], K_PARTS[j])):
                            e.dma_start(buf[g][j * DH:(j + 1) * DH, :, :],
                                        src[part, g * HG * DH:(g + 1) * HG * DH, at].rearrange("(h d) t -> d h t", d=DH)
                                        ).then_inc(ld[g], 16)
                    e.dma_start(k[g][PARTS_ROWS:MAX_ROWS, :, :],
                                S.mrows[l][:, at].rearrange("s (o t) -> s o t", o=1).broadcast_to([3, HG, SEQ])
                                ).then_inc(ld[g], 16)

                def maxima(b, g):
                    need(e, nout, b * G + g + 1)
                    for s in range(3):
                        e.dma_start(q[g][MAX_ROWS + s:MAX_ROWS + s + 1, :, :].rearrange("o h (t c) -> o (h t) c", c=P),
                                    nT[s * NMAX:(s + 1) * NMAX, :]).then_inc(mrow[g], 16)

                def body(e, b, g, first, last):
                    if not (last and g == G - 1):
                        maxima(*ahead(b, g, 1))
                    if not last:
                        need(e, scored, (b * G + g + 1) * SLOTS)
                        load(b + 1, g)

                need(e, ones_up, CLEARED)
                for g in range(G):
                    load(0, g)
                maxima(0, 0)
                groups(body)(e)

            @block.gpsimd
            def _(e):
                e.memset(nparts[:, :], 0.0).then_inc(cut, 1)

                def load_v(b, g):
                    e.dma_start(v[g][:, :, :, :].rearrange("p t h c -> p t (h c)"),
                                S.vs[l][ds(b * SEQ, SEQ), g * HG * VW:(g + 1) * HG * VW].rearrange("(t p) c -> p t c", p=P)
                                ).then_inc(ld_v[g], 16)

                def parts(b, g):
                    n = b * G + g
                    need(e, reduced, (n + 1) * NMAX)
                    need(e, nturned, n)
                    need(e, cut, 4 * n + 1)
                    gate(S, e)
                    e.tensor_copy(nparts[:, 0:NMAX], nmax[g][:, :]).then_inc(cut, 1)
                    need(e, cut, 4 * n + 2)
                    e.tensor_tensor(nrest[:, :], nmax[g][:, :], nparts[:, 0:NMAX], ALU.subtract).then_inc(cut, 1)
                    need(e, cut, 4 * n + 3)
                    gate(S, e)
                    e.tensor_copy(nparts[:, NMAX:2 * NMAX], nrest[:, :]).then_inc(cut, 1)
                    need(e, cut, 4 * n + 4)
                    e.tensor_tensor(nparts[:, 2 * NMAX:3 * NMAX], nrest[:, :], nparts[:, NMAX:2 * NMAX],
                                    ALU.subtract).then_inc(cut, 1)

                def body(e, b, g, first, last):
                    n = b * G + g
                    if not first and not (last and g > 0):
                        need(e, summed, n * TPB)
                        load_v(*((b, G - 1) if g == 0 else (b + 1, g - 1)))
                    if not (last and g >= G - 2):
                        parts(*ahead(b, g, 2))

                for g in range(G):
                    load_v(0, g)
                parts(0, 0)
                parts(0, 1)
                groups(body)(e)

            @block.tensor
            def _(e):
                def max_product(b, g, j):
                    n, h, t = b * G + g, j // TPB, j % TPB
                    need(e, reduced, n * NMAX + j - 1)
                    e.matmul(pmax[j % 2][:, :], q[g][0:MAX_ROWS, h, t * P:(t + 1) * P], k[g][0:MAX_ROWS, h, :],
                             start=True, stop=True).then_inc(maxed, 1)

                def turn_maxima(b, g):
                    n = b * G + g
                    need(e, cut, 4 * n + 5)
                    need(e, normed, n - 2)
                    e.transpose(pturn_n, nparts[:, :], S.identb[:, :]).then_inc(nturned, 1)

                def values(b, g, t):
                    n = b * G + g
                    if t == 0:
                        need(e, ld_v[g], 16 * b + 16)
                        need(e, oout, n)
                    need(e, exped, n * SLOTS + 2 * t + 2)
                    for h in range(HG):
                        last = e.matmul(pout[32 * h:32 * h + VW, :], v[g][:, t, h, :], pexp[t][:, h, :],
                                        start=(t == 0), stop=(t == TPB - 1))
                    last.then_inc(summed, 1)

                def turn_outputs(n, nturns):
                    need(e, oout, n + 1)
                    need(e, nout, nturns)
                    need(e, normed, n)
                    for t in range(TPB):
                        last = e.transpose(pturn[:, t, :], osb[:, t * P:(t + 1) * P], S.ident[:, :])
                    last.then_inc(turned, 1)

                def body(e, b, g, first, last):
                    n = b * G + g
                    for s in range(SLOTS):
                        t, pair = s // 2, s % 2
                        if not (first and s < 2):
                            need(e, exped, n * SLOTS + s - 1)
                        if s == 0:
                            need(e, mrow[g], 48 * b + 48)
                        for h in (2 * pair, 2 * pair + 1):
                            mm = e.matmul(pscore[s % 2][:, h % 2, :], k[g][0:ALL_ROWS, h, t * P:(t + 1) * P],
                                          q[g][0:ALL_ROWS, h, :], start=True, stop=True)
                        mm.then_inc(scored, 1)
                        if not (last and g >= G - 2):
                            b2, g2 = ahead(b, g, 2)
                            if s == 0:
                                need(e, ld[g2], LOADS * b2 + LOADS)
                            max_product(b2, g2, 2 * s)
                            max_product(b2, g2, 2 * s + 1)
                        if s == 1:
                            if not first:
                                values(*((b, g - 1) if g else (b - 1, G - 1)), TPB - 1)
                            if not (last and g == G - 1):
                                turn_maxima(*ahead(b, g, 1))
                        if s >= 3 and s % 2:
                            values(b, g, (s - 3) // 2)
                        if s == 4 and not first:
                            turn_outputs(n - 1, n + (1 if last and g == G - 1 else 2))

                need(e, ones_up, CLEARED)
                for g in range(2):
                    need(e, ld[g], LOADS)
                    for j in range(NMAX):
                        max_product(0, g, j)
                    if g == 0:
                        turn_maxima(0, 0)
                groups(body)(e)
                values(B - 1, G - 1, TPB - 1)
                turn_outputs(B * G - 1, B * G)

            @block.scalar
            def _(e):
                def take_outputs(n):
                    need(e, summed, (n + 1) * TPB)
                    need(e, turned, n)
                    e.activation(osb[:, :], pout[:, :], ACT.Copy).then_inc(oout, 1)

                def body(e, b, g, first, last):
                    n = b * G + g
                    for s in range(SLOTS):
                        t, pair = s // 2, s % 2
                        need(e, scored, n * SLOTS + s + 1)
                        if pair == 0 and not first:
                            need(e, summed, n * TPB + t - (TPB - 1))
                        e.activation(pexp[t][:, 2 * pair:2 * pair + 2, :], pscore[s % 2][:, :, :], ACT.Exp).then_inc(exped, 1)
                        if s == 2 and not first:
                            take_outputs(n - 1)

                groups(body)(e)
                take_outputs(B * G - 1)

            @block.vector
            def _(e):
                for g in range(G):
                    e.memset(q[g][PARTS_ROWS:ALL_ROWS, :, :], 1.0).then_inc(ones_up, 1)
                    e.memset(k[g][PARTS_ROWS:ALL_ROWS, :, :], 1.0).then_inc(ones_up, 1)
                e.memset(pout[:, :], 0.0).then_inc(ones_up, 1)

                def reduce(b, g, js):
                    n = b * G + g
                    for j in js:
                        if j == 0:
                            need(e, cut, 4 * n - 11)
                        need(e, maxed, n * NMAX + j + 1)
                        e.tensor_reduce(nmax[g][:, j:j + 1], pmax[j % 2][:, :], AX.X, ALU.max,
                                        negate=True).then_inc(reduced, 1)

                def take_maxima(b, g):
                    n = b * G + g
                    need(e, nturned, n + 1)
                    pb, pg = (b, g - 1) if g else (b - 1, G - 1)
                    need(e, mrow[pg], 48 * pb + 48)
                    e.tensor_copy(nT[:, :], pturn_n[0:3 * NMAX, :]).then_inc(nout, 1)

                def normalise(b, g):
                    n = b * G + g
                    turn = pturn[:, :, :].rearrange("p t (h c) -> p t h c", c=32)
                    need(e, turned, n + 1)
                    e.reciprocal(rden[:, :, :], turn[:, :, :, DH]).then_inc(rec, 1)
                    need(e, rec, n + 1)
                    e.tensor_tensor(S.BIG[:, ds(b * TPB, TPB), g * HG * DH:(g + 1) * HG * DH].rearrange("p t (h c) -> p t h c", c=DH),
                                    turn[:, :, :, 0:DH],
                                    rden[:, :, :].rearrange("p t (h o) -> p t h o", o=1).broadcast_to([P, TPB, HG, DH]),
                                    ALU.mult).then_inc(normed, 1)

                def body(e, b, g, first, last):
                    ahead2 = None if last and g >= G - 2 else ahead(b, g, 2)
                    if ahead2:
                        reduce(*ahead2, range(0, 4))
                    if not (last and g == G - 1):
                        take_maxima(*ahead(b, g, 1))
                    if ahead2:
                        reduce(*ahead2, range(4, 12))
                    if not first:
                        normalise(*((b, g - 1) if g else (b - 1, G - 1)))
                    if ahead2:
                        reduce(*ahead2, range(12, NMAX))

                reduce(0, 0, range(NMAX))
                reduce(0, 1, range(2))
                take_maxima(0, 0)
                reduce(0, 1, range(2, NMAX))
                groups(body)(e)
                normalise(B - 1, G - 1)


def tiles(b):
    return ds(b * TPB, TPB)


def turn(e, S, out, src):
    for k in range(KD):
        for t in range(TPB):
            last = e.transpose(out[:, k, t * P:(t + 1) * P], src[:, t, k * P:(k + 1) * P], S.ident[:, :])
    return last


def apply_weight(e, out, srcT, w):
    for t in range(TPB):
        for k in range(KD):
            last = e.matmul(out[:, t, :], srcT[:, k, t * P:(t + 1) * P], w[:, k, :], start=(k == 0), stop=(k == KD - 1))
    return last


def over_tiles(v, n=TPB):
    return v[:, :].rearrange("p (o d) -> p o d", o=1).broadcast_to([P, n, D])


def route(S):
    nc = S.nc
    ctx, sb, ps, sem = scope(S, "r")
    with ctx:
        att = sb("att", [P, TPB, D])
        attT = sb("attT", [P, KD, SEQ])
        yb = sb("yb", [P, TPB, D])
        hn = sb("hn", [P, TPB, D])
        hT = sb("hT", [P, KD, SEQ])
        nb = NormBuffers(sb)
        lmax, lsum, rsum = sb("lmax", [P, TPB]), sb("lsum", [P, TPB]), sb("rsum", [P, TPB])
        less, ex, score, top = (sb(x, [P, TPB, E]) for x in ("less", "ex", "score", "top"))
        topi = sb("topi", [P, TPB, E], U32)
        gs, gc, gr = sb("gs", [P, TPB]), sb("gc", [P, TPB]), sb("gr", [P, TPB])
        pA, pH, pY = (ps(x, [P, KD, SEQ]) for x in ("pA", "pH", "pY"))
        pYt = pY[:, :, :].rearrange("p k (t o) -> p (k t) o", o=D)
        pL = ps("pL", [P, TPB, E])
        staged, tra, ate, yd, trh, hte, ld = (sem(x) for x in ("staged", "tra", "ate", "yd", "trh", "hte", "ld"))
        mvr, pown, rsr, kept, vc, exd = (sem(x) for x in ("mvr", "pown", "rsr", "kept", "vc", "exd"))
        STEPS = NORM_STEPS + 2 + 16
        NORMED = NORM_STEPS + 2

        with nc.Block() as block:
            @block.tensor
            def _(e):
                @loop(e, B)
                def _(b):
                    need(e, staged, b + 1)
                    need(e, ate, b)
                    turn(e, S, pA, att).then_inc(tra, 1)
                    need(e, ate, b + 1)
                    need(e, vc, b * STEPS)
                    apply_weight(e, pYt, attT, S.w["wo0"]).then_inc(yd, 1)
                    need(e, vc, b * STEPS + NORMED)
                    turn(e, S, pH, hn).then_inc(trh, 1)
                    need(e, hte, b + 1)
                    apply_weight(e, pL, hT, S.w["wg"]).then_inc(ld, 1)

            @block.scalar
            def _(e):
                @loop(e, B)
                def _(b):
                    need(e, tra, b)
                    gate(S, e)
                    e.activation(att[:, :, :], S.BIG[:, tiles(b), :], ACT.Copy).then_inc(staged, 1)
                    need(e, tra, b + 1)
                    need(e, yd, b)
                    e.activation(attT[:, :, :], pA[:, :, :], ACT.Copy).then_inc(ate, 1)
                    need(e, trh, b + 1)
                    need(e, ld, b)
                    e.activation(hT[:, :, :], pH[:, :, :], ACT.Copy).then_inc(hte, 1)
                    need(e, vc, b * STEPS + NORMED + 2)
                    e.activation(ex[:, :, :], less[:, :, :], ACT.Exp).then_inc(exd, 1)

            @block.gpsimd
            def _(e):
                @loop(e, B)
                def _(b):
                    norm_gpsimd(S, e, nb, mvr, pown, rsr, b)
                    need(e, vc, b * STEPS + NORMED)
                    need(e, staged, b + 1)
                    gate(S, e)
                    e.tensor_copy(S.BIG[:, tiles(b), :], hn[:, :, :]).then_inc(kept, 1)

            @block.vector
            def _(e):
                c = Chain(vc, STEPS)
                @loop(e, B)
                def _(b):
                    c.begin(b)
                    need(e, yd, b + 1)
                    c.did(e.tensor_tensor(yb[:, :, :], pYt, over_tiles(S.w["bo_b"]), ALU.add))
                    c.wait(e)
                    x = S.X[:, tiles(b), :]
                    c.did(e.scalar_tensor_tensor(out=x, in0=yb[:, :, :], scalar=S.tg[:, 0:1], in1=x,
                                                 op0=ALU.mult, op1=ALU.add))
                    c.wait(e)
                    need(e, kept, b)
                    need(e, trh, b)
                    norm_vector(S, e, c, nb, x, hn, mvr, rsr, b)
                    need(e, ld, b + 1)
                    c.did(e.tensor_reduce(lmax[:, :], pL[:, :, :], AX.X, ALU.max))
                    c.wait(e)
                    per_tile = lambda v: v[:, :].rearrange("p (t o) -> p t o", o=1).broadcast_to([P, TPB, E])
                    c.did(e.tensor_tensor(less[:, :, :], pL[:, :, :], per_tile(lmax), ALU.subtract))
                    need(e, exd, b + 1)
                    c.did(e.tensor_reduce(lsum[:, :], ex[:, :, :], AX.X, ALU.add))
                    c.wait(e)
                    c.did(e.reciprocal(rsum[:, :], lsum[:, :]))
                    c.wait(e)
                    c.did(e.tensor_tensor(score[:, :, :], ex[:, :, :], per_tile(rsum), ALU.mult))
                    c.wait(e)
                    gate(S, e)
                    for t in range(TPB):
                        c.did(e.max(top[:, t, :], score[:, t, :]))
                    c.wait(e)
                    gate(S, e)
                    for t in range(TPB):
                        ins = e.max_index(topi[:, t, :], top[:, t, :], score[:, t, :])
                        if t == TPB - 1:
                            c.did(ins)
                    c.wait(e)
                    c.did(e.tensor_tensor(gs[:, :], top[:, :, 0], top[:, :, 1], ALU.add))
                    c.wait(e)
                    c.did(e.tensor_scalar(gc[:, :], gs[:, :], 1.1920929e-07, None, ALU.max))
                    c.wait(e)
                    c.did(e.reciprocal(gr[:, :], gc[:, :]))
                    c.wait(e)
                    pair = lambda v: v[:, :, 0:2].rearrange("p t k -> p k t")
                    c.did(e.tensor_tensor(S.gate[:, :, tiles(b)], pair(top),
                                          gr[:, :].rearrange("p (o t) -> p o t", o=1).broadcast_to([P, 2, TPB]), ALU.mult))
                    c.did(e.tensor_copy(S.idx[:, :, tiles(b)], pair(topi)))
                    c.wait(e)
                    for kk in range(2):
                        ins = e.tensor_tensor(
                            S.onehot[:, kk * E:(kk + 1) * E, tiles(b)],
                            S.iota8[:, 0:E].rearrange("p (x o) -> p x o", o=1).broadcast_to([P, E, TPB]),
                            S.idx[:, kk:kk + 1, tiles(b)].broadcast_to([P, E, TPB]), ALU.is_equal)
                        if kk:
                            c.did(ins)
                    c.end()


def place(S):
    nc = S.nc
    ctx, sb, ps, sem = scope(S, "l")
    SET = 2
    with ctx:
        tot = sb("tot", [P, 2 * E, NT])
        scan = [sb(f"scan{j}", [P, 2 * E, NT]) for j in range(2)]
        loc = sb("loc", [P, 2 * E, NT])
        mine = sb("mine", [P, 2 * E, NT])
        sel, pos, keep, off, spare, t1, t2, t3, t4 = (sb(x, [P, 2, NT]) for x in (
            "sel", "pos", "keep", "off", "spare", "t1", "t2", "t3", "t4"))
        rows = [sb(f"rows{j}", [P, TPB, D]) for j in range(SET)]
        at = [sb(f"at{j}", [P, 2, TPB], I32) for j in range(SET)]
        pC, pT = ps("pC", [P, 2 * E, NT]), ps("pT", [P, 2 * E, NT])
        mm, sp, vc = sem("mm"), sem("sp"), sem("vc")
        copied = [sem(f"copied{j}") for j in range(SET)]
        listed = [sem(f"listed{j}") for j in range(SET)]
        put = [sem(f"put{j}", keep=True) for j in range(SET)]
        LOC_STEPS = 29
        with nc.Block() as block:
            @block.tensor
            def _(e):
                flat = S.onehot[:, :, :].rearrange("p e t -> p (e t)")
                e.matmul(pC[:, :, :].rearrange("p e t -> p (e t)"), S.triu[:, :], flat, start=True, stop=True).then_inc(mm, 1)
                e.matmul(pT[:, :, :].rearrange("p e t -> p (e t)"), S.onesb[:, :], flat, start=True, stop=True).then_inc(mm, 1)

            @block.scalar
            def _(e):
                @loop(e, B // SET)
                def _(i):
                    for j in range(SET):
                        need(e, put[j], 16 * 2 * TPB * i)
                        gate(S, e)
                        e.activation(rows[j][:, :, :], S.BIG[:, ds((i * SET + j) * TPB, TPB), :], ACT.Copy).then_inc(copied[j], 1)

            @block.vector
            def _(e):
                c = Chain(vc)
                c.begin(0)
                need(e, mm, 2)
                c.did(e.tensor_copy(tot[:, :, :], pT[:, :, :]))
                c.wait(e)
                src = tot
                for n, d in enumerate((1, 2, 4, 8, 16)):
                    dst = scan[n % 2]
                    c.did(e.tensor_tensor(dst[:, :, d:NT], src[:, :, d:NT], src[:, :, 0:NT - d], ALU.add))
                    c.did(e.tensor_copy(dst[:, :, 0:d], src[:, :, 0:d]))
                    c.wait(e)
                    src = dst
                c.did(e.tensor_tensor(loc[:, :, :], src[:, :, :], tot[:, :, :], ALU.subtract))
                c.wait(e)
                c.did(e.tensor_tensor(mine[:, :, :], loc[:, :, :], pC[:, :, :], ALU.add))
                c.wait(e)
                c.did(e.tensor_tensor(mine[:, E:2 * E, :], mine[:, E:2 * E, :],
                                      src[:, 0:E, NT - 1:NT].broadcast_to([P, E, NT]), ALU.add))
                c.wait(e)
                c.did(e.tensor_tensor(loc[:, :, :], mine[:, :, :], S.onehot[:, :, :], ALU.mult))
                c.wait(e)
                for kk in range(2):
                    c.did(e.tensor_reduce(sel[:, kk, :], loc[:, kk * E:(kk + 1) * E, :].rearrange("p x t -> p t x"), AX.X, ALU.add))
                c.wait(e)
                c.did(e.tensor_scalar(t1[:, :, :], sel[:, :, :], -1.0, None, ALU.add))
                c.wait(e)
                c.did(e.tensor_scalar(keep[:, :, :], t1[:, :, :], float(CAP), None, ALU.is_lt))
                c.did(e.scalar_tensor_tensor(out=pos[:, :, :], in0=S.idx[:, :, :], scalar=float(CAP), in1=t1[:, :, :],
                                             op0=ALU.mult, op1=ALU.add))
                c.wait(e)
                c.did(e.tensor_tensor(S.gate[:, :, :], S.gate[:, :, :], keep[:, :, :], ALU.mult))
                c.did(e.tensor_scalar(t2[:, :, :], pos[:, :, :], -float(E * CAP), None, ALU.add))
                c.wait(e)
                c.did(e.tensor_tensor(t3[:, :, :], t2[:, :, :], keep[:, :, :], ALU.mult))
                c.wait(e)
                c.did(e.tensor_scalar(S.row_get[:, :, :], t3[:, :, :], float(E * CAP), None, ALU.add))
                need(e, sp, 1)
                c.did(e.tensor_tensor(t4[:, :, :], pos[:, :, :], spare[:, :, :], ALU.subtract))
                c.wait(e)
                c.did(e.tensor_tensor(off[:, :, :], t4[:, :, :], keep[:, :, :], ALU.mult))
                c.wait(e)
                c.did(e.tensor_tensor(S.row_put[:, :, :], off[:, :, :], spare[:, :, :], ALU.add))
                c.wait(e)
                @loop(e, B // SET)
                def _(i):
                    for j in range(SET):
                        need(e, put[j], 16 * 2 * TPB * i)
                        e.tensor_copy(at[j][:, :, :], S.row_put[:, :, ds((i * SET + j) * TPB, TPB)]).then_inc(listed[j], 1)

            @block.gpsimd
            def _(e):
                e.iota(spare[:, :, :], pattern=[[N, 2], [P, NT]], base=E * CAP, channel_multiplier=1,
                       allow_small_or_imprecise_dtypes=True).then_inc(sp, 1)
                need(e, *S.cleared)
                @loop(e, B // SET)
                def _(i):
                    for j in range(SET):
                        need(e, copied[j], i + 1)
                        need(e, listed[j], i + 1)
                        gate(S, e)
                        for kk in range(2):
                            for t in range(TPB):
                                e.indirect_dma_start(S.disp[:, :], bass.IndirectOffsetOnAxis(ap=at[j][:, kk, t:t + 1], axis=0),
                                                     rows[j][:, t, :], None).then_inc(put[j], 16)
                for j in range(SET):
                    need(e, put[j], 16 * 2 * TPB * (B // SET))


def experts(S):
    nc, a = S.nc, S.a
    ctx, sb, ps, sem = scope(S, "e")
    with ctx:
        raw1 = [sb(f"raw1{x}", [P, KF, D]) for x in range(2)]
        w1T = [sb(f"w1T{x}", [P, KD, FF]) for x in range(2)]
        w2 = [sb(f"w2{x}", [P, KF, D]) for x in range(2)]
        b2 = [sb(f"b2{x}", [P, D]) for x in range(2)]
        rows = [sb(f"rows{j}", [P, 2, D]) for j in range(2)]
        rowsT = [sb(f"rowsT{j}", [P, KD, CHUNK]) for j in range(2)]
        hid = sb("hid", [P, KF, CHUNK])
        y = [sb(f"y{j}", [P, 2, D]) for j in range(2)]
        pw = [ps(f"pw{j}", [P, 4, P]) for j in range(2)]
        pX = ps("pX", [P, KD, CHUNK])
        pH = [ps(f"pH{j}", [P, 2, CHUNK]) for j in range(KF // 2)]
        pY = ps("pY", [P, 2, D])
        ldw = [sem(f"ldw{x}") for x in range(2)]
        ldr = [sem(f"ldr{j}") for j in range(2)]
        trw, wte, trr, rte, up, act, down, ye = (sem(x) for x in ("trw", "wte", "trr", "rte", "up", "act", "down", "ye"))
        yst = [sem(f"yst{j}", keep=True) for j in range(2)]
        WG = 4

        def pairs(body):
            def run(e):
                @loop(e, E // 2 - 1)
                def _(i):
                    body(e, i, False)
                body(e, E // 2 - 1, True)
            return run

        with nc.Block() as block:
            @block.sync
            def _(e):
                def load_weights(n, x):
                    e.dma_start(raw1[x][:, :, :], a["L0_ffn_fc1_w"][ds(n, 1), :, :].rearrange("o (j p) d -> p (o j) d", p=P)).then_inc(ldw[x], 16)
                    e.dma_start(w2[x][:, :, :], a["L0_ffn_fc2_w"][ds(n, 1), :, :].rearrange("o (j p) d -> p (o j) d", p=P)).then_inc(ldw[x], 16)
                    e.dma_start(b2[x][:, :], a["L0_ffn_fc2_b"][ds(n, 1), :].broadcast_to([P, D])).then_inc(ldw[x], 16)

                def load_rows(m, j):
                    e.dma_start(rows[j][:, :, :], S.disp[ds(m * CHUNK, CHUNK), :].rearrange("(t p) d -> p t d", p=P)).then_inc(ldr[j], 16)

                def body(e, i, last):
                    for x in range(2):
                        n = i * 2 + x
                        for ch in range(NCH):
                            m, j = n * NCH + ch, (x * NCH + ch) % 2
                            if not (last and x == 1 and ch >= NCH - 2):
                                need(e, trr, m + 1)
                                load_rows(m + 2, j)
                        if not last:
                            need(e, ye, (n + 1) * NCH)
                            load_weights(n + 2, x)

                load_weights(0, 0)
                load_rows(0, 0)
                load_rows(1, 1)
                load_weights(1, 1)
                pairs(body)(e)

            @block.tensor
            def _(e):
                def turn_weights(n, x, w, loads):
                    m, k, j0 = n * WG + w, w // 2, (w % 2) * 4
                    if w == 0:
                        need(e, ldw[x], loads * 48)
                    need(e, wte, m - 1)
                    for j in range(4):
                        last = e.transpose(pw[w % 2][:, j, :], raw1[x][:, j0 + j, k * P:(k + 1) * P], S.ident[:, :])
                    last.then_inc(trw, 1)

                def turn_rows(m, j, loads):
                    need(e, ldr[j], 16 * loads)
                    need(e, rte, m)
                    for k in range(KD):
                        for t in range(2):
                            last = e.transpose(pX[:, k, t * P:(t + 1) * P], rows[j][:, t, k * P:(k + 1) * P], S.ident[:, :])
                    last.then_inc(trr, 1)

                def body(e, i, last):
                    for x in range(2):
                        n = i * 2 + x
                        for ch in range(NCH):
                            mi = x * NCH + ch
                            m, j = n * NCH + ch, mi % 2
                            need(e, rte, m + 1)
                            if ch == 0:
                                need(e, wte, (n + 1) * WG)
                            for q in range(KF // 2):
                                need(e, act, m * (KF // 2) + q + 1)
                                for f in (2 * q, 2 * q + 1):
                                    for k in range(KD):
                                        mm = e.matmul(pH[q][:, f % 2, :], w1T[x][:, k, f * P:(f + 1) * P], rowsT[j][:, k, :],
                                                      start=(k == 0), stop=(k == KD - 1))
                                mm.then_inc(up, 1)
                            if not (last and mi == 2 * NCH - 1):
                                turn_rows(m + 1, (mi + 1) % 2, i * NCH + (mi + 1) // 2 + 1)
                            if ch < WG and not (last and x == 1):
                                turn_weights(n + 1, 1 - x, ch, i + 1 + x)
                            need(e, ye, m)
                            for t in range(2):
                                for f in range(KF):
                                    if t == 0 and f % 2 == 0:
                                        need(e, act, (m + 1) * (KF // 2) + f // 2 + 1)
                                    mm = e.matmul(pY[:, t, :], hid[:, f, t * P:(t + 1) * P], w2[x][:, f, :],
                                                  start=(f == 0), stop=(f == KF - 1))
                            mm.then_inc(down, 1)

                for w in range(WG):
                    turn_weights(0, 0, w, 1)
                turn_rows(0, 0, 1)
                pairs(body)(e)

            @block.scalar
            def _(e):
                def body(e, i, last):
                    for x in range(2):
                        n = i * 2 + x
                        for ch in range(NCH):
                            m = n * NCH + ch
                            need(e, down, m)
                            for q in range(KF // 2):
                                need(e, up, m * (KF // 2) + q + 1)
                                gate(S, e)
                                for f in (2 * q, 2 * q + 1):
                                    ins = e.activation(hid[:, f, :], pH[q][:, f % 2, :], ACT.Silu, bias=S.b1T[:, ds(n * KF + f, 1)])
                                ins.then_inc(act, 1)
                e.sem_inc(act, KF // 2)
                pairs(body)(e)

            @block.vector
            def _(e):
                def take_weights(n, x, w):
                    m, k, j0 = n * WG + w, w // 2, (w % 2) * 4
                    need(e, trw, m + 1)
                    e.tensor_copy(w1T[x][:, k, j0 * P:(j0 + 4) * P], pw[w % 2][:, :, :]).then_inc(wte, 1)

                def take_rows(m, j):
                    need(e, trr, m + 1)
                    e.tensor_copy(rowsT[j][:, :, :], pX[:, :, :]).then_inc(rte, 1)

                def body(e, i, last):
                    for x in range(2):
                        n = i * 2 + x
                        for ch in range(NCH):
                            mi = x * NCH + ch
                            m, j = n * NCH + ch, mi % 2
                            if not (last and mi == 2 * NCH - 1):
                                take_rows(m + 1, (mi + 1) % 2)
                            if ch < WG and not (last and x == 1):
                                take_weights(n + 1, 1 - x, ch)
                            need(e, down, m + 1)
                            need(e, yst[j], 16 * (i * NCH + mi // 2))
                            e.tensor_tensor(y[j][:, :, :], pY[:, :, :], over_tiles(b2[x], 2), ALU.add).then_inc(ye, 1)

                for w in range(WG):
                    take_weights(0, 0, w)
                take_rows(0, 0)
                pairs(body)(e)

            @block.gpsimd
            def _(e):
                def body(e, i, last):
                    for mi in range(2 * NCH):
                        m = i * 2 * NCH + mi
                        need(e, ye, m + 1)
                        e.dma_start(S.ybuf[ds(m * CHUNK, CHUNK), :].rearrange("(t p) d -> p t d", p=P), y[mi % 2][:, :, :]
                                    ).then_inc(yst[mi % 2], 16)
                pairs(body)(e)
                for j in range(2):
                    need(e, yst[j], 16 * NCH * (E // 2))


def combine(S):
    nc = S.nc
    ctx, sb, ps, sem = scope(S, "c")
    with ctx:
        at = sb("at", [P, 2, TPB], I32)
        yg = sb("yg", [P, 2, TPB, D])
        acc = sb("acc", [P, 2, TPB, D])
        r = sb("r", [P, TPB, D])
        r1, r2 = sb("r1", [P, TPB, D]), sb("r2", [P, TPB, D])
        hn = sb("hn", [P, TPB, D])
        hT = sb("hT", [P, KD, SEQ])
        nb1, nb2 = NormBuffers(sb, "1"), NormBuffers(sb, "2")
        full, rest = sb("full", [P, KD, SEQ]), sb("rest", [P, KD, SEQ])
        parts = sb("parts", [P, 3, KD, SEQ], BF16)
        pH, pQ = ps("pH", [P, KD, SEQ]), ps("pQ", [P, KD, SEQ])
        got = sem("got", keep=True)
        listed, vc, trh, hte, qd, cutq, qst = (sem(x) for x in ("listed", "vc", "trh", "hte", "qd", "cutq", "qst"))
        mv1, own1, rs1, mv2, own2, rs2 = (sem(x) for x in ("mv1", "own1", "rs1", "mv2", "own2", "rs2"))
        GATED = 2 * TPB
        STEPS = GATED + 2 * NORM_STEPS + 3
        FULL, P0, REST, P1, P2 = 1, 2, 3, 4, 5

        with nc.Block() as block:
            @block.gpsimd
            def _(e):
                @loop(e, B)
                def _(b):
                    need(e, got, 16 * 2 * TPB * b)
                    gate(S, e)
                    e.tensor_copy(at[:, :, :], S.row_get[:, :, tiles(b)]).then_inc(listed, 1)
                    need(e, listed, b + 1)
                    gate(S, e)
                    need(e, vc, b * STEPS)
                    gate(S, e)
                    for kk in range(2):
                        for t in range(TPB):
                            e.indirect_dma_start(yg[:, kk, t, :], None, S.ybuf[:, :],
                                                 bass.IndirectOffsetOnAxis(ap=at[:, kk, t:t + 1], axis=0)).then_inc(got, 16)
                    norm_gpsimd(S, e, nb1, mv1, own1, rs1, b)
                    norm_gpsimd(S, e, nb2, mv2, own2, rs2, b)

            @block.vector
            def _(e):
                c = Chain(vc, STEPS)
                @loop(e, B)
                def _(b):
                    c.begin(b)
                    x = S.X[:, tiles(b), :]
                    need(e, got, 16 * 2 * TPB * (b + 1))
                    for kk in range(2):
                        for t in range(TPB):
                            c.did(e.scalar_tensor_tensor(
                                out=acc[:, kk, t, :], in0=yg[:, kk, t, :], scalar=S.gate[:, kk, ds(b * TPB + t, 1)],
                                in1=acc[:, 0, t, :] if kk else S.BIG[:, ds(b * TPB + t, 1), :].rearrange("p o d -> p (o d)"),
                                op0=ALU.mult, op1=ALU.add))
                        c.wait(e)
                    norm_vector(S, e, c, nb1, acc[:, 1, :, :], r, mv1, rs1, b)
                    c.wait(e)
                    c.did(e.tensor_tensor(r1[:, :, :], r[:, :, :], over_tiles(S.w["gamma_b"]), ALU.mult))
                    c.wait(e)
                    c.did(e.tensor_tensor(r2[:, :, :], r1[:, :, :], over_tiles(S.w["beta_b"]), ALU.add))
                    c.wait(e)
                    c.did(e.scalar_tensor_tensor(out=x, in0=r2[:, :, :], scalar=S.tg[:, 2:3], in1=x, op0=ALU.mult, op1=ALU.add))
                    c.wait(e)
                    need(e, trh, b)
                    norm_vector(S, e, c, nb2, x, hn, mv2, rs2, b)
                    c.end()
                    need(e, cutq, b * P2 + P0)
                    e.tensor_tensor(rest[:, :, :], full[:, :, :], parts[:, 0, :, :], ALU.subtract).then_inc(cutq, 1)
                    need(e, cutq, b * P2 + P1)
                    e.tensor_tensor(parts[:, 2, :, :], rest[:, :, :], parts[:, 1, :, :], ALU.subtract).then_inc(cutq, 1)

            @block.tensor
            def _(e):
                @loop(e, B)
                def _(b):
                    need(e, vc, (b + 1) * STEPS)
                    need(e, hte, b)
                    turn(e, S, pH, hn).then_inc(trh, 1)
                    need(e, hte, b + 1)
                    need(e, cutq, b * P2)
                    for t in range(KD):
                        for k in range(KD):
                            last = e.matmul(pQ[:, t, :], S.w["wq1"][:, k, t * P:(t + 1) * P], hT[:, k, :],
                                            start=(k == 0), stop=(k == KD - 1))
                    last.then_inc(qd, 1)

            @block.scalar
            def _(e):
                @loop(e, B)
                def _(b):
                    need(e, trh, b + 1)
                    need(e, qd, b)
                    e.activation(hT[:, :, :], pH[:, :, :], ACT.Copy).then_inc(hte, 1)
                    need(e, qd, b + 1)
                    need(e, cutq, b * P2)
                    e.activation(full[:, :, :], pQ[:, :, :], ACT.Copy, scale=0.25).then_inc(cutq, 1)
                    need(e, cutq, b * P2 + FULL)
                    need(e, qst, 48 * b)
                    e.activation(parts[:, 0, :, :], full[:, :, :], ACT.Copy).then_inc(cutq, 1)
                    need(e, cutq, b * P2 + REST)
                    e.activation(parts[:, 1, :, :], rest[:, :, :], ACT.Copy).then_inc(cutq, 1)

            @block.sync
            def _(e):
                @loop(e, B)
                def _(b):
                    need(e, cutq, (b + 1) * P2)
                    for s in range(3):
                        e.dma_start(S.qs[1][s, :, ds(b * SEQ, SEQ)].rearrange("(t p) c -> p t c", p=P),
                                    parts[:, s, :, :]).then_inc(qst, 16)
                need(e, qst, 48 * B)


def merge(S):
    nc = S.nc
    ctx, sb, ps, sem = scope(S, "m")
    with ctx:
        att = sb("att", [P, TPB, D])
        attT = sb("attT", [P, KD, SEQ])
        nb = NormBuffers(sb)
        pA = ps("pA", [P, KD, SEQ])
        pY = ps("pY", [P, TPB, D])
        staged, tra, ate, yd, mvr, pown, rsr, vc = (sem(x) for x in ("staged", "tra", "ate", "yd", "mvr", "pown", "rsr", "vc"))
        STEPS = NORM_STEPS + 2
        with nc.Block() as block:
            @block.tensor
            def _(e):
                @loop(e, B)
                def _(b):
                    need(e, staged, b + 1)
                    need(e, ate, b)
                    turn(e, S, pA, att).then_inc(tra, 1)
                    need(e, ate, b + 1)
                    need(e, vc, b * STEPS)
                    apply_weight(e, pY, attT, S.w["wo1"]).then_inc(yd, 1)

            @block.scalar
            def _(e):
                @loop(e, B)
                def _(b):
                    need(e, tra, b)
                    gate(S, e)
                    e.activation(att[:, :, :], S.BIG[:, tiles(b), :], ACT.Copy).then_inc(staged, 1)
                    need(e, tra, b + 1)
                    need(e, yd, b)
                    e.activation(attT[:, :, :], pA[:, :, :], ACT.Copy).then_inc(ate, 1)

            @block.gpsimd
            def _(e):
                @loop(e, B)
                def _(b):
                    norm_gpsimd(S, e, nb, mvr, pown, rsr, b)

            @block.vector
            def _(e):
                c = Chain(vc, STEPS)
                @loop(e, B)
                def _(b):
                    c.begin(b)
                    x = S.X[:, tiles(b), :]
                    need(e, yd, b + 1)
                    c.did(e.scalar_tensor_tensor(out=x, in0=pY[:, :, :], scalar=S.tg[:, 1:2], in1=x, op0=ALU.mult, op1=ALU.add))
                    c.wait(e)
                    need(e, staged, b + 1)
                    norm_vector(S, e, c, nb, x, S.BIG[:, tiles(b), :], mvr, rsr, b)
                    c.wait(e)
                    c.did(e.tensor_reduce(S.amax[:, ds(b, 1)], S.BIG[:, tiles(b), :], AX.XY, ALU.max,
                                          apply_absolute_value=True))
                    c.end()


def quantise(S):
    nc, a = S.nc, S.a
    ctx, sb, ps, sem = scope(S, "q")
    EXP_BITS = 0x7F800000
    with ctx:
        w = sb("w", [P, KD, D])
        am, amg, amc, rec, scale, rscale = (sb(x, [P, 2]) for x in ("am", "amg", "amc", "rec", "scale", "rscale"))
        inv = sb("inv", [P, 1])
        v = [sb(f"v{j}", [P, TPB, D]) for j in range(2)]
        m = [sb(f"m{j}", [P, TPB, D]) for j in range(2)]
        big = [sb(f"big{j}", [P, TPB, D]) for j in range(2)]
        vq = [sb(f"vq{j}", [P, TPB, D], BF16) for j in range(2)]
        wq = sb("wq", [P, KD, D], BF16)
        wqT = sb("wqT", [P, KD, D], BF16)
        vqT = sb("vqT", [P, KD, SEQ], BF16)
        t1 = sb("t1", [P, TPB, D])
        o = [sb(f"o{j}", [P, TPB, D]) for j in range(2)]
        pW = ps("pW", [P, KD, D], BF16)
        pV = ps("pV", [P, KD, SEQ], BF16)
        pY = [ps(f"pY{j}", [P, TPB, D]) for j in range(2)]
        ldw, vc, red, wsc, wtr, wte = (sem(x) for x in ("ldw", "vc", "red", "wsc", "wtr", "wte"))
        sc = [sem(f"sc{j}") for j in range(2)]
        trv, vte, yd, fin = sem("trv"), sem("vte"), sem("yd"), sem("fin")
        st = [sem(f"st{j}") for j in range(2)]
        SCALED, MASKED, ADDED, MADE, ROUNDED = 1, 2, 3, 4, 5

        def mask_exponent(e, out, src):
            return e.tensor_scalar(out.bitcast(I32), src.bitcast(I32), EXP_BITS, None, ALU.bitwise_and)

        def make_m(e, out, src):
            return e.tensor_scalar(out, src, 2.0 ** -6, 1.5 * 2.0 ** 20, ALU.max, ALU.mult)

        with nc.Block() as block:
            @block.sync
            def _(e):
                e.dma_start(w[:, :, :], a["L1_ffn_weight"].rearrange("(t p) c -> p t c", p=P)).then_inc(ldw, 16)
                @loop(e, B // 2)
                def _(i):
                    for j in range(2):
                        need(e, fin, i * 4 + 2 * j + 2)
                        e.dma_start(S.out[ds(i * 2 + j, 1), :, :].rearrange("o (t p) d -> p (o t) d", p=P),
                                    o[j][:, :, :]).then_inc(st[j], 16)
                for j in range(2):
                    need(e, st[j], 16 * (B // 2))

            @block.gpsimd
            def _(e):
                need(e, vc, 2)
                e.partition_all_reduce(amg[:, :], am[:, :], P, bass.bass_isa.ReduceOp.max).then_inc(red, 1)
                @loop(e, B // 2)
                def _(i):
                    for j in range(2):
                        need(e, sc[j], i * ROUNDED + MASKED)
                        gate(S, e)
                        make_m(e, m[j][:, :, :], m[j][:, :, :]).then_inc(sc[j], 1)

            @block.scalar
            def _(e):
                need(e, vc, 6)
                e.activation(v[1][:, 0:KD, :], w[:, :, :], ACT.Copy, scale=scale[:, 1:2]).then_inc(wsc, 1)
                need(e, wtr, 1)
                e.activation(wqT[:, :, :], pW[:, :, :], ACT.Copy).then_inc(wte, 1)
                @loop(e, B // 2)
                def _(i):
                    for j in range(2):
                        b = i * 2 + j
                        need(e, sc[j], i * ROUNDED)
                        need(e, wsc, 5)
                        gate(S, e)
                        e.activation(v[j][:, :, :], S.BIG[:, tiles(b), :], ACT.Copy, scale=scale[:, 0:1]).then_inc(sc[j], 1)
                        need(e, trv, b + 1)
                        need(e, yd, b)
                        e.activation(vqT[:, :, :], pV[:, :, :], ACT.Copy).then_inc(vte, 1)

            @block.tensor
            def _(e):
                need(e, wsc, 5)
                for k in range(KD):
                    for t in range(KD):
                        last = e.transpose(pW[:, k, t * P:(t + 1) * P], wq[:, t, k * P:(k + 1) * P], S.identb[:, :])
                last.then_inc(wtr, 1)
                need(e, wte, 1)
                @loop(e, B // 2)
                def _(i):
                    for j in range(2):
                        b = i * 2 + j
                        need(e, sc[j], (i + 1) * ROUNDED)
                        need(e, vte, b)
                        for k in range(KD):
                            for t in range(TPB):
                                last = e.transpose(pV[:, k, t * P:(t + 1) * P], vq[j][:, t, k * P:(k + 1) * P], S.identb[:, :])
                        last.then_inc(trv, 1)
                        need(e, vte, b + 1)
                        need(e, fin, i * 4)
                        apply_weight(e, pY[j], vqT, wqT).then_inc(yd, 1)

            @block.vector
            def _(e):
                c = Chain(vc)
                c.begin(0)
                c.did(e.tensor_reduce(am[:, 0:1], S.amax[:, :], AX.X, ALU.max))
                need(e, ldw, 16)
                c.did(e.tensor_reduce(am[:, 1:2], w[:, :, :], AX.XY, ALU.max, apply_absolute_value=True))
                need(e, red, 1)
                c.did(e.tensor_scalar(amc[:, :], amg[:, :], 1e-12, None, ALU.max))
                c.wait(e)
                c.did(e.reciprocal(rec[:, :], amc[:, :]))
                c.wait(e)
                c.did(e.tensor_scalar(scale[:, :], rec[:, :], FP8_MAX, None, ALU.mult))
                c.wait(e)
                c.did(e.reciprocal(rscale[:, :], scale[:, :]))
                c.wait(e)
                c.did(e.tensor_tensor(inv[:, :], rscale[:, 0:1], rscale[:, 1:2], ALU.mult))
                need(e, wsc, 1)
                mask_exponent(e, big[1][:, 0:KD, :], v[1][:, 0:KD, :]).then_inc(wsc, 1)
                need(e, wsc, 2)
                make_m(e, m[1][:, 0:KD, :], big[1][:, 0:KD, :]).then_inc(wsc, 1)
                need(e, wsc, 3)
                e.tensor_tensor(t1[:, 0:KD, :], v[1][:, 0:KD, :], m[1][:, 0:KD, :], ALU.add).then_inc(wsc, 1)
                need(e, wsc, 4)
                e.tensor_tensor(wq[:, :, :], t1[:, 0:KD, :], m[1][:, 0:KD, :], ALU.subtract).then_inc(wsc, 1)
                c.wait(e)
                need(e, wsc, 5)

                def round_first(i, j):
                    need(e, sc[j], i * ROUNDED + SCALED)
                    mask_exponent(e, m[j][:, :, :], v[j][:, :, :]).then_inc(sc[j], 1)

                @loop(e, B // 2)
                def _(i):
                    for j in range(2):
                        b = i * 2 + j
                        round_first(i, j)
                        need(e, sc[j], i * ROUNDED + ADDED)
                        need(e, trv, b)
                        e.tensor_tensor(big[j][:, :, :], v[j][:, :, :], m[j][:, :, :], ALU.add).then_inc(sc[j], 1)
                        need(e, sc[j], i * ROUNDED + MADE)
                        e.tensor_tensor(vq[j][:, :, :], big[j][:, :, :], m[j][:, :, :], ALU.subtract).then_inc(sc[j], 1)
                        need(e, yd, b + 1)
                        need(e, st[j], 16 * i)
                        for t in range(TPB):
                            ins = e.scalar_tensor_tensor(out=t1[:, t, :], in0=pY[j][:, t, :], scalar=inv[:, 0:1],
                                                         in1=S.w["fb_b"][:, :], op0=ALU.mult, op1=ALU.add)
                        ins.then_inc(fin, 1)
                        need(e, fin, i * 4 + 2 * j + 1)
                        e.scalar_tensor_tensor(out=o[j][:, :, :], in0=t1[:, :, :], scalar=S.tg[:, 3:4],
                                               in1=S.X[:, tiles(b), :], op0=ALU.mult, op1=ALU.add).then_inc(fin, 1)


_INS = ['x', 'ctx_1024', 'mask_Bx1xS2_if1', 'g_xattn', 'g_ffn', 'L0_xattn_wq', 'L0_xattn_bq', 'L0_xattn_wk',
        'L0_xattn_bk', 'L0_xattn_wv', 'L0_xattn_bv', 'L0_xattn_wo', 'L0_xattn_bo', 'L0_ffn_wg', 'L0_ffn_fc1_w',
        'L0_ffn_fc1_b', 'L0_ffn_fc2_w', 'L0_ffn_fc2_b', 'L0_ffn_ln_gamma', 'L0_ffn_ln_beta', 'L1_xattn_q_map',
        'L1_xattn_k_map', 'L1_xattn_v_map', 'L1_xattn_output_map', 'L1_ffn_weight', 'L1_ffn_bias']


def kernel(**inputs):
    import numpy as _np
    import concourse.bacc as _bacc
    from concourse import mybir as _mybir
    from concourse.bass_utils import run_bass_kernel_spmd as _run

    nc = _bacc.Bacc("TRN2", target_bir_lowering=False, num_devices=1)
    arrays, args = {}, {}
    for name in _INS:
        v = _np.ascontiguousarray(inputs[name])
        arrays[f"in_{name}"] = v
        args[name] = nc.dram_tensor(f"in_{name}", v.shape, _mybir.dt.from_np(v.dtype), kind="ExternalInput").ap()
    out = nc.dram_tensor("out_x", (B, SEQ, D), _mybir.dt.float32, kind="ExternalOutput").ap()
    build(nc, args, out)
    r = _run(nc, [arrays], core_ids=[0])
    return r.results[0]["out_x"]
```

```python
from contextlib import ExitStack

import concourse.bass as bass
from concourse import mybir

F32 = mybir.dt.float32
BF16 = mybir.dt.bfloat16
F32R = mybir.dt.float32r
I32 = mybir.dt.int32
U32 = mybir.dt.uint32
ACT = mybir.ActivationFunctionType
ALU = mybir.AluOpType
AX = mybir.AxisListType
ds = bass.ds

P = 128
B, SEQ, D = 8, 512, 256
TPB = SEQ // P
NT = B * TPB
N = B * SEQ
KD = D // P
H, DH = 16, 16
G, HG = 4, 4
E, FF = 8, 1024
KF = FF // P
CAP = 2 * int(1.25 * ((N + E - 1) // E))
ZROWS = E * CAP // (P * B)
CHUNK = 256
NCH = CAP // CHUNK
VW = DH + 1
Q_PARTS = (0, 1, 2, 0, 1, 0)
K_PARTS = (0, 0, 0, 1, 1, 2)
PARTS_ROWS = 6 * DH
MAX_ROWS = PARTS_ROWS + 3
ALL_ROWS = MAX_ROWS + 3
FP8_MAX = 448.0


class Shared:
    pass


def need(e, sem, value):
    if not isinstance(value, int) or value > 0:
        e.wait_ge(sem, value)


def rounds(e, lag, lead=0):
    def run(body):
        first, last = (lag + 3) // 2, (B - lead) // 2
        for i in range(2 * first):
            body(i, i % 2, i // 2)
        with e.Fori(first, last) as k:
            for j in range(2):
                body(k * 2 + j, j, k)
        for i in range(2 * last, B + lag):
            body(i, i % 2, i // 2)
    return run


def inside(b):
    return not isinstance(b, int) or 0 <= b < B


def loop3(e, n):
    def run(body):
        body(0, False)
        with e.Fori(1, n - 1) as i:
            body(i, False)
        body(n - 1, True)
    return run


def loop(e, n):
    def run(body):
        body(0)
        with e.Fori(1, n) as i:
            body(i)
    return run


class Chain:

    def __init__(self, sem, per=0):
        self.sem, self.per, self.base, self.k = sem, per, 0, 0

    def begin(self, i):
        self.i, self.k = i, 0

    def end(self):
        assert self.k == self.per, (self.sem, self.k, self.per)

    def did(self, ins):
        ins.then_inc(self.sem, 1)
        self.k += 1
        return self.k

    def wait(self, eng, k=None):
        k = self.k if k is None else k
        need(eng, self.sem, self.i * self.per + k)


def build(nc, a, out, stop=99):
    ctx = ExitStack()
    with ctx:
        S = Shared()
        S.nc, S.a, S.out, S.w = nc, a, out, {}
        S.sem = lambda name: ctx.enter_context(nc.semaphore(name))
        S.stage_sems, S.sems_ctx = [], ExitStack()

        S.gates = S.sem("gates")

        def sb(name, shape, dt=F32):
            return ctx.enter_context(nc.sbuf_tensor(name, shape, dt))

        def dram(name, shape, dt=F32):
            return nc.dram_tensor(name, shape, dt).ap()

        ctx.enter_context(nc.allow_non_contiguous_dma(reason="small vectors, head-wise rows"))
        S.X = sb("X", [P, NT, D])
        S.BIG = sb("BIG", [P, NT, D])
        S.ident = sb("ident", [P, P])
        S.identb = sb("identb", [P, P], BF16)
        S.onesb = sb("onesb", [P, P], BF16)
        S.triu = sb("triu", [P, P], BF16)
        S.onesrow = sb("onesrow", [1, P])
        S.rank8 = sb("rank8", [P, E])
        S.half = sb("half", [P, TPB])
        S.tg = sb("tg", [P, 4])
        for w in ("wq0", "wk0", "wv0", "wo0", "wq1", "wk1", "wv1", "wo1"):
            S.w[w] = sb(w, [P, KD, D])
        S.w["wg"] = sb("wg", [P, KD, E])
        S.w["bq"] = sb("bq", [P, KD])
        S.w["bk"] = sb("bk", [P, KD])
        for w in ("bv_b", "bo_b", "gamma_b", "beta_b", "fb_b"):
            S.w[w] = sb(w, [P, D])
        S.b1T = sb("b1T", [P, E * KF])
        S.idx = sb("idx", [P, 2, NT])
        S.gate = sb("gate", [P, 2, NT])
        S.logit = sb("logit", [P, NT, E])
        S.onehot = sb("onehot", [P, 2 * E, NT], BF16)
        S.row_put = sb("row_put", [P, 2, NT], I32)
        S.row_get = sb("row_get", [P, 2, NT], I32)
        S.amax = sb("amax", [P, B])
        S.qs = [dram(f"qs{l}", (3, D, N), BF16) for l in range(2)]
        S.ks = [dram(f"ks{l}", (3, D, N), BF16) for l in range(2)]
        S.vs = [dram(f"vs{l}", (N, H * VW)) for l in range(2)]
        S.extra = [dram(f"extra{l}", (6, N), BF16) for l in range(2)]
        S.disp = dram("disp", (E * CAP + 2 * N, D))
        S.ybuf = dram("ybuf", (E * CAP + P, D))

        stages = [setup, project, lambda S: attention(S, 0), route, place, recycle, experts, combine,
                  lambda S: attention(S, 1), merge, quantise]
        for n, stage in enumerate(stages):
            if n < stop:
                stage(S)
        S.sems_ctx.close()


def scope(S, n):
    ctx = ExitStack()
    nc = S.nc
    return (ctx, lambda name, shape, dt=F32: ctx.enter_context(nc.sbuf_tensor(f"{n}_{name}", shape, dt)),
            lambda name, shape, dt=F32: ctx.enter_context(nc.psum_tensor(f"{n}_{name}", shape, dt)),
            lambda name, keep=False: S.sem(f"{n}_{name}") if keep else stage_sem(S, f"{n}_{name}"))


def stage_sem(S, name):
    S.stage_sems.append(S.sems_ctx.enter_context(S.nc.semaphore(name)))
    return S.stage_sems[-1]


def recycle(S):
    with S.nc.Block() as block:
        @block.gpsimd
        def _(e):
            for sem in S.stage_sems:
                e.sem_clear(sem)
    S.sems_ctx.close()
    S.stage_sems, S.sems_ctx = [], ExitStack()


def setup(S):
    nc, a = S.nc, S.a
    ctx, sb, ps, sem = scope(S, "s")
    with ctx:
        raw = [sb(f"raw{j}", [P, KD, D]) for j in range(4)]
        b1raw = sb("b1raw", [E * KF, P])
        mi = sb("mi", [B, SEQ], I32)
        mf = sb("mf", [B, 3, SEQ])
        mparts = sb("mparts", [B, 3, SEQ], BF16)
        mzero = sb("mzero", [B, 3, SEQ], BF16)
        mone = sb("mone", [B, 3, SEQ], BF16)
        gl = sb("gl", [P, 4])
        pw = [ps(f"pw{j}", [P, KD, KD, P]) for j in range(4)]
        pb = ps("pb", [P, E * KF])
        ld_raw, ld, ld_mask, ld_g = sem("ld_raw"), sem("ld"), sem("ld_mask"), sem("ld_g")
        zs, id0, idd, tr, ev, vc, st = sem("zs"), sem("id0"), sem("idd"), sem("tr"), sem("ev"), sem("vc"), sem("st")

        with nc.Block() as block:
            @block.sync
            def _(e):
                for j, w in enumerate(("L0_xattn_wq", "L0_xattn_wk", "L0_xattn_wv", "L0_xattn_wo")):
                    e.dma_start(raw[j][:, :, :], a[w].rearrange("(t p) c -> p t c", p=P)).then_inc(ld_raw, 16)
                e.dma_start(b1raw[:, :], a["L0_ffn_fc1_b"].rearrange("e (j p) -> (e j) p", p=P)).then_inc(ld_raw, 16)
                e.dma_start(mi[:, :], a["mask_Bx1xS2_if1"][:, 0, :]).then_inc(ld_mask, 16)
                e.dma_start(gl[:, 0:2], a["g_xattn"].rearrange("(o n) -> o n", o=1).broadcast_to([P, 2])).then_inc(ld_g, 16)
                e.dma_start(gl[:, 2:4], a["g_ffn"].rearrange("(o n) -> o n", o=1).broadcast_to([P, 2])).then_inc(ld_g, 16)
                n = 0
                for w, src in (("wq1", "L1_xattn_q_map"), ("wk1", "L1_xattn_k_map"),
                               ("wv1", "L1_xattn_v_map"), ("wo1", "L1_xattn_output_map"), ("wg", "L0_ffn_wg")):
                    e.dma_start(S.w[w][:, :, :], a[src].rearrange("(k p) o -> p k o", p=P)).then_inc(ld, 16)
                    n += 1
                for w, src in (("bq", "L0_xattn_bq"), ("bk", "L0_xattn_bk")):
                    e.dma_start(S.w[w][:, :], a[src].rearrange("(k p) -> p k", p=P)).then_inc(ld, 16)
                    n += 1
                for w, src in (("bv_b", "L0_xattn_bv"), ("bo_b", "L0_xattn_bo"), ("gamma_b", "L0_ffn_ln_gamma"),
                               ("beta_b", "L0_ffn_ln_beta"), ("fb_b", "L1_ffn_bias")):
                    e.dma_start(S.w[w][:, :],
                                a[src].rearrange("(o n) -> o n", o=1).broadcast_to([P, D])).then_inc(ld, 16)
                    n += 1
                need(e, vc, 9)
                for l, rows in ((0, mparts), (1, mzero)):
                    e.dma_start(S.extra[l][0:3, :].rearrange("s (b t) -> b s t", b=B), rows[:, :, :]).then_inc(st, 16)
                    e.dma_start(S.extra[l][3:6, :].rearrange("s (b t) -> b s t", b=B), mone[:, :, :]).then_inc(st, 16)
                need(e, ld, 16 * n)
                need(e, st, 64)

            @block.gpsimd
            def _(e):
                e.memset(S.ident[:, :], 0.0).then_inc(id0, 1)
                e.memset(S.onesb[:, :], 1.0).then_inc(id0, 1)
                e.memset(S.half[:, :], -0.5).then_inc(idd, 1)
                e.memset(S.onesrow[:, :], 1.0).then_inc(idd, 1)
                need(e, id0, 2)
                e.affine_select(out=S.ident[:, :], in_=S.ident[:, :], compare_op=ALU.not_equal, fill=1.0,
                                base=0, pattern=[[-1, P]], channel_multiplier=1).then_inc(idd, 1)
                e.affine_select(out=S.triu[:, :], in_=S.onesb[:, :], compare_op=ALU.is_ge, fill=0.0,
                                base=0, pattern=[[1, P]], channel_multiplier=-1).then_inc(idd, 1)
                e.iota(S.rank8[:, :], pattern=[[-1, E]], base=E, channel_multiplier=0,
                       allow_small_or_imprecise_dtypes=True).then_inc(idd, 1)
                e.memset(S.BIG[:, 0:ZROWS, :], 0.0).then_inc(zs, 1)
                need(e, zs, 1)

            @block.tensor
            def _(e):
                need(e, idd, 5)
                need(e, ld_raw, 80)
                for j in range(4):
                    for k in range(KD):
                        for t in range(KD):
                            e.transpose(pw[j][:, k, t, :], raw[j][:, t, k * P:(k + 1) * P], S.ident[:, :]).then_inc(tr, 1)
                e.transpose(pb[:, :], b1raw[:, :], S.ident[0:E * KF, 0:E * KF]).then_inc(tr, 1)

            @block.scalar
            def _(e):
                need(e, ld_g, 32)
                e.activation(S.tg[:, :], gl[:, :], ACT.Tanh).then_inc(ev, 1)
                for j, w in enumerate(("wq0", "wk0", "wv0", "wo0")):
                    need(e, tr, 4 * j + 4)
                    e.activation(S.w[w][:, :, :], pw[j][:, :, :, :], ACT.Copy).then_inc(ev, 1)
                need(e, tr, 17)
                e.activation(S.b1T[:, :], pb[:, :], ACT.Copy).then_inc(ev, 1)

            @block.vector
            def _(e):
                c = Chain(vc)
                c.begin(0)
                c.did(e.memset(mzero[:, :, :], 0.0))
                c.did(e.memset(mone[:, :, :], 1.0))
                need(e, ld_mask, 16)
                c.did(e.tensor_scalar(mf[:, 0, :], mi[:, :], 0.0, -1.0, ALU.not_equal, ALU.add))
                c.wait(e)
                c.did(e.tensor_scalar(mf[:, 1, :], mf[:, 0, :], 1.0e9, None, ALU.mult))
                c.wait(e)
                split3(e, c, mf[:, 1, :], mf[:, 2, :], mparts[:, 0, :], mparts[:, 1, :], mparts[:, 2, :])
                need(e, idd, 5)
                c.did(e.tensor_copy(S.identb[:, :], S.ident[:, :]))


def split3(e, c, src, rest, p0, p1, p2):
    c.did(e.tensor_copy(p0, src))
    c.wait(e)
    c.did(e.tensor_tensor(rest, src, p0, ALU.subtract))
    c.wait(e)
    c.did(e.tensor_copy(p1, rest))
    c.wait(e)
    c.did(e.tensor_tensor(p2, rest, p1, ALU.subtract))


class Norm:

    def __init__(self, S, sb, sem, n="", sets=2):
        self.S, self.sets = S, sets
        self.stats6 = sb(f"stats{n}", [P, TPB, 6])
        self.mv = [sb(f"mv{n}{j}", [P, TPB, 2]) for j in range(sets)]
        self.var = [sb(f"var{n}{j}", [P, TPB]) for j in range(sets)]
        self.rstd = [sb(f"rstd{n}{j}", [P, TPB]) for j in range(sets)]
        self.stated, self.agg, self.vard, self.powed, self.normed = (
            sem(f"{x}{n}") for x in ("stated", "agg", "vard", "powed", "normed"))

    def stats(self, e, b, j, src):
        need(e, self.agg, b * TPB)
        gate(self.S, e)
        for t in range(TPB):
            e.bn_stats(self.stats6[:, t, :], src[:, t, :]).then_inc(self.stated, 1)
        need(e, self.stated, (b + 1) * TPB)
        gate(self.S, e)
        for t in range(TPB):
            e.bn_aggr(self.mv[j][:, t, :], self.stats6[:, t, :]).then_inc(self.agg, 1)

    def power(self, e, b, j):
        need(e, self.agg, (b + 1) * TPB)
        gate(self.S, e)
        e.tensor_scalar(self.var[j][:, :], self.mv[j][:, :, 1], 1e-5, None, ALU.add).then_inc(self.vard, 1)
        need(e, self.vard, b + 1)
        e.tensor_tensor(self.rstd[j][:, :], self.var[j][:, :], self.S.half[:, :], ALU.pow).then_inc(self.powed, 1)

    def apply(self, e, b, j, src, dst):
        need(e, self.agg, (b + 1) * TPB)
        need(e, self.powed, b + 1)
        for t in range(TPB):
            e.tensor_scalar(dst[:, t, :], src[:, t, :], self.mv[j][:, t, 0:1], self.rstd[j][:, t:t + 1],
                            ALU.subtract, ALU.mult).then_inc(self.normed, 1)

    def wait(self, e, b):
        need(e, self.normed, (b + 1) * TPB)


def gate(S, e):
    e.sem_inc(S.gates, 1)


def project(S):
    nc, a = S.nc, S.a
    ctx, sb, ps, sem = scope(S, "p")
    with ctx:
        cin = sb("cin", [P, TPB, D])
        cT = sb("cT", [P, KD, SEQ])
        hn = sb("hn", [P, TPB, D])
        hT = sb("hT", [P, KD, SEQ])
        mi = sb("mi", [P, SEQ], I32)
        mb = sb("mb", [P, SEQ])
        bq4 = sb("bq4", [P, KD])
        nb = Norm(S, sb, sem, sets=1)
        jobs = ("k0", "k1", "q0")
        full = {j: sb(f"full_{j}", [P, KD, SEQ]) for j in jobs}
        rest = {j: sb(f"rest_{j}", [P, KD, SEQ]) for j in jobs}
        parts = {j: sb(f"parts_{j}", [P, 3, KD, SEQ], BF16) for j in jobs}
        va = [sb(f"va{l}", [P, TPB, H, VW]) for l in range(2)]
        pT = [ps(f"pT{j}", [P, KD, SEQ]) for j in range(2)]
        pJ = [ps(f"pJ{j}", [P, KD, SEQ]) for j in range(2)]
        pV = pJ[1][:, :, :].rearrange("p k (t o) -> p (k t) o", o=D)
        one, ld_x, ld_c, ld_m = sem("one"), sem("ld_x"), sem("ld_c"), sem("ld_m")
        trc, trh, cte, hte, mke = (sem(x) for x in ("trc", "trh", "cte", "hte", "mke"))
        vc, cleared = sem("vc"), sem("cleared", keep=True)
        pj = {j: sem(f"pj_{j}") for j in ("k0", "k1", "q0", "v0", "v1")}
        stp = {j: sem(f"stp_{j}") for j in jobs}
        vev = [sem(f"vev{l}") for l in range(2)]
        kst = {j: sem(f"kst_{j}") for j in ("k0", "k1", "q0", "v0", "v1")}
        FULL, P0, REST, P1, P2 = KD, KD + 1, KD + 2, KD + 3, KD + 4
        dst = {"k0": S.ks[0], "k1": S.ks[1], "q0": S.qs[0]}
        w = {"k0": S.w["wk0"], "k1": S.w["wk1"], "q0": S.w["wq0"], "v0": S.w["wv0"], "v1": S.w["wv1"]}

        def load(e, b):
            need(e, trc, b)
            e.dma_start(cin[:, :, :], a["ctx_1024"][ds(b, 1), :, :].rearrange("o (t p) c -> p (o t) c", p=P)).then_inc(ld_c, 16)
            need(e, mke, b)
            e.dma_start(mi[:, :], a["mask_Bx1xS2_if1"][ds(b, 1), 0, :].broadcast_to([P, SEQ])).then_inc(ld_m, 16)
            need(e, ld_x, 16 * b)
            e.dma_start(S.X[:, ds(b * TPB, TPB), :], a["x"][ds(b, 1), :, :].rearrange("o (t p) c -> p (o t) c", p=P)).then_inc(ld_x, 16)

        def store(e, b):
            for j in ("k0", "v0", "k1", "v1", "q0"):
                if j[0] == "v":
                    l = int(j[1])
                    need(e, vev[l], b + 1)
                    e.dma_start(S.vs[l][ds(b * SEQ, SEQ), :].rearrange("(t p) c -> p t c", p=P),
                                va[l][:, :, :, :].rearrange("p t h c -> p t (h c)")).then_inc(kst[j], 16)
                else:
                    need(e, stp[j], b * P2 + P2)
                    for s in range(3):
                        e.dma_start(dst[j][s, :, ds(b * SEQ, SEQ)].rearrange("(t p) c -> p t c", p=P),
                                    parts[j][:, s, :, :]).then_inc(kst[j], 16)

        with nc.Block() as block:
            @block.sync
            def _(e):
                load(e, 0)
                @loop3(e, B)
                def _(b, last):
                    if not last:
                        load(e, b + 1)
                    store(e, b)
                for j in ("k0", "k1", "q0"):
                    need(e, kst[j], 48 * B)
                for j in ("v0", "v1"):
                    need(e, kst[j], 16 * B)

            @block.tensor
            def _(e):
                def product(j, b, src, out):
                    for t in range(KD):
                        for k in range(KD):
                            last = e.matmul(out[:, t, :], w[j][:, k, t * P:(t + 1) * P], src[:, k, :],
                                            start=(k == 0), stop=(k == KD - 1))
                    last.then_inc(pj[j], 1)

                def values(j, b, src):
                    for t in range(TPB):
                        for k in range(KD):
                            last = e.matmul(pV[:, t, :], src[:, k, t * P:(t + 1) * P], w[j][:, k, :],
                                            start=(k == 0), stop=(k == KD - 1))
                    last.then_inc(pj[j], 1)

                def turn_context(b):
                    need(e, ld_c, 16 * b + 16)
                    need(e, cte, b)
                    turn(e, S, pT[0], cin).then_inc(trc, 1)

                turn_context(0)

                @loop3(e, B)
                def _(b, last):
                    need(e, cte, b + 1)
                    need(e, stp["q0"], (b - 1) * P2 + FULL)
                    product("k0", b, cT, pJ[0])
                    need(e, vev[1], b)
                    values("v0", b, cT)
                    nb.wait(e, b)
                    need(e, hte, b)
                    turn(e, S, pT[1], hn).then_inc(trh, 1)
                    need(e, stp["k0"], b * P2 + FULL)
                    product("k1", b, cT, pJ[0])
                    need(e, vev[0], b + 1)
                    values("v1", b, cT)
                    if not last:
                        turn_context(b + 1)
                    need(e, hte, b + 1)
                    need(e, stp["k1"], b * P2 + FULL)
                    product("q0", b, hT, pJ[0])

            @block.gpsimd
            def _(e):
                e.dma_start(S.ybuf[E * CAP:E * CAP + P, :], S.BIG[:, 0, :]).then_inc(cleared, 16)

                @loop(e, B)
                def _(b):
                    nb.power(e, b, 0)
                    e.dma_start(S.disp[ds(b * ZROWS * P, ZROWS * P), :].rearrange("(p r) d -> p r d", p=P),
                                S.BIG[:, 0:ZROWS, :]).then_inc(cleared, 16)
                need(e, cleared, 16 * (B + 1))

            @block.scalar
            def _(e):
                e.activation(bq4[:, :], S.w["bq"][:, :], ACT.Copy, scale=0.25).then_inc(one, 1)
                need(e, one, 2)
                def take_context(b):
                    need(e, trc, b + 1)
                    need(e, pj["v1"], b)
                    e.activation(cT[:, :, :], pT[0][:, :, :], ACT.Copy).then_inc(cte, 1)

                take_context(0)

                @loop3(e, B)
                def _(b, last):
                    def casts(j):
                        need(e, stp[j], b * P2 + FULL)
                        need(e, kst[j], 48 * b)
                        e.activation(parts[j][:, 0, :, :], full[j][:, :, :], ACT.Copy).then_inc(stp[j], 1)
                        need(e, stp[j], b * P2 + REST)
                        e.activation(parts[j][:, 1, :, :], rest[j][:, :, :], ACT.Copy).then_inc(stp[j], 1)

                    casts("k0")
                    need(e, pj["k1"], b + 1)
                    need(e, stp["k1"], b * P2)
                    for t in range(KD):
                        e.activation(full["k1"][:, t, :], pJ[0][:, t, :], ACT.Copy).then_inc(stp["k1"], 1)
                    casts("k1")
                    need(e, pj["v1"], b + 1)
                    need(e, kst["v1"], 16 * b)
                    e.activation(va[1][:, :, :, 0:DH], pV.rearrange("p t (h c) -> p t h c", h=H), ACT.Copy).then_inc(vev[1], 1)
                    if not last:
                        take_context(b + 1)
                    need(e, pj["q0"], b + 1)
                    need(e, stp["q0"], b * P2)
                    for t in range(KD):
                        e.activation(full["q0"][:, t, :], pJ[0][:, t, :], ACT.Identity, bias=bq4[:, t:t + 1],
                                     scale=0.25).then_inc(stp["q0"], 1)
                    casts("q0")

            @block.vector
            def _(e):
                e.memset(va[0][:, :, :, DH:VW], 1.0).then_inc(vc, 1)
                e.memset(va[1][:, :, :, DH:VW], 1.0).then_inc(vc, 1)
                need(e, vc, 2)
                e.memset(mb[:, :], 0.0).then_inc(one, 1)
                need(e, one, 2)
                def prepare(b):
                    need(e, ld_m, 16 * b + 16)
                    need(e, stp["k0"], (b - 1) * P2 + FULL)
                    e.tensor_scalar(mb[:, :], mi[:, :], 0.0, None, ALU.not_equal).then_inc(mke, 1)
                    need(e, ld_x, 16 * b + 16)
                    need(e, trh, b)
                    x = S.X[:, ds(b * TPB, TPB), :]
                    nb.stats(e, b, 0, x)
                    nb.apply(e, b, 0, x, hn)

                prepare(0)

                @loop3(e, B)
                def _(b, last):
                    def remainders(j):
                        need(e, stp[j], b * P2 + P0)
                        e.tensor_tensor(rest[j][:, :, :], full[j][:, :, :], parts[j][:, 0, :, :], ALU.subtract).then_inc(stp[j], 1)
                        need(e, stp[j], b * P2 + P1)
                        e.tensor_tensor(parts[j][:, 2, :, :], rest[j][:, :, :], parts[j][:, 1, :, :], ALU.subtract).then_inc(stp[j], 1)

                    need(e, mke, b + 1)
                    need(e, pj["k0"], b + 1)
                    need(e, stp["k0"], b * P2)
                    for t in range(KD):
                        e.scalar_tensor_tensor(out=full["k0"][:, t, :], in0=pJ[0][:, t, :], scalar=S.w["bk"][:, t:t + 1],
                                               in1=mb[:, :], op0=ALU.add, op1=ALU.mult).then_inc(stp["k0"], 1)
                    need(e, pj["v0"], b + 1)
                    need(e, kst["v0"], 16 * b)
                    e.tensor_tensor(va[0][:, :, :, 0:DH], pV.rearrange("p t (h c) -> p t h c", h=H),
                                    S.w["bv_b"][:, :].rearrange("p (o h c) -> p o h c", o=1, h=H).broadcast_to([P, TPB, H, DH]),
                                    ALU.add).then_inc(vev[0], 1)
                    need(e, trh, b + 1)
                    need(e, pj["q0"], b)
                    e.tensor_copy(hT[:, :, :], pT[1][:, :, :]).then_inc(hte, 1)
                    remainders("k0")
                    remainders("k1")
                    if not last:
                        prepare(b + 1)
                    remainders("q0")


def attention(S, l):
    nc = S.nc
    ctx, sb, ps, sem = scope(S, f"a{l}")
    SLOTS = 2 * TPB
    NMAX = HG * TPB
    LOADS = 16 * 13
    with ctx:
        q = [sb(f"q{g}", [P, HG, SEQ], BF16) for g in range(G)]
        k = [sb(f"k{g}", [P, HG, SEQ], BF16) for g in range(G)]
        v = [sb(f"v{g}", [P, TPB, HG, VW]) for g in range(G)]
        pexp = [sb(f"pexp{t}", [P, HG, SEQ]) for t in range(TPB)]
        nmax = [sb(f"nmax{g}", [P, NMAX]) for g in range(G)]
        nrest = sb("nrest", [P, NMAX])
        nparts = sb("nparts", [P, P], BF16)
        nT = sb("nT", [3 * NMAX, P], BF16)
        osb = sb("osb", [P, SEQ])
        rden = sb("rden", [P, TPB, HG])
        pmax = [ps(f"pmax{j}", [P, SEQ]) for j in range(2)]
        pscore = [ps(f"pscore{j}", [P, 2, SEQ]) for j in range(2)]
        pout = ps("pout", [P, SEQ])
        pturn = ps("pturn", [P, TPB, P])
        pturn_n = pturn[:, 0, 0:P // 2].bitcast(BF16)[0:P, :]
        ld_ones = [sem(f"ld_ones{g}") for g in range(G)]
        clear, ld_v = sem("clear"), [sem(f"ld_v{g}", keep=True) for g in range(G)]
        ld = [sem(f"ld{g}") for g in range(G)]
        mrow = [sem(f"mrow{g}") for g in range(G)]
        maxed, reduced, cut, nturned, nout = (sem(x) for x in ("maxed", "reduced", "cut", "nturned", "nout"))
        scored, exped, summed, oout, turned, rec, normed = (
            sem(x) for x in ("scored", "exped", "summed", "oout", "turned", "rec", "normed"))

        def groups(body):
            def run(e):
                for g in range(G):
                    body(e, 0, g, g == 0, False)
                with e.Fori(1, B - 1) as b:
                    for g in range(G):
                        body(e, b, g, False, False)
                for g in range(G):
                    body(e, B - 1, g, False, True)
            return run

        def ahead(b, g, by):
            return (b, g + by) if g + by < G else (b + 1, g + by - G)

        with nc.Block() as block:
            @block.sync
            def _(e):
                def load(b, g):
                    at = ds(b * SEQ, SEQ)
                    for j in range(6):
                        for buf, src, part in ((q, S.qs[l], Q_PARTS[j]), (k, S.ks[l], K_PARTS[j])):
                            e.dma_start(buf[g][j * DH:(j + 1) * DH, :, :],
                                        src[part, g * HG * DH:(g + 1) * HG * DH, at].rearrange("(h d) t -> d h t", d=DH)
                                        ).then_inc(ld[g], 16)
                    e.dma_start(k[g][PARTS_ROWS:ALL_ROWS, :, :],
                                S.extra[l][:, at].rearrange("s (o t) -> s o t", o=1).broadcast_to([6, HG, SEQ])
                                ).then_inc(ld[g], 16)

                def maxima(b, g):
                    need(e, nout, b * G + g + 1)
                    for s in range(3):
                        e.dma_start(q[g][MAX_ROWS + s:MAX_ROWS + s + 1, :, :].rearrange("o h (t c) -> o (h t) c", c=P),
                                    nT[s * NMAX:(s + 1) * NMAX, :]).then_inc(mrow[g], 16)

                def body(e, b, g, first, last):
                    if not (last and g == G - 1):
                        maxima(*ahead(b, g, 1))
                    if not last:
                        need(e, scored, (b * G + g + 1) * SLOTS)
                        load(b + 1, g)

                for g in range(G):
                    load(0, g)
                    e.dma_start(q[g][PARTS_ROWS:MAX_ROWS, :, :],
                                S.extra[l][3:6, 0:SEQ].rearrange("s (o t) -> s o t", o=1).broadcast_to([3, HG, SEQ])
                                ).then_inc(ld_ones[g], 16)
                maxima(0, 0)
                groups(body)(e)

            @block.gpsimd
            def _(e):
                e.memset(nparts[:, :], 0.0).then_inc(cut, 1)

                def load_v(b, g):
                    e.dma_start(v[g][:, :, :, :].rearrange("p t h c -> p t (h c)"),
                                S.vs[l][ds(b * SEQ, SEQ), g * HG * VW:(g + 1) * HG * VW].rearrange("(t p) c -> p t c", p=P)
                                ).then_inc(ld_v[g], 16)

                def parts(b, g):
                    n = b * G + g
                    need(e, reduced, (n + 1) * NMAX)
                    need(e, nturned, n)
                    need(e, cut, 4 * n + 1)
                    gate(S, e)
                    e.tensor_copy(nparts[:, 0:NMAX], nmax[g][:, :]).then_inc(cut, 1)
                    need(e, cut, 4 * n + 2)
                    e.tensor_tensor(nrest[:, :], nmax[g][:, :], nparts[:, 0:NMAX], ALU.subtract).then_inc(cut, 1)
                    need(e, cut, 4 * n + 3)
                    gate(S, e)
                    e.tensor_copy(nparts[:, NMAX:2 * NMAX], nrest[:, :]).then_inc(cut, 1)
                    need(e, cut, 4 * n + 4)
                    e.tensor_tensor(nparts[:, 2 * NMAX:3 * NMAX], nrest[:, :], nparts[:, NMAX:2 * NMAX],
                                    ALU.subtract).then_inc(cut, 1)

                def body(e, b, g, first, last):
                    n = b * G + g
                    if not first and not (last and g > 0):
                        need(e, summed, n * TPB)
                        load_v(*((b, G - 1) if g == 0 else (b + 1, g - 1)))
                    if not (last and g >= G - 2):
                        parts(*ahead(b, g, 2))

                for g in range(G):
                    load_v(0, g)
                parts(0, 0)
                parts(0, 1)
                groups(body)(e)

            @block.tensor
            def _(e):
                def max_product(b, g, j):
                    n, h, t = b * G + g, j // TPB, j % TPB
                    need(e, reduced, n * NMAX + j - 1)
                    e.matmul(pmax[j % 2][:, :], q[g][0:MAX_ROWS, h, t * P:(t + 1) * P], k[g][0:MAX_ROWS, h, :],
                             start=True, stop=True).then_inc(maxed, 1)

                def turn_maxima(b, g):
                    n = b * G + g
                    need(e, cut, 4 * n + 5)
                    need(e, normed, n - 2)
                    e.transpose(pturn_n, nparts[:, :], S.identb[:, :]).then_inc(nturned, 1)

                def values(b, g, t):
                    n = b * G + g
                    if t == 0:
                        need(e, ld_v[g], 16 * b + 16)
                        need(e, oout, n)
                    need(e, exped, n * SLOTS + 2 * t + 2)
                    for h in range(HG):
                        last = e.matmul(pout[32 * h:32 * h + VW, :], v[g][:, t, h, :], pexp[t][:, h, :],
                                        start=(t == 0), stop=(t == TPB - 1))
                    last.then_inc(summed, 1)

                def turn_outputs(n, nturns):
                    need(e, oout, n + 1)
                    need(e, nout, nturns)
                    need(e, normed, n)
                    for t in range(TPB):
                        last = e.transpose(pturn[:, t, :], osb[:, t * P:(t + 1) * P], S.ident[:, :])
                    last.then_inc(turned, 1)

                def body(e, b, g, first, last):
                    n = b * G + g
                    for s in range(SLOTS):
                        t, pair = s // 2, s % 2
                        if not (first and s < 2):
                            need(e, exped, n * SLOTS + s - 1)
                        if s == 0:
                            need(e, mrow[g], 48 * b + 48)
                        for h in (2 * pair, 2 * pair + 1):
                            mm = e.matmul(pscore[s % 2][:, h % 2, :], k[g][0:ALL_ROWS, h, t * P:(t + 1) * P],
                                          q[g][0:ALL_ROWS, h, :], start=True, stop=True)
                        mm.then_inc(scored, 1)
                        if not (last and g >= G - 2):
                            b2, g2 = ahead(b, g, 2)
                            if s == 0:
                                need(e, ld[g2], LOADS * b2 + LOADS)
                            max_product(b2, g2, 2 * s)
                            max_product(b2, g2, 2 * s + 1)
                        if s == 1:
                            if not first:
                                values(*((b, g - 1) if g else (b - 1, G - 1)), TPB - 1)
                            if not (last and g == G - 1):
                                turn_maxima(*ahead(b, g, 1))
                        if s >= 3 and s % 2:
                            values(b, g, (s - 3) // 2)
                        if s == 4 and not first:
                            turn_outputs(n - 1, n + (1 if last and g == G - 1 else 2))

                need(e, clear, 1)
                for g in range(G):
                    if g < 2:
                        need(e, ld[g], LOADS)
                    need(e, ld_ones[g], 16)
                    if g >= 2:
                        continue
                    for j in range(NMAX):
                        max_product(0, g, j)
                    if g == 0:
                        turn_maxima(0, 0)
                groups(body)(e)
                values(B - 1, G - 1, TPB - 1)
                turn_outputs(B * G - 1, B * G)

            @block.scalar
            def _(e):
                def take_outputs(n):
                    need(e, summed, (n + 1) * TPB)
                    need(e, turned, n)
                    e.activation(osb[:, :], pout[:, :], ACT.Copy).then_inc(oout, 1)

                def body(e, b, g, first, last):
                    n = b * G + g
                    for s in range(SLOTS):
                        t, pair = s // 2, s % 2
                        need(e, scored, n * SLOTS + s + 1)
                        if pair == 0 and not first:
                            need(e, summed, n * TPB + t - (TPB - 1))
                        e.activation(pexp[t][:, 2 * pair:2 * pair + 2, :], pscore[s % 2][:, :, :], ACT.Exp).then_inc(exped, 1)
                        if s == 2 and not first:
                            take_outputs(n - 1)

                groups(body)(e)
                take_outputs(B * G - 1)

            @block.vector
            def _(e):
                e.memset(pout[:, :], 0.0).then_inc(clear, 1)

                def reduce(b, g, js):
                    n = b * G + g
                    for j in js:
                        if j == 0:
                            need(e, cut, 4 * n - 11)
                        need(e, maxed, n * NMAX + j + 1)
                        e.tensor_reduce(nmax[g][:, j:j + 1], pmax[j % 2][:, :], AX.X, ALU.max,
                                        negate=True).then_inc(reduced, 1)

                def take_maxima(b, g):
                    n = b * G + g
                    need(e, nturned, n + 1)
                    pb, pg = (b, g - 1) if g else (b - 1, G - 1)
                    need(e, mrow[pg], 48 * pb + 48)
                    e.tensor_copy(nT[:, :], pturn_n[0:3 * NMAX, :]).then_inc(nout, 1)

                def normalise(b, g):
                    n = b * G + g
                    turn = pturn[:, :, :].rearrange("p t (h c) -> p t h c", c=32)
                    need(e, turned, n + 1)
                    e.reciprocal(rden[:, :, :], turn[:, :, :, DH]).then_inc(rec, 1)
                    need(e, rec, n + 1)
                    e.tensor_tensor(S.BIG[:, ds(b * TPB, TPB), g * HG * DH:(g + 1) * HG * DH].rearrange("p t (h c) -> p t h c", c=DH),
                                    turn[:, :, :, 0:DH],
                                    rden[:, :, :].rearrange("p t (h o) -> p t h o", o=1).broadcast_to([P, TPB, HG, DH]),
                                    ALU.mult).then_inc(normed, 1)

                def body(e, b, g, first, last):
                    ahead2 = None if last and g >= G - 2 else ahead(b, g, 2)
                    if ahead2:
                        reduce(*ahead2, range(0, 4))
                    if not (last and g == G - 1):
                        take_maxima(*ahead(b, g, 1))
                    if ahead2:
                        reduce(*ahead2, range(4, 12))
                    if not first:
                        normalise(*((b, g - 1) if g else (b - 1, G - 1)))
                    if ahead2:
                        reduce(*ahead2, range(12, NMAX))

                reduce(0, 0, range(NMAX))
                reduce(0, 1, range(2))
                take_maxima(0, 0)
                reduce(0, 1, range(2, NMAX))
                groups(body)(e)
                normalise(B - 1, G - 1)


def tiles(b):
    return ds(b * TPB, TPB)


def turn(e, S, out, src):
    for k in range(KD):
        for t in range(TPB):
            last = e.transpose(out[:, k, t * P:(t + 1) * P], src[:, t, k * P:(k + 1) * P], S.ident[:, :])
    return last


def apply_weight(e, out, srcT, w):
    for t in range(TPB):
        for k in range(KD):
            last = e.matmul(out[:, t, :], srcT[:, k, t * P:(t + 1) * P], w[:, k, :], start=(k == 0), stop=(k == KD - 1))
    return last


def over_tiles(v, n=TPB):
    return v[:, :].rearrange("p (o d) -> p o d", o=1).broadcast_to([P, n, D])


def route(S):
    nc = S.nc
    ctx, sb, ps, sem = scope(S, "r")
    with ctx:
        att = sb("att", [P, TPB, D])
        attT = sb("attT", [P, KD, SEQ])
        yb = sb("yb", [P, TPB, D])
        hn = sb("hn", [P, TPB, D])
        hT = sb("hT", [P, KD, SEQ])
        nb = Norm(S, sb, sem)
        pA, pH, pY = (ps(x, [P, KD, SEQ]) for x in ("pA", "pH", "pY"))
        pYt = pY[:, :, :].rearrange("p k (t o) -> p (k t) o", o=D)
        pL = ps("pL", [P, TPB, E])
        staged, tra, ate, yd, ybd, upd, kept, trh, hte, ld, lkept = (
            sem(x) for x in ("staged", "tra", "ate", "yd", "ybd", "upd", "kept", "trh", "hte", "ld", "lkept"))

        with nc.Block() as block:
            @block.tensor
            def _(e):
                def turn_attention(b):
                    need(e, staged, b + 1)
                    need(e, ate, b)
                    turn(e, S, pA, att).then_inc(tra, 1)

                def output(b):
                    need(e, ate, b + 1)
                    need(e, ybd, b)
                    apply_weight(e, pYt, attT, S.w["wo0"]).then_inc(yd, 1)

                def turn_normed(b):
                    nb.wait(e, b)
                    need(e, hte, b)
                    turn(e, S, pH, hn).then_inc(trh, 1)

                def logits(b):
                    need(e, hte, b + 1)
                    need(e, lkept, b)
                    apply_weight(e, pL, hT, S.w["wg"]).then_inc(ld, 1)

                turn_attention(0)
                output(0)

                @rounds(e, 2, 1)
                def _(i, j, k):
                    if inside(i + 1):
                        turn_attention(i + 1)
                    if inside(i - 2):
                        logits(i - 2)
                    if inside(i + 1):
                        output(i + 1)
                    if inside(i - 1):
                        turn_normed(i - 1)

            @block.scalar
            def _(e):
                def stage(b):
                    need(e, tra, b)
                    gate(S, e)
                    e.activation(att[:, :, :], S.BIG[:, tiles(b), :], ACT.Copy).then_inc(staged, 1)

                def take_attention(b):
                    need(e, tra, b + 1)
                    need(e, yd, b)
                    e.activation(attT[:, :, :], pA[:, :, :], ACT.Copy).then_inc(ate, 1)

                def keep(b):
                    nb.wait(e, b)
                    need(e, staged, b + 1)
                    gate(S, e)
                    e.activation(S.BIG[:, tiles(b), :], hn[:, :, :], ACT.Copy).then_inc(kept, 1)

                def take_normed(b):
                    need(e, trh, b + 1)
                    need(e, ld, b)
                    e.activation(hT[:, :, :], pH[:, :, :], ACT.Copy).then_inc(hte, 1)

                stage(0)
                take_attention(0)
                stage(1)

                @rounds(e, 2, 2)
                def _(i, j, k):
                    if inside(i + 1):
                        take_attention(i + 1)
                    if inside(i + 2):
                        stage(i + 2)
                    if inside(i - 1):
                        keep(i - 1)
                        take_normed(i - 1)

            @block.gpsimd
            def _(e):
                @rounds(e, 0)
                def _(b, j, k):
                    nb.power(e, b, j)

            @block.vector
            def _(e):
                @rounds(e, 2)
                def _(i, j, k):
                    if inside(i):
                        x = S.X[:, tiles(i), :]
                        need(e, yd, i + 1)
                        need(e, upd, i)
                        e.tensor_tensor(yb[:, :, :], pYt, over_tiles(S.w["bo_b"]), ALU.add).then_inc(ybd, 1)
                        need(e, ybd, i + 1)
                        e.scalar_tensor_tensor(out=x, in0=yb[:, :, :], scalar=S.tg[:, 0:1], in1=x,
                                               op0=ALU.mult, op1=ALU.add).then_inc(upd, 1)
                        need(e, upd, i + 1)
                        nb.stats(e, i, j, x)
                    if inside(i - 2):
                        need(e, ld, i - 1)
                        e.tensor_copy(S.logit[:, tiles(i - 2), :], pL[:, :, :]).then_inc(lkept, 1)
                    if inside(i - 1):
                        need(e, kept, i - 1)
                        need(e, trh, i - 1)
                        nb.apply(e, i - 1, 1 - j, S.X[:, tiles(i - 1), :], hn)


def place(S):
    nc = S.nc
    ctx, sb, ps, sem = scope(S, "l")
    SET = 2
    with ctx:
        tot = sb("tot", [P, 2 * E, NT])
        scan = [sb(f"scan{j}", [P, 2 * E, NT]) for j in range(2)]
        loc = sb("loc", [P, 2 * E, NT])
        mine = sb("mine", [P, 2 * E, NT])
        sel, pos, keep, off, spare, t1, t2, t3, t4 = (sb(x, [P, 2, NT]) for x in (
            "sel", "pos", "keep", "off", "spare", "t1", "t2", "t3", "t4"))
        rows = [sb(f"rows{j}", [P, TPB, D]) for j in range(SET)]
        at = [sb(f"at{j}", [P, 2, TPB], I32) for j in range(SET)]
        lmax, lsum, rsum, gs, gc, gr = (sb(x, [P, NT]) for x in ("lmax", "lsum", "rsum", "gs", "gc", "gr"))
        less, ex, score, is_top, rank = (sb(x, [P, NT, E]) for x in ("less", "ex", "score", "is_top", "rank"))
        top, topr = sb("top", [P, 2, NT]), sb("topr", [P, 2, NT])
        pC, pT = ps("pC", [P, 2 * E, NT]), ps("pT", [P, 2 * E, NT])
        mm, sp, vc, exd, chosen = sem("mm"), sem("sp"), sem("vc"), sem("exd"), sem("chosen")
        copied = [sem(f"copied{j}") for j in range(SET)]
        listed = [sem(f"listed{j}") for j in range(SET)]
        put = [sem(f"put{j}", keep=True) for j in range(SET)]
        with nc.Block() as block:
            @block.tensor
            def _(e):
                need(e, chosen, 1)
                flat = S.onehot[:, :, :].rearrange("p e t -> p (e t)")
                e.matmul(pC[:, :, :].rearrange("p e t -> p (e t)"), S.triu[:, :], flat, start=True, stop=True).then_inc(mm, 1)
                e.matmul(pT[:, :, :].rearrange("p e t -> p (e t)"), S.onesb[:, :], flat, start=True, stop=True).then_inc(mm, 1)

            @block.scalar
            def _(e):
                need(e, vc, 2)
                e.activation(ex[:, :, :], less[:, :, :], ACT.Exp).then_inc(exd, 1)
                @loop(e, B // SET)
                def _(i):
                    for j in range(SET):
                        need(e, put[j], 16 * 2 * TPB * i)
                        gate(S, e)
                        e.activation(rows[j][:, :, :], S.BIG[:, ds((i * SET + j) * TPB, TPB), :], ACT.Copy).then_inc(copied[j], 1)

            @block.vector
            def _(e):
                c = Chain(vc)
                c.begin(0)
                each_expert = lambda v: v.rearrange("p (t o) -> p t o", o=1).broadcast_to([P, NT, E])
                c.did(e.tensor_reduce(lmax[:, :], S.logit[:, :, :], AX.X, ALU.max))
                c.wait(e)
                c.did(e.tensor_tensor(less[:, :, :], S.logit[:, :, :], each_expert(lmax[:, :]), ALU.subtract))
                need(e, exd, 1)
                c.did(e.tensor_reduce(lsum[:, :], ex[:, :, :], AX.X, ALU.add))
                c.wait(e)
                c.did(e.reciprocal(rsum[:, :], lsum[:, :]))
                c.wait(e)
                c.did(e.tensor_tensor(score[:, :, :], ex[:, :, :], each_expert(rsum[:, :]), ALU.mult))
                c.wait(e)
                for kk in range(2):
                    c.did(e.tensor_reduce(top[:, kk, :], score[:, :, :], AX.X, ALU.max))
                    c.wait(e)
                    c.did(e.tensor_tensor(is_top[:, :, :], score[:, :, :], each_expert(top[:, kk, :]), ALU.is_equal))
                    c.wait(e)
                    ranks = S.rank8[:, :].rearrange("p (o x) -> p o x", o=1).broadcast_to([P, NT, E])
                    c.did(e.tensor_tensor(rank[:, :, :], is_top[:, :, :], ranks, ALU.mult))
                    c.wait(e)
                    c.did(e.tensor_reduce(topr[:, kk, :], rank[:, :, :], AX.X, ALU.max))
                    c.wait(e)
                    c.did(e.tensor_tensor(is_top[:, :, :], ranks, each_expert(topr[:, kk, :]), ALU.is_equal))
                    c.wait(e)
                    ins = e.tensor_copy(S.onehot[:, kk * E:(kk + 1) * E, :].rearrange("p x t -> p t x"), is_top[:, :, :])
                    if kk == 0:
                        c.did(ins)
                        c.did(e.scalar_tensor_tensor(out=score[:, :, :], in0=is_top[:, :, :], scalar=-2.0, in1=score[:, :, :],
                                                     op0=ALU.mult, op1=ALU.add))
                        c.wait(e)
                    else:
                        ins.then_inc(chosen, 1)
                c.did(e.tensor_scalar(S.idx[:, :, :], topr[:, :, :], -1.0, float(E), ALU.mult, ALU.add))
                c.did(e.tensor_tensor(gs[:, :], top[:, 0, :], top[:, 1, :], ALU.add))
                c.wait(e)
                c.did(e.tensor_scalar(gc[:, :], gs[:, :], 1.1920929e-07, None, ALU.max))
                c.wait(e)
                c.did(e.reciprocal(gr[:, :], gc[:, :]))
                c.wait(e)
                c.did(e.tensor_tensor(S.gate[:, :, :], top[:, :, :],
                                      gr[:, :].rearrange("p (o t) -> p o t", o=1).broadcast_to([P, 2, NT]), ALU.mult))
                need(e, chosen, 1)
                need(e, mm, 2)
                c.did(e.tensor_copy(tot[:, :, :], pT[:, :, :]))
                c.wait(e)
                src = tot
                for n, d in enumerate((1, 2, 4, 8, 16)):
                    dst = scan[n % 2]
                    c.did(e.tensor_tensor(dst[:, :, d:NT], src[:, :, d:NT], src[:, :, 0:NT - d], ALU.add))
                    c.did(e.tensor_copy(dst[:, :, 0:d], src[:, :, 0:d]))
                    c.wait(e)
                    src = dst
                c.did(e.tensor_tensor(loc[:, :, :], src[:, :, :], tot[:, :, :], ALU.subtract))
                c.wait(e)
                c.did(e.tensor_tensor(mine[:, :, :], loc[:, :, :], pC[:, :, :], ALU.add))
                c.wait(e)
                c.did(e.tensor_tensor(mine[:, E:2 * E, :], mine[:, E:2 * E, :],
                                      src[:, 0:E, NT - 1:NT].broadcast_to([P, E, NT]), ALU.add))
                c.wait(e)
                c.did(e.tensor_tensor(loc[:, :, :], mine[:, :, :], S.onehot[:, :, :], ALU.mult))
                c.wait(e)
                for kk in range(2):
                    c.did(e.tensor_reduce(sel[:, kk, :], loc[:, kk * E:(kk + 1) * E, :].rearrange("p x t -> p t x"), AX.X, ALU.add))
                c.wait(e)
                c.did(e.tensor_scalar(t1[:, :, :], sel[:, :, :], -1.0, None, ALU.add))
                c.wait(e)
                c.did(e.tensor_scalar(keep[:, :, :], t1[:, :, :], float(CAP), None, ALU.is_lt))
                c.did(e.scalar_tensor_tensor(out=pos[:, :, :], in0=S.idx[:, :, :], scalar=float(CAP), in1=t1[:, :, :],
                                             op0=ALU.mult, op1=ALU.add))
                c.wait(e)
                c.did(e.tensor_tensor(S.gate[:, :, :], S.gate[:, :, :], keep[:, :, :], ALU.mult))
                c.did(e.tensor_scalar(t2[:, :, :], pos[:, :, :], -float(E * CAP), None, ALU.add))
                c.wait(e)
                c.did(e.tensor_tensor(t3[:, :, :], t2[:, :, :], keep[:, :, :], ALU.mult))
                c.wait(e)
                c.did(e.tensor_scalar(S.row_get[:, :, :], t3[:, :, :], float(E * CAP), None, ALU.add))
                need(e, sp, 1)
                c.did(e.tensor_tensor(t4[:, :, :], pos[:, :, :], spare[:, :, :], ALU.subtract))
                c.wait(e)
                c.did(e.tensor_tensor(off[:, :, :], t4[:, :, :], keep[:, :, :], ALU.mult))
                c.wait(e)
                c.did(e.tensor_tensor(S.row_put[:, :, :], off[:, :, :], spare[:, :, :], ALU.add))
                c.wait(e)
                @loop(e, B // SET)
                def _(i):
                    for j in range(SET):
                        need(e, put[j], 16 * 2 * TPB * i)
                        e.tensor_copy(at[j][:, :, :], S.row_put[:, :, ds((i * SET + j) * TPB, TPB)]).then_inc(listed[j], 1)

            @block.gpsimd
            def _(e):
                e.iota(spare[:, :, :], pattern=[[N, 2], [P, NT]], base=E * CAP, channel_multiplier=1,
                       allow_small_or_imprecise_dtypes=True).then_inc(sp, 1)
                @loop(e, B // SET)
                def _(i):
                    for j in range(SET):
                        need(e, copied[j], i + 1)
                        need(e, listed[j], i + 1)
                        gate(S, e)
                        for kk in range(2):
                            for t in range(TPB):
                                e.indirect_dma_start(S.disp[:, :], bass.IndirectOffsetOnAxis(ap=at[j][:, kk, t:t + 1], axis=0),
                                                     rows[j][:, t, :], None).then_inc(put[j], 16)
                for j in range(SET):
                    need(e, put[j], 16 * 2 * TPB * (B // SET))


def experts(S):
    nc, a = S.nc, S.a
    ctx, sb, ps, sem = scope(S, "e")
    HI, LO = range(2)
    PASSES = ((HI, HI), (HI, LO), (LO, HI))
    with ctx:
        parts = lambda name, shape: [sb(f"{name}_{p}", shape, F32R) for p in ("hi", "lo")]
        raw1 = sb("raw1", [P, KF, D])
        w1T = [parts(f"w1T{x}", [P, KD, FF]) for x in range(2)]
        raw2 = sb("raw2", [P, KF, D])
        w2 = [parts(f"w2{x}", [P, KF, D]) for x in range(2)]
        b2 = [sb(f"b2{x}", [P, D]) for x in range(2)]
        rowsT = [parts(f"rowsT{j}", [P, KD, CHUNK]) for j in range(2)]
        full = [sb(f"full{q}", [P, 2, CHUNK]) for q in range(2)]
        hid = parts("hid", [P, KF, CHUNK])
        rows = [S.w["wq0"], S.w["wk0"]]
        y = [S.w["wv0"], S.w["wo0"]]
        pw = [ps(f"pw{j}", [P, 4, P]) for j in range(2)]
        pX = ps("pX", [P, KD, CHUNK])
        pH = [ps(f"pH{j}", [P, 2, CHUNK]) for j in range(KF // 2)]
        pY = ps("pY", [P, 2, D])
        ldw1, ldw2 = sem("ldw1"), sem("ldw2")
        ldb = [sem(f"ldb{x}") for x in range(2)]
        ldr = [sem(f"ldr{j}") for j in range(2)]
        trw, wte, w2e, trr, rte, up, act, hi, lo, down, ye, scaled = (
            sem(x) for x in ("trw", "wte", "w2e", "trr", "rte", "up", "act", "hi", "lo", "down", "ye", "scaled"))
        yst = [sem(f"yst{j}", keep=True) for j in range(2)]
        WG = 4
        HQ = KF // 2

        def pairs(body):
            def run(e):
                @loop(e, E // 2 - 1)
                def _(i):
                    body(e, i, False)
                body(e, E // 2 - 1, True)
            return run

        with nc.Block() as block:
            @block.sync
            def _(e):
                def load_fc1(n):
                    need(e, trw, n * WG)
                    e.dma_start(raw1[:, :, :], a["L0_ffn_fc1_w"][ds(n, 1), :, :].rearrange("o (j p) d -> p (o j) d", p=P)).then_inc(ldw1, 16)

                def load_fc2(n, x):
                    need(e, w2e, n * 2 * WG)
                    e.dma_start(raw2[:, :, :], a["L0_ffn_fc2_w"][ds(n, 1), :, :].rearrange("o (j p) d -> p (o j) d", p=P)).then_inc(ldw2, 16)
                    need(e, ye, (n - 1) * NCH)
                    e.dma_start(b2[x][:, :], a["L0_ffn_fc2_b"][ds(n, 1), :].broadcast_to([P, D])).then_inc(ldb[x], 16)

                def load_rows(m, j):
                    e.dma_start(rows[j][:, :, :], S.disp[ds(m * CHUNK, CHUNK), :].rearrange("(t p) d -> p t d", p=P)).then_inc(ldr[j], 16)

                def body(e, i, last):
                    for x in range(2):
                        n = i * 2 + x
                        for ch in range(NCH):
                            m, j = n * NCH + ch, (x * NCH + ch) % 2
                            if not (last and x == 1 and ch >= NCH - 2):
                                need(e, trr, m + 1)
                                load_rows(m + 2, j)
                            if ch == NCH - 1 and not last:
                                load_fc1(n + 2)
                                load_fc2(n + 2, x)

                load_fc1(0)
                load_rows(0, 0)
                load_rows(1, 1)
                load_fc2(0, 0)
                load_fc1(1)
                load_fc2(1, 1)
                pairs(body)(e)

            @block.tensor
            def _(e):
                def turn_weights(n, x, w):
                    m, k, j0 = n * WG + w, w // 2, (w % 2) * 4
                    if w == 0:
                        need(e, ldw1, (n + 1) * 16)
                    need(e, wte, (m - 1) * 2)
                    for j in range(4):
                        last = e.transpose(pw[w % 2][:, j, :], raw1[:, j0 + j, k * P:(k + 1) * P], S.ident[:, :])
                    last.then_inc(trw, 1)

                def turn_rows(m, j, loads):
                    need(e, ldr[j], 16 * loads)
                    need(e, rte, 2 * m)
                    for k in range(KD):
                        for t in range(2):
                            last = e.transpose(pX[:, k, t * P:(t + 1) * P], rows[j][:, t, k * P:(k + 1) * P], S.ident[:, :])
                    last.then_inc(trr, 1)

                def body(e, i, last):
                    for x in range(2):
                        n = i * 2 + x
                        for ch in range(NCH):
                            mi = x * NCH + ch
                            m, j = n * NCH + ch, mi % 2
                            need(e, rte, 2 * m + 2)
                            if ch == 0:
                                need(e, wte, (n + 1) * WG * 2)
                            for q in range(HQ):
                                need(e, act, (m - 1) * HQ + q + 1)
                                for f in (2 * q, 2 * q + 1):
                                    for k in range(KD):
                                        for n_pass, (pl, pr) in enumerate(PASSES):
                                            mm = e.matmul(pH[q][:, f % 2, :], w1T[x][pl][:, k, f * P:(f + 1) * P],
                                                          rowsT[j][pr][:, k, :], start=(k == 0 and n_pass == 0),
                                                          stop=(k == KD - 1 and n_pass == 2))
                                mm.then_inc(up, 1)
                            if not (last and mi == 2 * NCH - 1):
                                turn_rows(m + 1, (mi + 1) % 2, i * NCH + (mi + 1) // 2 + 1)
                            if ch < WG and not (last and x == 1):
                                turn_weights(n + 1, 1 - x, ch)
                            if ch == 0:
                                need(e, w2e, (n + 1) * 2 * WG)
                            need(e, ye, m)
                            for t in range(2):
                                for f in range(KF):
                                    if t == 0 and f % 2 == 0:
                                        need(e, lo, m * HQ + f // 2 + 1)
                                    for n_pass, (pl, pr) in enumerate(PASSES):
                                        mm = e.matmul(pY[:, t, :], hid[pl][:, f, t * P:(t + 1) * P], w2[x][pr][:, f, :],
                                                      start=(f == 0 and n_pass == 0), stop=(f == KF - 1 and n_pass == 2))
                            mm.then_inc(down, 1)

                for w in range(WG):
                    turn_weights(0, 0, w)
                turn_rows(0, 0, 1)
                pairs(body)(e)

            @block.scalar
            def _(e):
                def body(e, i, last):
                    for x in range(2):
                        n = i * 2 + x
                        for ch in range(NCH):
                            m = n * NCH + ch
                            for q in range(HQ):
                                hq = m * HQ + q
                                need(e, up, hq + 1)
                                need(e, lo, hq - 1)
                                gate(S, e)
                                for f in (2 * q, 2 * q + 1):
                                    ins = e.activation(full[q % 2][:, f % 2, :], pH[q][:, f % 2, :], ACT.Silu,
                                                       bias=S.b1T[:, ds(n * KF + f, 1)])
                                ins.then_inc(act, 1)
                                if q == 0:
                                    need(e, down, m)
                                need(e, act, hq + 1)
                                e.activation(hid[HI][:, 2 * q:2 * q + 2, :], full[q % 2][:, :, :], ACT.Copy).then_inc(hi, 1)
                pairs(body)(e)

            @block.vector
            def _(e):
                def cut(hi, lo, src, count, before):
                    e.tensor_copy(hi, src).then_inc(count, 1)
                    need(e, count, before + 1)
                    e.tensor_tensor(lo, src, hi, ALU.subtract).then_inc(count, 1)

                def take_weights(n, x, w):
                    m, k, j0 = n * WG + w, w // 2, (w % 2) * 4
                    need(e, trw, m + 1)
                    cut(w1T[x][HI][:, k, j0 * P:(j0 + 4) * P], w1T[x][LO][:, k, j0 * P:(j0 + 4) * P],
                        pw[w % 2][:, :, :], wte, 2 * m)

                def cut_fc2(n, x, w):
                    if w == 0:
                        need(e, ldw2, (n + 1) * 16)
                    at = slice(2 * w, 2 * w + 2)
                    cut(w2[x][HI][:, at, :], w2[x][LO][:, at, :], raw2[:, at, :], w2e, 2 * (n * WG + w))

                def take_rows(m, j):
                    need(e, trr, m + 1)
                    cut(rowsT[j][HI][:, :, :], rowsT[j][LO][:, :, :], pX[:, :, :], rte, 2 * m)

                def body(e, i, last):
                    for x in range(2):
                        n = i * 2 + x
                        for ch in range(NCH):
                            mi = x * NCH + ch
                            m, j = n * NCH + ch, mi % 2
                            more = ch < WG and not (last and x == 1)
                            for q in range(HQ):
                                hq = m * HQ + q
                                need(e, hi, hq + 1)
                                e.tensor_tensor(hid[LO][:, 2 * q:2 * q + 2, :], full[q % 2][:, :, :],
                                                hid[HI][:, 2 * q:2 * q + 2, :], ALU.subtract).then_inc(lo, 1)
                                if q == 0 and more:
                                    cut_fc2(n + 1, 1 - x, ch)
                            if not (last and mi == 2 * NCH - 1):
                                take_rows(m + 1, (mi + 1) % 2)
                            if more:
                                take_weights(n + 1, 1 - x, ch)
                            need(e, down, m + 1)
                            if ch == 0:
                                need(e, ldb[x], (i + 1) * 16)
                            need(e, yst[j], 16 * (i * NCH + mi // 2))
                            e.tensor_tensor(y[j][:, :, :], pY[:, :, :], over_tiles(b2[x], 2), ALU.add).then_inc(ye, 1)

                for w in ("gamma_b", "beta_b"):
                    e.tensor_scalar(S.w[w][:, :], S.w[w][:, :], S.tg[:, 2:3], None, ALU.mult).then_inc(scaled, 1)
                need(e, scaled, 2)
                e.tensor_tensor(S.X[:, :, :], S.X[:, :, :], over_tiles(S.w["beta_b"], NT), ALU.add).then_inc(scaled, 1)
                for w in range(WG):
                    take_weights(0, 0, w)
                take_rows(0, 0)
                for w in range(WG):
                    cut_fc2(0, 0, w)
                pairs(body)(e)

            @block.gpsimd
            def _(e):
                def body(e, i, last):
                    for mi in range(2 * NCH):
                        m = i * 2 * NCH + mi
                        need(e, ye, m + 1)
                        e.dma_start(S.ybuf[ds(m * CHUNK, CHUNK), :].rearrange("(t p) d -> p t d", p=P), y[mi % 2][:, :, :]
                                    ).then_inc(yst[mi % 2], 16)
                pairs(body)(e)
                for j in range(2):
                    need(e, yst[j], 16 * NCH * (E // 2))


def combine(S):
    nc = S.nc
    ctx, sb, ps, sem = scope(S, "c")
    with ctx:
        at = [sb(f"at{j}", [P, 2, TPB], I32) for j in range(2)]
        yg = [sb(f"yg{j}", [P, 2, TPB, D]) for j in range(2)]
        acc = sb("acc", [P, 2, TPB, D])
        r = sb("r", [P, TPB, D])
        hn = sb("hn", [P, TPB, D])
        hT = sb("hT", [P, KD, SEQ])
        nb1, nb2 = Norm(S, sb, sem, "1", 1), Norm(S, sb, sem, "2", 1)
        full, rest = sb("full", [P, KD, SEQ]), sb("rest", [P, KD, SEQ])
        parts = sb("parts", [P, 3, KD, SEQ], BF16)
        pH, pQ = ps("pH", [P, KD, SEQ]), ps("pQ", [P, KD, SEQ])
        got = [[sem(f"got{j}{kk}", keep=True) for kk in range(2)] for j in range(2)]
        listed, added, centred, upd, trh, hte, qd, cutq, qst = (
            sem(x) for x in ("listed", "added", "centred", "upd", "trh", "hte", "qd", "cutq", "qst"))
        ADDS = 2 * TPB
        FULL, P0, REST, P1, P2 = 1, 2, 3, 4, 5

        with nc.Block() as block:
            @block.gpsimd
            def _(e):
                def list_rows(b, j, k):
                    for kk in range(2):
                        need(e, got[j][kk], 16 * TPB * k)
                    gate(S, e)
                    e.tensor_copy(at[j][:, :, :], S.row_get[:, :, tiles(b)]).then_inc(listed, 1)
                    need(e, listed, b + 1)
                    gate(S, e)
                    need(e, added, (b - 1) * ADDS)
                    gate(S, e)

                def gather(j, first, last):
                    for kk, t in [(n // TPB, n % TPB) for n in range(first, last)]:
                        e.indirect_dma_start(yg[j][:, kk, t, :], None, S.ybuf[:, :],
                                             bass.IndirectOffsetOnAxis(ap=at[j][:, kk, t:t + 1], axis=0)).then_inc(got[j][kk], 16)

                list_rows(0, 0, 0)
                gather(0, 0, 2 * TPB)

                @rounds(e, 0, 1)
                def _(i, j, k):
                    if inside(i + 1):
                        list_rows(i + 1, 1 - j, k + j)
                    nb1.power(e, i, 0)
                    if inside(i + 1):
                        gather(1 - j, 0, 5)
                    nb2.power(e, i, 0)
                    if inside(i + 1):
                        gather(1 - j, 5, 2 * TPB)

            @block.vector
            def _(e):
                @rounds(e, 2)
                def _(i, j, k):
                    b = i
                    if inside(b):
                        x = S.X[:, tiles(b), :]
                        need(e, centred, b * TPB)
                        for kk in range(2):
                            need(e, got[j][kk], 16 * TPB * (k + 1))
                            for t in range(TPB):
                                e.scalar_tensor_tensor(
                                    out=acc[:, kk, t, :], in0=yg[j][:, kk, t, :], scalar=S.gate[:, kk, ds(b * TPB + t, 1)],
                                    in1=acc[:, 0, t, :] if kk else S.BIG[:, ds(b * TPB + t, 1), :].rearrange("p o d -> p (o d)"),
                                    op0=ALU.mult, op1=ALU.add).then_inc(added, 1)
                            need(e, added, b * ADDS + (kk + 1) * TPB)
                        nb1.stats(e, b, 0, acc[:, 1, :, :])
                        need(e, nb1.agg, (b + 1) * TPB)
                        need(e, upd, b * TPB)
                        for t in range(TPB):
                            e.scalar_tensor_tensor(out=r[:, t, :], in0=acc[:, 1, t, :], scalar=nb1.mv[0][:, t, 0:1],
                                                   in1=S.w["gamma_b"][:, :], op0=ALU.subtract, op1=ALU.mult).then_inc(centred, 1)
                    if inside(i - 2):
                        need(e, cutq, (i - 2) * P2 + P1)
                        e.tensor_tensor(parts[:, 2, :, :], rest[:, :, :], parts[:, 1, :, :], ALU.subtract).then_inc(cutq, 1)
                    if inside(b):
                        need(e, centred, (b + 1) * TPB)
                        need(e, nb1.powed, b + 1)
                        for t in range(TPB):
                            e.scalar_tensor_tensor(out=x[:, t, :], in0=r[:, t, :], scalar=nb1.rstd[0][:, t:t + 1], in1=x[:, t, :],
                                                   op0=ALU.mult, op1=ALU.add).then_inc(upd, 1)
                        need(e, upd, (b + 1) * TPB)
                        nb2.stats(e, b, 0, x)
                    if inside(i - 1):
                        need(e, cutq, (i - 1) * P2 + P0)
                        e.tensor_tensor(rest[:, :, :], full[:, :, :], parts[:, 0, :, :], ALU.subtract).then_inc(cutq, 1)
                    if inside(b):
                        need(e, trh, b)
                        nb2.apply(e, b, 0, x, hn)

            @block.tensor
            def _(e):
                @loop(e, B)
                def _(b):
                    nb2.wait(e, b)
                    need(e, hte, b)
                    turn(e, S, pH, hn).then_inc(trh, 1)
                    need(e, hte, b + 1)
                    need(e, cutq, (b - 1) * P2 + FULL)
                    for t in range(KD):
                        for k in range(KD):
                            last = e.matmul(pQ[:, t, :], S.w["wq1"][:, k, t * P:(t + 1) * P], hT[:, k, :],
                                            start=(k == 0), stop=(k == KD - 1))
                    last.then_inc(qd, 1)

            @block.scalar
            def _(e):
                @loop(e, B)
                def _(b):
                    need(e, trh, b + 1)
                    need(e, qd, b)
                    e.activation(hT[:, :, :], pH[:, :, :], ACT.Copy).then_inc(hte, 1)
                    need(e, qd, b + 1)
                    need(e, cutq, b * P2)
                    e.activation(full[:, :, :], pQ[:, :, :], ACT.Copy, scale=0.25).then_inc(cutq, 1)
                    need(e, cutq, b * P2 + FULL)
                    need(e, qst, 48 * b)
                    e.activation(parts[:, 0, :, :], full[:, :, :], ACT.Copy).then_inc(cutq, 1)
                    need(e, cutq, b * P2 + REST)
                    e.activation(parts[:, 1, :, :], rest[:, :, :], ACT.Copy).then_inc(cutq, 1)

            @block.sync
            def _(e):
                @loop(e, B)
                def _(b):
                    need(e, cutq, (b + 1) * P2)
                    for s in range(3):
                        e.dma_start(S.qs[1][s, :, ds(b * SEQ, SEQ)].rearrange("(t p) c -> p t c", p=P),
                                    parts[:, s, :, :]).then_inc(qst, 16)
                need(e, qst, 48 * B)


def merge(S):
    nc = S.nc
    ctx, sb, ps, sem = scope(S, "m")
    with ctx:
        att = sb("att", [P, TPB, D])
        attT = sb("attT", [P, KD, SEQ])
        nb = Norm(S, sb, sem)
        pA = ps("pA", [P, KD, SEQ])
        pY = ps("pY", [P, TPB, D])
        staged, tra, ate, yd, upd, maxed = (sem(x) for x in ("staged", "tra", "ate", "yd", "upd", "maxed"))

        with nc.Block() as block:
            @block.tensor
            def _(e):
                def turn_attention(b):
                    need(e, staged, b + 1)
                    need(e, ate, b)
                    turn(e, S, pA, att).then_inc(tra, 1)

                turn_attention(0)

                @rounds(e, 0, 1)
                def _(b, j, k):
                    if inside(b + 1):
                        turn_attention(b + 1)
                    need(e, ate, b + 1)
                    need(e, upd, b)
                    apply_weight(e, pY, attT, S.w["wo1"]).then_inc(yd, 1)

            @block.scalar
            def _(e):
                def stage(b):
                    need(e, tra, b)
                    gate(S, e)
                    e.activation(att[:, :, :], S.BIG[:, tiles(b), :], ACT.Copy).then_inc(staged, 1)

                stage(0)

                @rounds(e, 0, 1)
                def _(b, j, k):
                    need(e, tra, b + 1)
                    need(e, yd, b)
                    e.activation(attT[:, :, :], pA[:, :, :], ACT.Copy).then_inc(ate, 1)
                    if inside(b + 1):
                        stage(b + 1)

            @block.gpsimd
            def _(e):
                @rounds(e, 0)
                def _(b, j, k):
                    nb.power(e, b, j)

            @block.vector
            def _(e):
                @rounds(e, 1)
                def _(i, j, k):
                    if inside(i):
                        x = S.X[:, tiles(i), :]
                        need(e, yd, i + 1)
                        e.scalar_tensor_tensor(out=x, in0=pY[:, :, :], scalar=S.tg[:, 1:2], in1=x, op0=ALU.mult,
                                               op1=ALU.add).then_inc(upd, 1)
                        need(e, upd, i + 1)
                        nb.stats(e, i, j, x)
                    if inside(i - 1):
                        b = i - 1
                        need(e, staged, b + 1)
                        nb.apply(e, b, 1 - j, S.X[:, tiles(b), :], S.BIG[:, tiles(b), :])
                        nb.wait(e, b)
                        e.tensor_reduce(S.amax[:, ds(b, 1)], S.BIG[:, tiles(b), :], AX.XY, ALU.max,
                                        apply_absolute_value=True).then_inc(maxed, 1)


def quantise(S):
    nc, a = S.nc, S.a
    ctx, sb, ps, sem = scope(S, "q")
    EXP_BITS = 0x7F800000
    with ctx:
        w = sb("w", [P, KD, D])
        am, amg, amc, rec, scale, rscale = (sb(x, [P, 2]) for x in ("am", "amg", "amc", "rec", "scale", "rscale"))
        inv = sb("inv", [P, 1])
        v = [sb(f"v{j}", [P, TPB, D]) for j in range(2)]
        m = [sb(f"m{j}", [P, TPB, D]) for j in range(2)]
        big = [sb(f"big{j}", [P, TPB, D]) for j in range(2)]
        vq = [sb(f"vq{j}", [P, TPB, D], BF16) for j in range(2)]
        wq = sb("wq", [P, KD, D], BF16)
        wqT = sb("wqT", [P, KD, D], BF16)
        vqT = sb("vqT", [P, KD, SEQ], BF16)
        t1 = sb("t1", [P, TPB, D])
        o = [sb(f"o{j}", [P, TPB, D]) for j in range(2)]
        pW = ps("pW", [P, KD, D], BF16)
        pV = ps("pV", [P, KD, SEQ], BF16)
        pY = [ps(f"pY{j}", [P, TPB, D]) for j in range(2)]
        ldw, vc, red, wsc, wtr, wte = (sem(x) for x in ("ldw", "vc", "red", "wsc", "wtr", "wte"))
        sc = [sem(f"sc{j}") for j in range(2)]
        trv, vte, yd, fin = sem("trv"), sem("vte"), sem("yd"), sem("fin")
        st = [sem(f"st{j}") for j in range(2)]
        SCALED, MASKED, ADDED, MADE, ROUNDED = 1, 2, 3, 4, 5

        def mask_exponent(e, out, src):
            return e.tensor_scalar(out.bitcast(I32), src.bitcast(I32), EXP_BITS, None, ALU.bitwise_and)

        def make_m(e, out, src):
            return e.tensor_scalar(out, src, 2.0 ** -6, 1.5 * 2.0 ** 20, ALU.max, ALU.mult)

        with nc.Block() as block:
            @block.sync
            def _(e):
                e.dma_start(w[:, :, :], a["L1_ffn_weight"].rearrange("(t p) c -> p t c", p=P)).then_inc(ldw, 16)
                @loop(e, B // 2)
                def _(i):
                    for j in range(2):
                        need(e, fin, i * 4 + 2 * j + 2)
                        e.dma_start(S.out[ds(i * 2 + j, 1), :, :].rearrange("o (t p) d -> p (o t) d", p=P),
                                    o[j][:, :, :]).then_inc(st[j], 16)
                for j in range(2):
                    need(e, st[j], 16 * (B // 2))

            @block.gpsimd
            def _(e):
                need(e, vc, 2)
                e.partition_all_reduce(amg[:, :], am[:, :], P, bass.bass_isa.ReduceOp.max).then_inc(red, 1)
                @loop(e, B // 2)
                def _(i):
                    for j in range(2):
                        need(e, sc[j], i * ROUNDED + MASKED)
                        gate(S, e)
                        make_m(e, m[j][:, :, :], m[j][:, :, :]).then_inc(sc[j], 1)

            @block.scalar
            def _(e):
                need(e, vc, 6)
                e.activation(v[1][:, 0:KD, :], w[:, :, :], ACT.Copy, scale=scale[:, 1:2]).then_inc(wsc, 1)
                need(e, wtr, 1)
                e.activation(wqT[:, :, :], pW[:, :, :], ACT.Copy).then_inc(wte, 1)
                need(e, wsc, 5)

                def scaled(b, i, j):
                    need(e, sc[j], i * ROUNDED)
                    gate(S, e)
                    e.activation(v[j][:, :, :], S.BIG[:, tiles(b), :], ACT.Copy, scale=scale[:, 0:1]).then_inc(sc[j], 1)

                scaled(0, 0, 0)
                scaled(1, 0, 1)

                @rounds(e, 0, 2)
                def _(b, j, i):
                    if inside(b):
                        need(e, trv, b + 1)
                        need(e, yd, b)
                        e.activation(vqT[:, :, :], pV[:, :, :], ACT.Copy).then_inc(vte, 1)
                    if inside(b + 2):
                        scaled(b + 2, i + 1, j)

            @block.tensor
            def _(e):
                need(e, wsc, 5)
                for k in range(KD):
                    for t in range(KD):
                        last = e.transpose(pW[:, k, t * P:(t + 1) * P], wq[:, t, k * P:(k + 1) * P], S.identb[:, :])
                last.then_inc(wtr, 1)
                need(e, wte, 1)
                @loop(e, B // 2)
                def _(i):
                    for j in range(2):
                        b = i * 2 + j
                        need(e, sc[j], (i + 1) * ROUNDED)
                        need(e, vte, b)
                        for k in range(KD):
                            for t in range(TPB):
                                last = e.transpose(pV[:, k, t * P:(t + 1) * P], vq[j][:, t, k * P:(k + 1) * P], S.identb[:, :])
                        last.then_inc(trv, 1)
                        need(e, vte, b + 1)
                        need(e, fin, i * 4)
                        apply_weight(e, pY[j], vqT, wqT).then_inc(yd, 1)

            @block.vector
            def _(e):
                c = Chain(vc)
                c.begin(0)
                c.did(e.tensor_reduce(am[:, 0:1], S.amax[:, :], AX.X, ALU.max))
                need(e, ldw, 16)
                c.did(e.tensor_reduce(am[:, 1:2], w[:, :, :], AX.XY, ALU.max, apply_absolute_value=True))
                need(e, red, 1)
                c.did(e.tensor_scalar(amc[:, :], amg[:, :], 1e-12, None, ALU.max))
                c.wait(e)
                c.did(e.reciprocal(rec[:, :], amc[:, :]))
                c.wait(e)
                c.did(e.tensor_scalar(scale[:, :], rec[:, :], FP8_MAX, None, ALU.mult))
                c.wait(e)
                c.did(e.reciprocal(rscale[:, :], scale[:, :]))
                c.wait(e)
                c.did(e.tensor_tensor(inv[:, :], rscale[:, 0:1], rscale[:, 1:2], ALU.mult))
                need(e, wsc, 1)
                mask_exponent(e, big[1][:, 0:KD, :], v[1][:, 0:KD, :]).then_inc(wsc, 1)
                need(e, wsc, 2)
                make_m(e, m[1][:, 0:KD, :], big[1][:, 0:KD, :]).then_inc(wsc, 1)
                need(e, wsc, 3)
                e.tensor_tensor(t1[:, 0:KD, :], v[1][:, 0:KD, :], m[1][:, 0:KD, :], ALU.add).then_inc(wsc, 1)
                need(e, wsc, 4)
                e.tensor_tensor(wq[:, :, :], t1[:, 0:KD, :], m[1][:, 0:KD, :], ALU.subtract).then_inc(wsc, 1)
                c.wait(e)
                need(e, wsc, 5)

                def exponents(i, j):
                    need(e, sc[j], i * ROUNDED + SCALED)
                    mask_exponent(e, m[j][:, :, :], v[j][:, :, :]).then_inc(sc[j], 1)

                def output(b, i, j):
                    need(e, yd, b + 1)
                    need(e, st[j], 16 * i)
                    need(e, fin, b * 2)
                    for t in range(TPB):
                        ins = e.scalar_tensor_tensor(out=t1[:, t, :], in0=pY[j][:, t, :], scalar=inv[:, 0:1],
                                                     in1=S.w["fb_b"][:, :], op0=ALU.mult, op1=ALU.add)
                    ins.then_inc(fin, 1)
                    need(e, fin, b * 2 + 1)
                    e.scalar_tensor_tensor(out=o[j][:, :, :], in0=t1[:, :, :], scalar=S.tg[:, 3:4],
                                           in1=S.X[:, tiles(b), :], op0=ALU.mult, op1=ALU.add).then_inc(fin, 1)

                exponents(0, 0)

                @rounds(e, 1, 1)
                def _(b, j, i):
                    if inside(b + 1):
                        exponents(i + j, 1 - j)
                    if inside(b):
                        need(e, sc[j], i * ROUNDED + ADDED)
                        need(e, trv, b)
                        e.tensor_tensor(big[j][:, :, :], v[j][:, :, :], m[j][:, :, :], ALU.add).then_inc(sc[j], 1)
                        need(e, sc[j], i * ROUNDED + MADE)
                        e.tensor_tensor(vq[j][:, :, :], big[j][:, :, :], m[j][:, :, :], ALU.subtract).then_inc(sc[j], 1)
                    if inside(b - 1):
                        output(b - 1, i + j - 1, 1 - j)


_INS = ['x', 'ctx_1024', 'mask_Bx1xS2_if1', 'g_xattn', 'g_ffn', 'L0_xattn_wq', 'L0_xattn_bq', 'L0_xattn_wk',
        'L0_xattn_bk', 'L0_xattn_wv', 'L0_xattn_bv', 'L0_xattn_wo', 'L0_xattn_bo', 'L0_ffn_wg', 'L0_ffn_fc1_w',
        'L0_ffn_fc1_b', 'L0_ffn_fc2_w', 'L0_ffn_fc2_b', 'L0_ffn_ln_gamma', 'L0_ffn_ln_beta', 'L1_xattn_q_map',
        'L1_xattn_k_map', 'L1_xattn_v_map', 'L1_xattn_output_map', 'L1_ffn_weight', 'L1_ffn_bias']


def kernel(**inputs):
    import numpy as _np
    import concourse.bacc as _bacc
    from concourse import mybir as _mybir
    from concourse.bass_utils import run_bass_kernel_spmd as _run

    nc = _bacc.Bacc("TRN2", target_bir_lowering=False, num_devices=1)
    arrays, args = {}, {}
    for name in _INS:
        v = _np.ascontiguousarray(inputs[name])
        arrays[f"in_{name}"] = v
        args[name] = nc.dram_tensor(f"in_{name}", v.shape, _mybir.dt.from_np(v.dtype), kind="ExternalInput").ap()
    out = nc.dram_tensor("out_x", (B, SEQ, D), _mybir.dt.float32, kind="ExternalOutput").ap()
    build(nc, args, out)
    r = _run(nc, [arrays], core_ids=[0])
    return r.results[0]["out_x"]
```

```python
from contextlib import ExitStack

import concourse.bass as bass
from concourse import mybir

F32 = mybir.dt.float32
BF16 = mybir.dt.bfloat16
F32R = mybir.dt.float32r
I32 = mybir.dt.int32
ACT = mybir.ActivationFunctionType
ALU = mybir.AluOpType
AX = mybir.AxisListType
ds = bass.ds

P = 128
B, SEQ, D = 8, 512, 256
TPB = SEQ // P
NT = B * TPB
N = B * SEQ
KD = D // P
H, DH = 16, 16
G, HG = 4, 4
E, FF = 8, 1024
KF = FF // P
CAP = 2 * int(1.25 * ((N + E - 1) // E))
ZROWS = E * CAP // (P * B)
CHUNK = 256
NCH = CAP // CHUNK
VW = DH + 1
RUNS = ((0, 3, 0, 0),
        (3, 2, 0, 1),
        (5, 1, 0, 2))
Q_PLACE, K_PLACE = (0, 1, 2), (2, 1, 0)
PARTS_ROWS = 6 * DH
MAX_ROWS = PARTS_ROWS + 3
ALL_ROWS = MAX_ROWS + 3
FP8_MAX = 448.0
HI, LO = range(2)
PASSES = ((HI, HI), (HI, LO), (LO, HI))


class Shared:
    pass


def need(e, sem, value):
    if not isinstance(value, int) or value > 0:
        e.wait_ge(sem, value)


def rounds(e, lag, lead=0):
    def run(body):
        first, last = (lag + 3) // 2, (B - lead) // 2
        for i in range(2 * first):
            body(i, i % 2, i // 2)
        with e.Fori(first, last) as k:
            for j in range(2):
                body(k * 2 + j, j, k)
        for i in range(2 * last, B + lag):
            body(i, i % 2, i // 2)
    return run


def inside(b):
    return not isinstance(b, int) or 0 <= b < B


def loop3(e, n):
    def run(body):
        body(0, False)
        with e.Fori(1, n - 1) as i:
            body(i, False)
        body(n - 1, True)
    return run


def loop(e, n):
    def run(body):
        body(0)
        with e.Fori(1, n) as i:
            body(i)
    return run


class Chain:

    def __init__(self, sem):
        self.sem, self.k = sem, 0

    def did(self, ins):
        ins.then_inc(self.sem, 1)
        self.k += 1

    def wait(self, eng):
        need(eng, self.sem, self.k)


def build(nc, a, out, stop=99):
    ctx = ExitStack()
    with ctx:
        S = Shared()
        S.nc, S.a, S.out, S.w = nc, a, out, {}
        S.sem = lambda name: ctx.enter_context(nc.semaphore(name))
        S.stage_sems, S.sems_ctx = [], ExitStack()

        S.gates = S.sem("gates")

        def sb(name, shape, dt=F32):
            return ctx.enter_context(nc.sbuf_tensor(name, shape, dt))

        def dram(name, shape, dt=F32):
            return nc.dram_tensor(name, shape, dt).ap()

        ctx.enter_context(nc.allow_non_contiguous_dma(reason="small vectors, head-wise rows"))
        S.X = sb("X", [P, NT, D])
        S.BIG = sb("BIG", [P, NT, D])
        S.ident = sb("ident", [P, P])
        S.identb = sb("identb", [P, P], BF16)
        S.onesb = sb("onesb", [P, P], BF16)
        S.triu = sb("triu", [P, P], BF16)
        S.rank8 = sb("rank8", [P, E])
        S.half = sb("half", [P, TPB])
        S.tg = sb("tg", [P, 4])
        for w in ("wq0", "wk0", "wv0", "wo0", "wq1", "wk1", "wv1", "wo1"):
            S.w[w] = sb(w, [P, KD, D])
        S.w["wg"] = sb("wg", [P, KD, E])
        S.w["bq"] = sb("bq", [P, KD])
        S.w["bk"] = sb("bk", [P, KD])
        for w in ("bv_b", "bo_b", "gamma_b", "beta_b", "fb_b"):
            S.w[w] = sb(w, [P, D])
        S.b1T = sb("b1T", [P, E * KF])
        S.idx = sb("idx", [P, 2, NT])
        S.gate = sb("gate", [P, 2, NT])
        S.logit = sb("logit", [P, NT, E])
        S.onehot = sb("onehot", [P, 2 * E, NT], BF16)
        S.row_put = sb("row_put", [P, 2, NT], I32)
        S.row_get = sb("row_get", [P, 2, NT], I32)
        S.amax = sb("amax", [P, B])
        S.wrscale = sb("wrscale", [P, 1])
        S.qs = [dram(f"qs{l}", (H, 3, DH, N), BF16) for l in range(2)]
        S.ks = [dram(f"ks{l}", (H, 3, DH, N), BF16) for l in range(2)]
        S.vs = [dram(f"vs{l}", (N, H * VW)) for l in range(2)]
        S.extra = [dram(f"extra{l}", (6, N), BF16) for l in range(2)]
        S.disp = dram("disp", (E * CAP + 2 * N, D))
        S.ybuf = dram("ybuf", (E * CAP + P, D))

        stages = [setup, project, lambda S: attention(S, 0), route, place, experts, combine,
                  lambda S: attention(S, 1), merge, quantise]
        for n, stage in enumerate(stages):
            if n < stop:
                stage(S)
        S.sems_ctx.close()


def scope(S, n):
    ctx = ExitStack()
    nc = S.nc
    return (ctx, lambda name, shape, dt=F32: ctx.enter_context(nc.sbuf_tensor(f"{n}_{name}", shape, dt)),
            lambda name, shape, dt=F32: ctx.enter_context(nc.psum_tensor(f"{n}_{name}", shape, dt)),
            lambda name, keep=False: S.sem(f"{n}_{name}") if keep else stage_sem(S, f"{n}_{name}"))


def stage_sem(S, name):
    S.stage_sems.append(S.sems_ctx.enter_context(S.nc.semaphore(name)))
    return S.stage_sems[-1]


def recycle(S, e):
    for sem in S.stage_sems:
        e.sem_clear(sem)
    S.stage_sems = []


def setup(S):
    nc, a = S.nc, S.a
    ctx, sb, ps, sem = scope(S, "s")
    with ctx:
        raw = [sb(f"raw{j}", [P, KD, D]) for j in range(4)]
        b1raw = sb("b1raw", [E * KF, P])
        mi = sb("mi", [B, SEQ], I32)
        mf = sb("mf", [B, 3, SEQ])
        mparts = sb("mparts", [B, 3, SEQ], BF16)
        mzero = sb("mzero", [B, 3, SEQ], BF16)
        mone = sb("mone", [B, 3, SEQ], BF16)
        gl = sb("gl", [P, 4])
        pw = [ps(f"pw{j}", [P, KD, KD, P]) for j in range(4)]
        pb = ps("pb", [P, E * KF])
        S.ld_c, S.ld_x = sem("ld_c"), sem("ld_x")
        ld_raw, ld, ld_mask, ld_g = sem("ld_raw"), sem("ld"), sem("ld_mask"), sem("ld_g")
        id0, idd, tr, ev, vc, st = sem("id0"), sem("idd"), sem("tr"), sem("ev"), sem("vc"), sem("st")

        with nc.Block() as block:
            @block.sync
            def _(e):
                for j, w in enumerate(("L0_xattn_wq", "L0_xattn_wk", "L0_xattn_wv", "L0_xattn_wo")):
                    e.dma_start(raw[j][:, :, :], a[w].rearrange("(t p) c -> p t c", p=P)).then_inc(ld_raw, 16)
                e.dma_start(b1raw[:, :], a["L0_ffn_fc1_b"].rearrange("e (j p) -> (e j) p", p=P)).then_inc(ld_raw, 16)
                e.dma_start(mi[:, :], a["mask_Bx1xS2_if1"][:, 0, :]).then_inc(ld_mask, 16)
                e.dma_start(gl[:, 0:2], a["g_xattn"].rearrange("(o n) -> o n", o=1).broadcast_to([P, 2])).then_inc(ld_g, 16)
                e.dma_start(gl[:, 2:4], a["g_ffn"].rearrange("(o n) -> o n", o=1).broadcast_to([P, 2])).then_inc(ld_g, 16)
                load_context(S, e, 0)
                load_tokens(S, e, 0)
                n = 0
                for w, src in (("wq1", "L1_xattn_q_map"), ("wk1", "L1_xattn_k_map"),
                               ("wv1", "L1_xattn_v_map"), ("wo1", "L1_xattn_output_map"), ("wg", "L0_ffn_wg")):
                    e.dma_start(S.w[w][:, :, :], a[src].rearrange("(k p) o -> p k o", p=P)).then_inc(ld, 16)
                    n += 1
                for w, src in (("bq", "L0_xattn_bq"), ("bk", "L0_xattn_bk")):
                    e.dma_start(S.w[w][:, :], a[src].rearrange("(k p) -> p k", p=P)).then_inc(ld, 16)
                    n += 1
                for w, src in (("bv_b", "L0_xattn_bv"), ("bo_b", "L0_xattn_bo"), ("gamma_b", "L0_ffn_ln_gamma"),
                               ("beta_b", "L0_ffn_ln_beta"), ("fb_b", "L1_ffn_bias")):
                    e.dma_start(S.w[w][:, :],
                                a[src].rearrange("(o n) -> o n", o=1).broadcast_to([P, D])).then_inc(ld, 16)
                    n += 1
                need(e, vc, 9)
                for l, rows in ((0, mparts), (1, mzero)):
                    e.dma_start(S.extra[l][0:3, :].rearrange("s (b t) -> b s t", b=B), rows[:, :, :]).then_inc(st, 16)
                    e.dma_start(S.extra[l][3:6, :].rearrange("s (b t) -> b s t", b=B), mone[:, :, :]).then_inc(st, 16)
                need(e, ld, 16 * n)
                need(e, st, 64)

            @block.gpsimd
            def _(e):
                e.memset(S.ident[:, :], 0.0).then_inc(id0, 1)
                e.memset(S.onesb[:, :], 1.0).then_inc(id0, 1)
                e.memset(S.half[:, :], -0.5).then_inc(idd, 1)
                need(e, id0, 2)
                e.affine_select(out=S.ident[:, :], in_=S.ident[:, :], compare_op=ALU.not_equal, fill=1.0,
                                base=0, pattern=[[-1, P]], channel_multiplier=1).then_inc(idd, 1)
                e.affine_select(out=S.triu[:, :], in_=S.onesb[:, :], compare_op=ALU.is_ge, fill=0.0,
                                base=0, pattern=[[1, P]], channel_multiplier=-1).then_inc(idd, 1)
                e.iota(S.rank8[:, :], pattern=[[-1, E]], base=E, channel_multiplier=0,
                       allow_small_or_imprecise_dtypes=True).then_inc(idd, 1)

            @block.tensor
            def _(e):
                need(e, idd, 4)
                need(e, ld_raw, 80)
                for j in range(4):
                    for k in range(KD):
                        for t in range(KD):
                            e.transpose(pw[j][:, k, t, :], raw[j][:, t, k * P:(k + 1) * P], S.ident[:, :]).then_inc(tr, 1)
                e.transpose(pb[:, :], b1raw[:, :], S.ident[0:E * KF, 0:E * KF]).then_inc(tr, 1)

            @block.scalar
            def _(e):
                need(e, ld_g, 32)
                e.activation(S.tg[:, :], gl[:, :], ACT.Tanh).then_inc(ev, 1)
                for j, w in enumerate(("wq0", "wk0", "wv0", "wo0")):
                    need(e, tr, 4 * j + 4)
                    e.activation(S.w[w][:, :, :], pw[j][:, :, :, :], ACT.Copy).then_inc(ev, 1)
                need(e, tr, 17)
                e.activation(S.b1T[:, :], pb[:, :], ACT.Copy).then_inc(ev, 1)

            @block.vector
            def _(e):
                c = Chain(vc)
                c.did(e.memset(mzero[:, :, :], 0.0))
                c.did(e.memset(mone[:, :, :], 1.0))
                need(e, ld_mask, 16)
                c.did(e.tensor_scalar(mf[:, 0, :], mi[:, :], 0.0, -1.0, ALU.not_equal, ALU.add))
                c.wait(e)
                c.did(e.tensor_scalar(mf[:, 1, :], mf[:, 0, :], 1.0e9, None, ALU.mult))
                c.wait(e)
                split3(e, c, mf[:, 1, :], mf[:, 2, :], mparts[:, 0, :], mparts[:, 1, :], mparts[:, 2, :])
                need(e, idd, 4)
                c.did(e.tensor_copy(S.identb[:, :], S.ident[:, :]))


def context_buffer(S):
    return S.BIG[:, 0:TPB, :]


def load_context(S, e, b):
    e.dma_start(context_buffer(S), S.a["ctx_1024"][ds(b, 1), :, :].rearrange("o (t p) c -> p (o t) c", p=P)).then_inc(S.ld_c, 16)


def load_tokens(S, e, b):
    e.dma_start(S.X[:, ds(b * TPB, TPB), :], S.a["x"][ds(b, 1), :, :].rearrange("o (t p) c -> p (o t) c", p=P)).then_inc(S.ld_x, 16)


def split3(e, c, src, rest, p0, p1, p2):
    c.did(e.tensor_copy(p0, src))
    c.wait(e)
    c.did(e.tensor_tensor(rest, src, p0, ALU.subtract))
    c.wait(e)
    c.did(e.tensor_copy(p1, rest))
    c.wait(e)
    c.did(e.tensor_tensor(p2, rest, p1, ALU.subtract))


class Norm:

    def __init__(self, S, sb, sem, n="", sets=2):
        self.S, self.sets = S, sets
        self.stats6 = sb(f"stats{n}", [P, TPB, 6])
        self.mv = [sb(f"mv{n}{j}", [P, TPB, 2]) for j in range(sets)]
        self.var = [sb(f"var{n}{j}", [P, TPB]) for j in range(sets)]
        self.rstd = [sb(f"rstd{n}{j}", [P, TPB]) for j in range(sets)]
        self.stated, self.agg, self.vard, self.powed, self.normed = (
            sem(f"{x}{n}") for x in ("stated", "agg", "vard", "powed", "normed"))

    def stats(self, e, b, j, src):
        need(e, self.agg, b * TPB)
        gate(self.S, e)
        for t in range(TPB):
            e.bn_stats(self.stats6[:, t, :], src[:, t, :]).then_inc(self.stated, 1)
        need(e, self.stated, (b + 1) * TPB)
        gate(self.S, e)
        for t in range(TPB):
            e.bn_aggr(self.mv[j][:, t, :], self.stats6[:, t, :]).then_inc(self.agg, 1)

    def power(self, e, b, j):
        need(e, self.agg, (b + 1) * TPB)
        gate(self.S, e)
        e.tensor_scalar(self.var[j][:, :], self.mv[j][:, :, 1], 1e-5, None, ALU.add).then_inc(self.vard, 1)
        need(e, self.vard, b + 1)
        e.tensor_tensor(self.rstd[j][:, :], self.var[j][:, :], self.S.half[:, :], ALU.pow).then_inc(self.powed, 1)

    def apply(self, e, b, j, src, dst):
        need(e, self.agg, (b + 1) * TPB)
        need(e, self.powed, b + 1)
        for t in range(TPB):
            e.tensor_scalar(dst[:, t, :], src[:, t, :], self.mv[j][:, t, 0:1], self.rstd[j][:, t:t + 1],
                            ALU.subtract, ALU.mult).then_inc(self.normed, 1)

    def wait(self, e, b):
        need(e, self.normed, (b + 1) * TPB)


def store_part(e, dst, place, b, part, count):
    for t in range(KD):
        hpt = P // DH
        e.dma_start(dst[t * hpt:(t + 1) * hpt, place, :, ds(b * SEQ, SEQ)],
                    part[:, t, :]).then_inc(count, 16)


def gate(S, e):
    e.sem_inc(S.gates, 1)


def project(S):
    nc, a = S.nc, S.a
    ctx, sb, ps, sem = scope(S, "p")
    with ctx:
        cin = context_buffer(S)
        cT = [sb(f"cT{p}", [P, KD, SEQ], F32R) for p in ("hi", "lo")]
        hn = sb("hn", [P, TPB, D])
        hT = [sb(f"hT{p}", [P, KD, SEQ], F32R) for p in ("hi", "lo")]
        mi = sb("mi", [P, SEQ], I32)
        mb = sb("mb", [P, SEQ])
        bq4 = sb("bq4", [P, KD])
        nb = Norm(S, sb, sem, sets=1)
        jobs = ("k0", "k1", "q0")
        full = {j: sb(f"full_{j}", [P, KD, SEQ]) for j in jobs}
        rest = {j: sb(f"rest_{j}", [P, KD, SEQ]) for j in jobs}
        va = [sb(f"va{l}", [P, TPB, H, VW]) for l in range(2)]
        pT = [ps(f"pT{j}", [P, KD, SEQ]) for j in range(2)]
        pJ = [ps(f"pJ{j}", [P, KD, SEQ]) for j in range(2)]
        pV = pJ[1][:, :, :].rearrange("p k (t o) -> p (k t) o", o=D)
        one, ld_x, ld_c, ld_m = sem("one"), S.ld_x, S.ld_c, sem("ld_m")
        trc, cth, ctl, trh, hth, htl, mke = (sem(x) for x in ("trc", "cth", "ctl", "trh", "hth", "htl", "mke"))
        vc = sem("vc")
        pj = {j: sem(f"pj_{j}") for j in ("k0", "k1", "q0", "v0", "v1")}
        stp = {j: sem(f"stp_{j}") for j in jobs}
        vev = [sem(f"vev{l}") for l in range(2)]
        kst = {j: sem(f"kst_{j}") for j in ("k0", "k1", "q0", "v0", "v1")}
        FULL, P0, REST, P1, P2 = KD, KD + 1, KD + 2, KD + 3, KD + 4
        dst = {"k0": S.ks[0], "k1": S.ks[1], "q0": S.qs[0]}
        raw = {"k0": S.w["wk0"], "v0": S.w["wv0"], "k1": S.w["wk1"], "v1": S.w["wv1"], "q0": S.w["wq0"]}
        w = {j: [sb(f"w_{j}_{p}", [P, KD, D], F32R)[:, :, :] for p in ("hi", "lo")] for j in raw}
        whi, wlo = sem("whi"), sem("wlo")
        parts = {j: sb(f"parts_{j}", [P, 3, KD, SEQ], BF16) for j in ("k0", "k1", "q0")}

        def load(e, b):
            first = isinstance(b, int) and b == 0
            if not first:
                need(e, trc, b)
                load_context(S, e, b)
            need(e, mke, b)
            e.dma_start(mi[:, :], a["mask_Bx1xS2_if1"][ds(b, 1), 0, :].broadcast_to([P, SEQ])).then_inc(ld_m, 16)
            if not first:
                need(e, ld_x, 16 * b)
                load_tokens(S, e, b)

        def store(e, j, b):
            if isinstance(b, int) and b < 0:
                return
            if j[0] == "v":
                l = int(j[1])
                need(e, vev[l], b + 1)
                e.dma_start(S.vs[l][ds(b * SEQ, SEQ), :].rearrange("(t p) c -> p t c", p=P),
                            va[l][:, :, :, :].rearrange("p t h c -> p t (h c)")).then_inc(kst[j], 16)
            else:
                need(e, stp[j], b * P2 + P2)
                for s in range(3):
                    store_part(e, dst[j], (Q_PLACE if j[0] == "q" else K_PLACE)[s], b, parts[j][:, s, :, :], kst[j])

        with nc.Block() as block:
            @block.sync
            def _(e):
                load(e, 0)
                @loop3(e, B)
                def _(b, last):
                    if not last:
                        load(e, b + 1)
                    for j, by in (("v0", 0), ("q0", 1), ("k0", 0), ("v1", 0), ("k1", 0)):
                        store(e, j, b - by)
                store(e, "q0", B - 1)
                need(e, kst["k0"], 96 * B)
                for j in ("v0", "v1"):
                    need(e, kst[j], 16 * B)
                S.stored = [(kst["q0"], 96), (kst["k1"], 96)]

            @block.tensor
            def _(e):
                def product(j, b, src, out):
                    for t in range(KD):
                        for k in range(KD):
                            for pw, px in PASSES:
                                last = e.matmul(out[:, t, :], w[j][pw][:, k, t * P:(t + 1) * P], src[px][:, k, :],
                                                start=(k == 0 and (pw, px) == PASSES[0]),
                                                stop=(k == KD - 1 and (pw, px) == PASSES[-1]))
                    last.then_inc(pj[j], 1)

                def values(j, b, src):
                    for t in range(TPB):
                        for k in range(KD):
                            for px, pw in PASSES:
                                last = e.matmul(pV[:, t, :], src[px][:, k, t * P:(t + 1) * P], w[j][pw][:, k, :],
                                                start=(k == 0 and (px, pw) == PASSES[0]),
                                                stop=(k == KD - 1 and (px, pw) == PASSES[-1]))
                    last.then_inc(pj[j], 1)

                def turn_context(b):
                    need(e, ld_c, 16 * b + 16)
                    need(e, ctl, b)
                    turn(e, S, pT[0], cin).then_inc(trc, 1)

                turn_context(0)
                need(e, wlo, 5)

                @loop3(e, B)
                def _(b, last):
                    need(e, ctl, b + 1)
                    need(e, stp["q0"], (b - 1) * P2 + FULL)
                    product("k0", b, cT, pJ[0])
                    need(e, vev[1], b)
                    values("v0", b, cT)
                    nb.wait(e, b)
                    need(e, htl, b)
                    turn(e, S, pT[1], hn).then_inc(trh, 1)
                    need(e, stp["k0"], b * P2 + FULL)
                    product("k1", b, cT, pJ[0])
                    need(e, vev[0], b + 1)
                    values("v1", b, cT)
                    if not last:
                        turn_context(b + 1)
                    need(e, htl, b + 1)
                    need(e, stp["k1"], b * P2 + FULL)
                    product("q0", b, hT, pJ[0])

            @block.gpsimd
            def _(e):
                @loop(e, B)
                def _(b):
                    nb.power(e, b, 0)

            @block.scalar
            def _(e):
                e.activation(bq4[:, :], S.w["bq"][:, :], ACT.Copy, scale=0.25).then_inc(one, 1)
                need(e, one, 2)
                for n, j in enumerate(raw):
                    e.activation(w[j][HI], raw[j][:, :, :], ACT.Copy).then_inc(whi, 1)

                def take_context(b):
                    need(e, trc, b + 1)
                    need(e, pj["v1"], b)
                    e.activation(cT[HI][:, :, :], pT[0][:, :, :], ACT.Copy).then_inc(cth, 1)

                def take_tokens(b):
                    need(e, trh, b + 1)
                    need(e, pj["q0"], b)
                    e.activation(hT[HI][:, :, :], pT[1][:, :, :], ACT.Copy).then_inc(hth, 1)

                take_context(0)

                def cast(j, b, first):
                    if first:
                        need(e, stp[j], b * P2 + FULL)
                        need(e, kst[j], 96 * b)
                        e.activation(parts[j][:, 0, :, :], full[j][:, :, :], ACT.Copy).then_inc(stp[j], 1)
                    else:
                        need(e, stp[j], b * P2 + REST)
                        e.activation(parts[j][:, 1, :, :], rest[j][:, :, :], ACT.Copy).then_inc(stp[j], 1)

                @loop3(e, B)
                def _(b, last):
                    cast("k0", b, True)
                    if not (isinstance(b, int) and b == 0):
                        cast("q0", b - 1, False)
                    take_tokens(b)
                    cast("k0", b, False)
                    need(e, pj["k1"], b + 1)
                    need(e, stp["k1"], b * P2)
                    for t in range(KD):
                        e.activation(full["k1"][:, t, :], pJ[0][:, t, :], ACT.Copy).then_inc(stp["k1"], 1)
                    cast("k1", b, True)
                    need(e, pj["v1"], b + 1)
                    need(e, kst["v1"], 16 * b)
                    e.activation(va[1][:, :, :, 0:DH], pV.rearrange("p t (h c) -> p t h c", h=H), ACT.Copy).then_inc(vev[1], 1)
                    if not last:
                        take_context(b + 1)
                    need(e, pj["q0"], b + 1)
                    need(e, stp["q0"], b * P2)
                    for t in range(KD):
                        e.activation(full["q0"][:, t, :], pJ[0][:, t, :], ACT.Identity, bias=bq4[:, t:t + 1],
                                     scale=0.25).then_inc(stp["q0"], 1)
                    cast("k1", b, False)
                    cast("q0", b, True)
                cast("q0", B - 1, False)

            @block.vector
            def _(e):
                e.memset(va[0][:, :, :, DH:VW], 1.0).then_inc(vc, 1)
                e.memset(va[1][:, :, :, DH:VW], 1.0).then_inc(vc, 1)
                need(e, vc, 2)
                e.memset(mb[:, :], 0.0).then_inc(one, 1)
                need(e, one, 2)
                def prepare(b):
                    need(e, ld_m, 16 * b + 16)
                    need(e, stp["k0"], (b - 1) * P2 + FULL)
                    e.tensor_scalar(mb[:, :], mi[:, :], 0.0, None, ALU.not_equal).then_inc(mke, 1)
                    need(e, ld_x, 16 * b + 16)
                    nb.stats(e, b, 0, S.X[:, ds(b * TPB, TPB), :])

                def apply(b):
                    need(e, trh, b)
                    nb.apply(e, b, 0, S.X[:, ds(b * TPB, TPB), :], hn)

                def rest_of_context(b):
                    need(e, cth, b + 1)
                    e.tensor_tensor(cT[LO][:, :, :], pT[0][:, :, :], cT[HI][:, :, :], ALU.subtract).then_inc(ctl, 1)

                prepare(0)
                apply(0)
                for n, j in enumerate(raw):
                    need(e, whi, n + 1)
                    e.tensor_tensor(w[j][LO], raw[j][:, :, :], w[j][HI], ALU.subtract).then_inc(wlo, 1)
                rest_of_context(0)

                def remainder(j, b, first):
                    if first:
                        need(e, stp[j], b * P2 + P0)
                        e.tensor_tensor(rest[j][:, :, :], full[j][:, :, :], parts[j][:, 0, :, :], ALU.subtract).then_inc(stp[j], 1)
                    else:
                        need(e, stp[j], b * P2 + P1)
                        e.tensor_tensor(parts[j][:, 2, :, :], rest[j][:, :, :], parts[j][:, 1, :, :], ALU.subtract).then_inc(stp[j], 1)

                @loop3(e, B)
                def _(b, last):
                    before = not (isinstance(b, int) and b == 0)
                    need(e, mke, b + 1)
                    need(e, pj["k0"], b + 1)
                    need(e, stp["k0"], b * P2)
                    for t in range(KD):
                        e.scalar_tensor_tensor(out=full["k0"][:, t, :], in0=pJ[0][:, t, :], scalar=S.w["bk"][:, t:t + 1],
                                               in1=mb[:, :], op0=ALU.add, op1=ALU.mult).then_inc(stp["k0"], 1)
                    if before:
                        remainder("q0", b - 1, True)
                    need(e, pj["v0"], b + 1)
                    need(e, kst["v0"], 16 * b)
                    e.tensor_tensor(va[0][:, :, :, 0:DH], pV.rearrange("p t (h c) -> p t h c", h=H),
                                    S.w["bv_b"][:, :].rearrange("p (o h c) -> p o h c", o=1, h=H).broadcast_to([P, TPB, H, DH]),
                                    ALU.add).then_inc(vev[0], 1)
                    remainder("k0", b, True)
                    if before:
                        remainder("q0", b - 1, False)
                    need(e, hth, b + 1)
                    e.tensor_tensor(hT[LO][:, :, :], pT[1][:, :, :], hT[HI][:, :, :], ALU.subtract).then_inc(htl, 1)
                    remainder("k0", b, False)
                    if not last:
                        prepare(b + 1)
                        rest_of_context(b + 1)
                    remainder("k1", b, True)
                    if not last:
                        apply(b + 1)
                    remainder("k1", b, False)
                for first in (True, False):
                    remainder("q0", B - 1, first)


def attention(S, l):
    nc = S.nc
    ctx, sb, ps, sem = scope(S, f"a{l}")
    SLOTS = 2 * TPB
    NMAX = HG * TPB
    LOADS = 16 * 7
    with ctx:
        q = [sb(f"q{g}", [P, HG, SEQ], BF16) for g in range(G)]
        k = [sb(f"k{g}", [P, HG, SEQ], BF16) for g in range(G)]
        v = [sb(f"v{g}", [P, TPB, HG, VW]) for g in range(G)]
        pexp = [sb(f"pexp{t}", [P, HG, SEQ]) for t in range(TPB)]
        nmax = [sb(f"nmax{g}", [P, NMAX]) for g in range(G)]
        nrest = sb("nrest", [P, NMAX])
        nparts = sb("nparts", [P, P], BF16)
        nT = sb("nT", [3 * NMAX, P], BF16)
        osb = sb("osb", [P, SEQ])
        rden = sb("rden", [P, TPB, HG])
        pring = [ps(f"pring{j}", [P, SEQ]) for j in range(3)]
        USES = [("scores", j) for j in range(6)] + ["maxima"] + [("scores", j) for j in range(6, 15)] + [
            "outputs", ("scores", 15)]
        assert len(USES) == NMAX + 2 and len(USES) % 3 == 0
        bank = lambda use: pring[USES.index(use) % 3]
        EARLY = [(0, j) for j in range(NMAX)] + [(1, j) for j in range(6)] + ["maxima"] + [
            (1, j) for j in range(6, NMAX)]
        pturn = bank("outputs")[:, :].rearrange("p (t c) -> p t c", c=P)
        pturn_n = {early: ring[:, 0:P // 2].bitcast(BF16)[0:P, :]
                   for early, ring in ((False, bank("maxima")), (True, pring[EARLY.index("maxima") % 3]))}
        pscore = [ps(f"pscore{j}", [P, 2, SEQ]) for j in range(2)]
        pout = ps("pout", [P, SEQ])
        ld_ones = [sem(f"ld_ones{g}") for g in range(G)]
        if l == 0:
            zeros, zeroed, cleared = sb("zeros", [P, ZROWS, D]), sem("zeroed"), sem("cleared", keep=True)
        clear, ld_v = sem("clear"), [sem(f"ld_v{g}", keep=True) for g in range(G)]
        ld = [sem(f"ld{g}") for g in range(G)]
        mrow = [sem(f"mrow{g}") for g in range(G)]
        maxed, reduced, cut, nturned, nout = (sem(x) for x in ("maxed", "reduced", "cut", "nturned", "nout"))
        scored, exped, summed, oout, turned, rec, normed = (
            sem(x) for x in ("scored", "exped", "summed", "oout", "turned", "rec", "normed"))

        def groups(body):
            def run(e):
                for g in range(G):
                    body(e, 0, g, g == 0, False)
                with e.Fori(1, B - 1) as b:
                    for g in range(G):
                        body(e, b, g, False, False)
                for g in range(G):
                    body(e, B - 1, g, False, True)
            return run

        def ahead(b, g, by):
            return (b, g + by) if g + by < G else (b + 1, g + by - G)

        with nc.Block() as block:
            @block.sync
            def _(e):
                def load(b, g):
                    at = ds(b * SEQ, SEQ)
                    for block, n, q_at, k_at in RUNS:
                        for buf, src, place in ((q, S.qs[l], q_at), (k, S.ks[l], k_at)):
                            e.dma_start(buf[g][block * DH:(block + n) * DH, :, :],
                                        src[g * HG:(g + 1) * HG, place:place + n, :, at].rearrange("h s d t -> (s d) h t")
                                        ).then_inc(ld[g], 16)
                    e.dma_start(k[g][PARTS_ROWS:ALL_ROWS, :, :],
                                S.extra[l][:, at].rearrange("s (o t) -> s o t", o=1).broadcast_to([6, HG, SEQ])
                                ).then_inc(ld[g], 16)

                def maxima(b, g):
                    need(e, nout, b * G + g + 1)
                    for s in range(3):
                        e.dma_start(q[g][MAX_ROWS + s:MAX_ROWS + s + 1, :, :].rearrange("o h (t c) -> o (h t) c", c=P),
                                    nT[s * NMAX:(s + 1) * NMAX, :]).then_inc(mrow[g], 16)

                def body(e, b, g, first, last):
                    if not (last and g == G - 1):
                        maxima(*ahead(b, g, 1))
                    if first:
                        for stored, each in S.stored:
                            need(e, stored, each * B)
                    if not last:
                        need(e, scored, (b * G + g + 1) * SLOTS)
                        load(b + 1, g)

                for stored, each in S.stored:
                    need(e, stored, each * (B - 1))
                for g in range(G):
                    load(0, g)
                    e.dma_start(q[g][PARTS_ROWS:MAX_ROWS, :, :],
                                S.extra[l][3:6, 0:SEQ].rearrange("s (o t) -> s o t", o=1).broadcast_to([3, HG, SEQ])
                                ).then_inc(ld_ones[g], 16)
                maxima(0, 0)
                groups(body)(e)

            @block.gpsimd
            def _(e):
                e.memset(nparts[:, :], 0.0).then_inc(cut, 1)

                def load_v(b, g):
                    e.dma_start(v[g][:, :, :, :].rearrange("p t h c -> p t (h c)"),
                                S.vs[l][ds(b * SEQ, SEQ), g * HG * VW:(g + 1) * HG * VW].rearrange("(t p) c -> p t c", p=P)
                                ).then_inc(ld_v[g], 16)

                def parts(b, g):
                    n = b * G + g
                    need(e, reduced, (n + 1) * NMAX)
                    need(e, nturned, n)
                    need(e, cut, 4 * n + 1)
                    gate(S, e)
                    e.tensor_copy(nparts[:, 0:NMAX], nmax[g][:, :]).then_inc(cut, 1)
                    need(e, cut, 4 * n + 2)
                    e.tensor_tensor(nrest[:, :], nmax[g][:, :], nparts[:, 0:NMAX], ALU.subtract).then_inc(cut, 1)
                    need(e, cut, 4 * n + 3)
                    gate(S, e)
                    e.tensor_copy(nparts[:, NMAX:2 * NMAX], nrest[:, :]).then_inc(cut, 1)
                    need(e, cut, 4 * n + 4)
                    e.tensor_tensor(nparts[:, 2 * NMAX:3 * NMAX], nrest[:, :], nparts[:, NMAX:2 * NMAX],
                                    ALU.subtract).then_inc(cut, 1)

                def body(e, b, g, first, last):
                    n = b * G + g
                    if l == 0 and g == 0:
                        e.dma_start(S.disp[ds(b * ZROWS * P, ZROWS * P), :].rearrange("(p r) d -> p r d", p=P),
                                    zeros[:, :, :]).then_inc(cleared, 16)
                    if not first and not (last and g > 0):
                        need(e, summed, n * TPB)
                        load_v(*((b, G - 1) if g == 0 else (b + 1, g - 1)))
                    if not (last and g >= G - 2):
                        parts(*ahead(b, g, 2))

                for g in range(G):
                    load_v(0, g)
                parts(0, 0)
                parts(0, 1)
                if l == 0:
                    e.memset(zeros[:, :, :], 0.0).then_inc(zeroed, 1)
                    need(e, zeroed, 1)
                    e.dma_start(S.ybuf[E * CAP:E * CAP + P, :], zeros[:, 0, :]).then_inc(cleared, 16)
                groups(body)(e)
                if l == 0:
                    need(e, cleared, 16 * (B + 1))

            @block.tensor
            def _(e):
                def bank_free(b, g, first, last, use):
                    u = USES.index(use) - 3
                    while True:
                        if u < 0:
                            if first:
                                need(e, reduced, 2 * NMAX)
                                return
                            u, last = u + len(USES), last and g > 0
                            b, g = (b, g - 1) if g else (b - 1, G - 1)
                            first = isinstance(b, int) and b == 0 and g == 0
                        n, held = b * G + g, USES[u]
                        if held == "maxima":
                            if not (last and g == G - 1):
                                need(e, nout, n + 2)
                                return
                        elif held == "outputs":
                            if not first:
                                need(e, normed, n)
                                return
                        elif not (last and g >= G - 2):
                            need(e, reduced, (n + 2) * NMAX + held[1] + 1)
                            return
                        u -= 3

                def max_product(b, g, j, out):
                    h, t = j // TPB, j % TPB
                    e.matmul(out[:, :], q[g][0:MAX_ROWS, h, t * P:(t + 1) * P], k[g][0:MAX_ROWS, h, :],
                             start=True, stop=True).then_inc(maxed, 1)

                def turn_maxima(b, g, early=False):
                    need(e, cut, 4 * (b * G + g) + 5)
                    e.transpose(pturn_n[early], nparts[:, :], S.identb[:, :]).then_inc(nturned, 1)

                def values(b, g, t):
                    n = b * G + g
                    if t == 0:
                        need(e, ld_v[g], 16 * b + 16)
                        need(e, oout, n)
                    need(e, exped, n * SLOTS + 2 * t + 2)
                    for h in range(HG):
                        last = e.matmul(pout[32 * h:32 * h + VW, :], v[g][:, t, h, :], pexp[t][:, h, :],
                                        start=(t == 0), stop=(t == TPB - 1))
                    last.then_inc(summed, 1)

                def turn_outputs(n):
                    need(e, oout, n + 1)
                    for t in range(TPB):
                        last = e.transpose(pturn[:, t, :], osb[:, t * P:(t + 1) * P], S.ident[:, :])
                    last.then_inc(turned, 1)

                def scores(b, g, first, s):
                    n, t, pair = b * G + g, s // 2, s % 2
                    if not (first and s < 2):
                        need(e, exped, n * SLOTS + s - 1)
                    if s == 0:
                        need(e, mrow[g], 48 * b + 48)
                    for h in (2 * pair, 2 * pair + 1):
                        mm = e.matmul(pscore[s % 2][:, h % 2, :], k[g][0:ALL_ROWS, h, t * P:(t + 1) * P],
                                      q[g][0:ALL_ROWS, h, :], start=True, stop=True)
                    mm.then_inc(scored, 1)

                def body(e, b, g, first, last):
                    n = b * G + g
                    before = (b, g - 1) if g else (b - 1, G - 1)
                    more = not (last and g >= G - 2)
                    b2, g2 = ahead(b, g, 2)
                    if more:
                        need(e, ld[g2], LOADS * b2 + LOADS)

                    def max_ahead(j):
                        if more:
                            bank_free(b, g, first, last, ("scores", j))
                            max_product(b2, g2, j, bank(("scores", j)))

                    for p in range(SLOTS // 2):
                        max_ahead(4 * p)
                        max_ahead(4 * p + 1)
                        if p >= 2:
                            values(b, g, p - 2)
                        elif not first:
                            values(*before, p + 2)
                        if p == 1 and not (last and g == G - 1):
                            bank_free(b, g, first, last, "maxima")
                            turn_maxima(*ahead(b, g, 1))
                        max_ahead(4 * p + 2)
                        if p == 3 and not first:
                            bank_free(b, g, first, last, "outputs")
                            turn_outputs(n - 1)
                        scores(b, g, first, 2 * p)
                        max_ahead(4 * p + 3)
                        scores(b, g, first, 2 * p + 1)

                need(e, clear, 1)
                for u, use in enumerate(EARLY):
                    if u >= 3:
                        held = EARLY[u - 3]
                        need(e, *((nout, 1) if held == "maxima" else (reduced, held[0] * NMAX + held[1] + 1)))
                    if use == "maxima":
                        turn_maxima(0, 0, early=True)
                        continue
                    g, j = use
                    if j == 0:
                        need(e, ld[g], LOADS)
                        need(e, ld_ones[g], 16)
                    max_product(0, g, j, pring[u % 3])
                for g in (2, 3):
                    need(e, ld_ones[g], 16)
                groups(body)(e)
                for t in (TPB - 2, TPB - 1):
                    values(B - 1, G - 1, t)
                need(e, normed, B * G - 1)
                turn_outputs(B * G - 1)

            @block.scalar
            def _(e):
                def take_outputs(n):
                    need(e, summed, (n + 1) * TPB)
                    need(e, turned, n)
                    e.activation(osb[:, :], pout[:, :], ACT.Copy).then_inc(oout, 1)

                def body(e, b, g, first, last):
                    n = b * G + g
                    for s in range(SLOTS):
                        t, pair = s // 2, s % 2
                        need(e, scored, n * SLOTS + s + 1)
                        if pair == 0 and not first:
                            need(e, summed, n * TPB + t - (TPB - 1))
                        e.activation(pexp[t][:, 2 * pair:2 * pair + 2, :], pscore[s % 2][:, :, :], ACT.Exp).then_inc(exped, 1)
                        if s == 1 and not first:
                            take_outputs(n - 1)

                groups(body)(e)
                take_outputs(B * G - 1)

            @block.vector
            def _(e):
                e.memset(pout[:, :], 0.0).then_inc(clear, 1)

                def reduce(b, g, js, early=False):
                    n = b * G + g
                    for j in js:
                        if j == 0:
                            need(e, cut, 4 * n - 11)
                        need(e, maxed, n * NMAX + j + 1)
                        e.tensor_reduce(nmax[g][:, j:j + 1], (pring[EARLY.index((g, j)) % 3] if early else bank(("scores", j)))[:, :], AX.X, ALU.max,
                                        negate=True).then_inc(reduced, 1)

                def take_maxima(b, g, early=False):
                    n = b * G + g
                    need(e, nturned, n + 1)
                    pb, pg = (b, g - 1) if g else (b - 1, G - 1)
                    need(e, mrow[pg], 48 * pb + 48)
                    e.tensor_copy(nT[:, :], pturn_n[early][0:3 * NMAX, :]).then_inc(nout, 1)

                def normalise(b, g):
                    n = b * G + g
                    turn = pturn[:, :, :].rearrange("p t (h c) -> p t h c", c=32)
                    need(e, turned, n + 1)
                    e.reciprocal(rden[:, :, :], turn[:, :, :, DH]).then_inc(rec, 1)
                    need(e, rec, n + 1)
                    e.tensor_tensor(S.BIG[:, ds(b * TPB, TPB), g * HG * DH:(g + 1) * HG * DH].rearrange("p t (h c) -> p t h c", c=DH),
                                    turn[:, :, :, 0:DH],
                                    rden[:, :, :].rearrange("p t (h o) -> p t h o", o=1).broadcast_to([P, TPB, HG, DH]),
                                    ALU.mult).then_inc(normed, 1)

                def body(e, b, g, first, last):
                    ahead2 = None if last and g >= G - 2 else ahead(b, g, 2)
                    if ahead2:
                        reduce(*ahead2, range(0, 6))
                    if not (last and g == G - 1):
                        take_maxima(*ahead(b, g, 1))
                    if ahead2:
                        reduce(*ahead2, range(6, 15))
                    if not first:
                        normalise(*((b, g - 1) if g else (b - 1, G - 1)))
                    if ahead2:
                        reduce(*ahead2, range(15, NMAX))

                reduce(0, 0, range(NMAX), early=True)
                reduce(0, 1, range(6), early=True)
                take_maxima(0, 0, early=True)
                reduce(0, 1, range(6, NMAX), early=True)
                groups(body)(e)
                normalise(B - 1, G - 1)


def tiles(b):
    return ds(b * TPB, TPB)


def turn(e, S, out, src):
    for k in range(KD):
        for t in range(TPB):
            last = e.transpose(out[:, k, t * P:(t + 1) * P], src[:, t, k * P:(k + 1) * P], S.ident[:, :])
    return last


def apply_weight(e, out, srcT, w):
    for t in range(TPB):
        for k in range(KD):
            last = e.matmul(out[:, t, :], srcT[:, k, t * P:(t + 1) * P], w[:, k, :], start=(k == 0), stop=(k == KD - 1))
    return last


def over_tiles(v, n=TPB):
    return v[:, :].rearrange("p (o d) -> p o d", o=1).broadcast_to([P, n, D])


def route(S):
    nc = S.nc
    ctx, sb, ps, sem = scope(S, "r")
    with ctx:
        att = sb("att", [P, TPB, D])
        attT = sb("attT", [P, KD, SEQ])
        yb = sb("yb", [P, TPB, D])
        hn = sb("hn", [P, TPB, D])
        hT = sb("hT", [P, KD, SEQ])
        nb = Norm(S, sb, sem)
        pA, pH, pY = (ps(x, [P, KD, SEQ]) for x in ("pA", "pH", "pY"))
        pYt = pY[:, :, :].rearrange("p k (t o) -> p (k t) o", o=D)
        pL = ps("pL", [P, TPB, E])
        staged, tra, ate, yd, ybd, upd, kept, trh, hte, ld, lkept = (
            sem(x) for x in ("staged", "tra", "ate", "yd", "ybd", "upd", "kept", "trh", "hte", "ld", "lkept"))

        with nc.Block() as block:
            @block.tensor
            def _(e):
                def turn_attention(b):
                    need(e, staged, b + 1)
                    need(e, ate, b)
                    turn(e, S, pA, att).then_inc(tra, 1)

                def output(b):
                    need(e, ate, b + 1)
                    need(e, ybd, b)
                    apply_weight(e, pYt, attT, S.w["wo0"]).then_inc(yd, 1)

                def turn_normed(b):
                    nb.wait(e, b)
                    need(e, hte, b)
                    turn(e, S, pH, hn).then_inc(trh, 1)

                def logits(b):
                    need(e, hte, b + 1)
                    need(e, lkept, b)
                    apply_weight(e, pL, hT, S.w["wg"]).then_inc(ld, 1)

                turn_attention(0)
                output(0)

                @rounds(e, 2, 1)
                def _(i, j, k):
                    if inside(i + 1):
                        turn_attention(i + 1)
                    if inside(i - 2):
                        logits(i - 2)
                    if inside(i + 1):
                        output(i + 1)
                    if inside(i - 1):
                        turn_normed(i - 1)

            @block.scalar
            def _(e):
                def stage(b):
                    need(e, tra, b)
                    gate(S, e)
                    e.activation(att[:, :, :], S.BIG[:, tiles(b), :], ACT.Copy).then_inc(staged, 1)

                def take_attention(b):
                    need(e, tra, b + 1)
                    need(e, yd, b)
                    e.activation(attT[:, :, :], pA[:, :, :], ACT.Copy).then_inc(ate, 1)

                def keep(b):
                    nb.wait(e, b)
                    need(e, staged, b + 1)
                    gate(S, e)
                    e.activation(S.BIG[:, tiles(b), :], hn[:, :, :], ACT.Copy).then_inc(kept, 1)

                def take_normed(b):
                    need(e, trh, b + 1)
                    need(e, ld, b)
                    e.activation(hT[:, :, :], pH[:, :, :], ACT.Copy).then_inc(hte, 1)

                stage(0)
                take_attention(0)
                stage(1)

                @rounds(e, 2, 2)
                def _(i, j, k):
                    if inside(i + 1):
                        take_attention(i + 1)
                    if inside(i + 2):
                        stage(i + 2)
                    if inside(i - 1):
                        keep(i - 1)
                        take_normed(i - 1)

            @block.gpsimd
            def _(e):
                @rounds(e, 0)
                def _(b, j, k):
                    nb.power(e, b, j)

            @block.vector
            def _(e):
                @rounds(e, 2)
                def _(i, j, k):
                    if inside(i):
                        x = S.X[:, tiles(i), :]
                        need(e, yd, i + 1)
                        need(e, upd, i)
                        e.tensor_tensor(yb[:, :, :], pYt, over_tiles(S.w["bo_b"]), ALU.add).then_inc(ybd, 1)
                        need(e, ybd, i + 1)
                        e.scalar_tensor_tensor(out=x, in0=yb[:, :, :], scalar=S.tg[:, 0:1], in1=x,
                                               op0=ALU.mult, op1=ALU.add).then_inc(upd, 1)
                        need(e, upd, i + 1)
                        nb.stats(e, i, j, x)
                    if inside(i - 2):
                        need(e, ld, i - 1)
                        e.tensor_copy(S.logit[:, tiles(i - 2), :], pL[:, :, :]).then_inc(lkept, 1)
                    if inside(i - 1):
                        need(e, kept, i - 1)
                        need(e, trh, i - 1)
                        nb.apply(e, i - 1, 1 - j, S.X[:, tiles(i - 1), :], hn)


def place(S):
    nc = S.nc
    ctx, sb, ps, sem = scope(S, "l")
    SET = 2
    sem = lambda name, keep=True: S.sem(f"l_{name}")
    S.fc = ExpertWeights(S)
    with ctx:
        tot = sb("tot", [P, 2 * E, NT])
        scan = [sb(f"scan{j}", [P, 2 * E, NT]) for j in range(2)]
        loc = sb("loc", [P, 2 * E, NT])
        mine = sb("mine", [P, 2 * E, NT])
        sel, pos, keep, off, spare, t1, t2, t3, t4 = (sb(x, [P, 2, NT]) for x in (
            "sel", "pos", "keep", "off", "spare", "t1", "t2", "t3", "t4"))
        rows = [sb(f"rows{j}", [P, TPB, D]) for j in range(SET)]
        at = [sb(f"at{j}", [P, 2, TPB], I32) for j in range(SET)]
        lmax, lsum, rsum, gs, gc, gr = (sb(x, [P, NT]) for x in ("lmax", "lsum", "rsum", "gs", "gc", "gr"))
        less, ex, score, is_top, rank = (sb(x, [P, NT, E]) for x in ("less", "ex", "score", "is_top", "rank"))
        top, topr = sb("top", [P, 2, NT]), sb("topr", [P, 2, NT])
        pC, pT = ps("pC", [P, 2 * E, NT]), ps("pT", [P, 2 * E, NT])
        mm, sp, vc, exd, chosen, scaled = (sem(x) for x in ("mm", "sp", "vc", "exd", "chosen", "scaled"))
        copied = [sem(f"copied{j}") for j in range(SET)]
        listed = [sem(f"listed{j}") for j in range(SET)]
        put = [sem(f"put{j}", keep=True) for j in range(SET)]
        with nc.Block() as block:
            @block.tensor
            def _(e):
                need(e, chosen, 1)
                flat = S.onehot[:, :, :].rearrange("p e t -> p (e t)")
                e.matmul(pC[:, :, :].rearrange("p e t -> p (e t)"), S.triu[:, :], flat, start=True, stop=True).then_inc(mm, 1)
                e.matmul(pT[:, :, :].rearrange("p e t -> p (e t)"), S.onesb[:, :], flat, start=True, stop=True).then_inc(mm, 1)
                for w in range(S.fc.GROUPS):
                    S.fc.turn_fc1(e, 0, 0, w)

            @block.sync
            def _(e):
                S.fc.load_fc1(e, 0)
                S.fc.load_fc2(e, 0)
                S.fc.load_fc1(e, 1)
                S.fc.load_fc2(e, 1)

            @block.scalar
            def _(e):
                need(e, vc, 2)
                e.activation(ex[:, :, :], less[:, :, :], ACT.Exp).then_inc(exd, 1)
                @loop(e, B // SET)
                def _(i):
                    for j in range(SET):
                        need(e, put[j], 16 * 2 * TPB * i)
                        gate(S, e)
                        e.activation(rows[j][:, :, :], S.BIG[:, ds((i * SET + j) * TPB, TPB), :], ACT.Copy).then_inc(copied[j], 1)

            @block.vector
            def _(e):
                c = Chain(vc)
                each_expert = lambda v: v.rearrange("p (t o) -> p t o", o=1).broadcast_to([P, NT, E])
                c.did(e.tensor_reduce(lmax[:, :], S.logit[:, :, :], AX.X, ALU.max))
                c.wait(e)
                c.did(e.tensor_tensor(less[:, :, :], S.logit[:, :, :], each_expert(lmax[:, :]), ALU.subtract))
                need(e, exd, 1)
                c.did(e.tensor_reduce(lsum[:, :], ex[:, :, :], AX.X, ALU.add))
                c.wait(e)
                c.did(e.reciprocal(rsum[:, :], lsum[:, :]))
                c.wait(e)
                c.did(e.tensor_tensor(score[:, :, :], ex[:, :, :], each_expert(rsum[:, :]), ALU.mult))
                c.wait(e)
                for kk in range(2):
                    c.did(e.tensor_reduce(top[:, kk, :], score[:, :, :], AX.X, ALU.max))
                    c.wait(e)
                    c.did(e.tensor_tensor(is_top[:, :, :], score[:, :, :], each_expert(top[:, kk, :]), ALU.is_equal))
                    c.wait(e)
                    ranks = S.rank8[:, :].rearrange("p (o x) -> p o x", o=1).broadcast_to([P, NT, E])
                    c.did(e.tensor_tensor(rank[:, :, :], is_top[:, :, :], ranks, ALU.mult))
                    c.wait(e)
                    c.did(e.tensor_reduce(topr[:, kk, :], rank[:, :, :], AX.X, ALU.max))
                    c.wait(e)
                    c.did(e.tensor_tensor(is_top[:, :, :], ranks, each_expert(topr[:, kk, :]), ALU.is_equal))
                    c.wait(e)
                    ins = e.tensor_copy(S.onehot[:, kk * E:(kk + 1) * E, :].rearrange("p x t -> p t x"), is_top[:, :, :])
                    if kk == 0:
                        c.did(ins)
                        c.did(e.scalar_tensor_tensor(out=score[:, :, :], in0=is_top[:, :, :], scalar=-2.0, in1=score[:, :, :],
                                                     op0=ALU.mult, op1=ALU.add))
                        c.wait(e)
                    else:
                        ins.then_inc(chosen, 1)
                c.did(e.tensor_scalar(S.idx[:, :, :], topr[:, :, :], -1.0, float(E), ALU.mult, ALU.add))
                c.did(e.tensor_tensor(gs[:, :], top[:, 0, :], top[:, 1, :], ALU.add))
                c.wait(e)
                c.did(e.tensor_scalar(gc[:, :], gs[:, :], 1.1920929e-07, None, ALU.max))
                c.wait(e)
                c.did(e.reciprocal(gr[:, :], gc[:, :]))
                c.wait(e)
                c.did(e.tensor_tensor(S.gate[:, :, :], top[:, :, :],
                                      gr[:, :].rearrange("p (o t) -> p o t", o=1).broadcast_to([P, 2, NT]), ALU.mult))
                need(e, chosen, 1)
                need(e, mm, 2)
                c.did(e.tensor_copy(tot[:, :, :], pT[:, :, :]))
                c.wait(e)
                src = tot
                for n, d in enumerate((1, 2, 4, 8, 16)):
                    dst = scan[n % 2]
                    c.did(e.tensor_tensor(dst[:, :, d:NT], src[:, :, d:NT], src[:, :, 0:NT - d], ALU.add))
                    c.did(e.tensor_copy(dst[:, :, 0:d], src[:, :, 0:d]))
                    c.wait(e)
                    src = dst
                c.did(e.tensor_tensor(loc[:, :, :], src[:, :, :], tot[:, :, :], ALU.subtract))
                c.wait(e)
                c.did(e.tensor_tensor(mine[:, :, :], loc[:, :, :], pC[:, :, :], ALU.add))
                c.wait(e)
                c.did(e.tensor_tensor(mine[:, E:2 * E, :], mine[:, E:2 * E, :],
                                      src[:, 0:E, NT - 1:NT].broadcast_to([P, E, NT]), ALU.add))
                c.wait(e)
                c.did(e.tensor_tensor(loc[:, :, :], mine[:, :, :], S.onehot[:, :, :], ALU.mult))
                c.wait(e)
                for kk in range(2):
                    c.did(e.tensor_reduce(sel[:, kk, :], loc[:, kk * E:(kk + 1) * E, :].rearrange("p x t -> p t x"), AX.X, ALU.add))
                c.wait(e)
                c.did(e.tensor_scalar(t1[:, :, :], sel[:, :, :], -1.0, None, ALU.add))
                c.wait(e)
                c.did(e.tensor_scalar(keep[:, :, :], t1[:, :, :], float(CAP), None, ALU.is_lt))
                c.did(e.scalar_tensor_tensor(out=pos[:, :, :], in0=S.idx[:, :, :], scalar=float(CAP), in1=t1[:, :, :],
                                             op0=ALU.mult, op1=ALU.add))
                c.wait(e)
                c.did(e.tensor_tensor(S.gate[:, :, :], S.gate[:, :, :], keep[:, :, :], ALU.mult))
                c.did(e.tensor_scalar(t2[:, :, :], pos[:, :, :], -float(E * CAP), None, ALU.add))
                c.wait(e)
                c.did(e.tensor_tensor(t3[:, :, :], t2[:, :, :], keep[:, :, :], ALU.mult))
                c.wait(e)
                c.did(e.tensor_scalar(S.row_get[:, :, :], t3[:, :, :], float(E * CAP), None, ALU.add))
                need(e, sp, 1)
                c.did(e.tensor_tensor(t4[:, :, :], pos[:, :, :], spare[:, :, :], ALU.subtract))
                c.wait(e)
                c.did(e.tensor_tensor(off[:, :, :], t4[:, :, :], keep[:, :, :], ALU.mult))
                c.wait(e)
                c.did(e.tensor_tensor(S.row_put[:, :, :], off[:, :, :], spare[:, :, :], ALU.add))
                c.wait(e)
                def work_ahead():
                    for w in ("gamma_b", "beta_b"):
                        e.tensor_scalar(S.w[w][:, :], S.w[w][:, :], S.tg[:, 2:3], None, ALU.mult).then_inc(scaled, 1)
                    for w in range(S.fc.GROUPS):
                        S.fc.take_fc1(e, 0, 0, w)
                    for w in range(S.fc.GROUPS):
                        S.fc.cut_fc2(e, 0, 0, w)

                @loop(e, B // SET)
                def _(i):
                    for j in range(SET):
                        need(e, put[j], 16 * 2 * TPB * i)
                        e.tensor_copy(at[j][:, :, :], S.row_put[:, :, ds((i * SET + j) * TPB, TPB)]).then_inc(listed[j], 1)
                        if isinstance(i, int) and j == SET - 1:
                            work_ahead()
                need(e, scaled, 2)
                e.tensor_tensor(S.X[:, :, :], S.X[:, :, :], over_tiles(S.w["beta_b"], NT), ALU.add).then_inc(scaled, 1)

            @block.gpsimd
            def _(e):
                e.iota(spare[:, :, :], pattern=[[N, 2], [P, NT]], base=E * CAP, channel_multiplier=1,
                       allow_small_or_imprecise_dtypes=True).then_inc(sp, 1)
                recycle(S, e)
                @loop(e, B // SET)
                def _(i):
                    for j in range(SET):
                        need(e, copied[j], i + 1)
                        need(e, listed[j], i + 1)
                        gate(S, e)
                        for kk in range(2):
                            for t in range(TPB):
                                e.indirect_dma_start(S.disp[:, :], bass.IndirectOffsetOnAxis(ap=at[j][:, kk, t:t + 1], axis=0),
                                                     rows[j][:, t, :], None).then_inc(put[j], 16)
                for j in range(SET):
                    need(e, put[j], 16 * 2 * TPB * (B // SET))
    S.sems_ctx.close()
    S.sems_ctx = ExitStack()


class ExpertWeights:
    GROUPS = 4

    def __init__(self, S):
        self.S, self.ctx = S, ExitStack()
        sb = lambda name, shape, dt=F32: self.ctx.enter_context(S.nc.sbuf_tensor(f"fc_{name}", shape, dt))
        parts = lambda name, shape: [sb(f"{name}_{p}", shape, F32R) for p in ("hi", "lo")]
        self.raw1, self.raw2 = sb("raw1", [P, KF, D]), sb("raw2", [P, KF, D])
        self.w1T = [parts(f"w1T{x}", [P, KD, FF]) for x in range(2)]
        self.w2 = [parts(f"w2{x}", [P, KF, D]) for x in range(2)]
        self.pw = [self.ctx.enter_context(S.nc.psum_tensor(f"fc_pw{j}", [P, 4, P], F32)) for j in range(2)]
        self.ldw1, self.ldw2, self.trw, self.wte, self.w2e = (
            S.sem(f"fc_{x}") for x in ("ldw1", "ldw2", "trw", "wte", "w2e"))

    def load_fc1(self, e, n):
        need(e, self.trw, n * self.GROUPS)
        e.dma_start(self.raw1[:, :, :], self.S.a["L0_ffn_fc1_w"][ds(n, 1), :, :].rearrange("o (j p) d -> p (o j) d", p=P)
                    ).then_inc(self.ldw1, 16)

    def load_fc2(self, e, n):
        need(e, self.w2e, n * 2 * self.GROUPS)
        e.dma_start(self.raw2[:, :, :], self.S.a["L0_ffn_fc2_w"][ds(n, 1), :, :].rearrange("o (j p) d -> p (o j) d", p=P)
                    ).then_inc(self.ldw2, 16)

    def turn_fc1(self, e, n, x, w):
        m, k, j0 = n * self.GROUPS + w, w // 2, (w % 2) * 4
        if w == 0:
            need(e, self.ldw1, (n + 1) * 16)
        need(e, self.wte, (m - 1) * 2)
        for j in range(4):
            last = e.transpose(self.pw[w % 2][:, j, :], self.raw1[:, j0 + j, k * P:(k + 1) * P], self.S.ident[:, :])
        last.then_inc(self.trw, 1)

    def take_fc1(self, e, n, x, w):
        m, k, j0 = n * self.GROUPS + w, w // 2, (w % 2) * 4
        need(e, self.trw, m + 1)
        cut(e, self.w1T[x][HI][:, k, j0 * P:(j0 + 4) * P], self.w1T[x][LO][:, k, j0 * P:(j0 + 4) * P],
            self.pw[w % 2][:, :, :], self.wte, 2 * m)

    def cut_fc2(self, e, n, x, w):
        if w == 0:
            need(e, self.ldw2, (n + 1) * 16)
        at = slice(2 * w, 2 * w + 2)
        cut(e, self.w2[x][HI][:, at, :], self.w2[x][LO][:, at, :], self.raw2[:, at, :], self.w2e,
            2 * (n * self.GROUPS + w))


def cut(e, hi, lo, src, count, before):
    e.tensor_copy(hi, src).then_inc(count, 1)
    need(e, count, before + 1)
    e.tensor_tensor(lo, src, hi, ALU.subtract).then_inc(count, 1)


def experts(S):
    nc, a = S.nc, S.a
    ctx, sb, ps, sem = scope(S, "e")
    with ctx:
        parts = lambda name, shape: [sb(f"{name}_{p}", shape, F32R) for p in ("hi", "lo")]
        b2 = [sb(f"b2{x}", [P, D]) for x in range(2)]
        rowsT = [parts(f"rowsT{j}", [P, KD, CHUNK]) for j in range(2)]
        full = [sb(f"full{q}", [P, 2, CHUNK]) for q in range(2)]
        hid = parts("hid", [P, KF, CHUNK])
        rows = [S.w["wq0"], S.w["wk0"]]
        y = [S.w["wv0"], S.w["wo0"]]
        pX = ps("pX", [P, KD, CHUNK])
        pH = [ps(f"pH{j}", [P, 2, CHUNK]) for j in range(KF // 2)]
        pY = ps("pY", [P, 2, D])
        ldb = [sem(f"ldb{x}") for x in range(2)]
        ldr = [sem(f"ldr{j}") for j in range(2)]
        trr, rte, up, act, hi, lo, down, ye = (sem(x) for x in ("trr", "rte", "up", "act", "hi", "lo", "down", "ye"))
        yst = [sem(f"yst{j}", keep=True) for j in range(2)]
        fc, WG = S.fc, S.fc.GROUPS
        w1T, w2 = fc.w1T, fc.w2
        HQ = KF // 2

        def pairs(body):
            def run(e):
                @loop(e, E // 2 - 1)
                def _(i):
                    body(e, i, False)
                body(e, E // 2 - 1, True)
            return run

        with nc.Block() as block:
            @block.sync
            def _(e):
                def load_b2(n, x):
                    need(e, ye, (n - 1) * NCH)
                    e.dma_start(b2[x][:, :], a["L0_ffn_fc2_b"][ds(n, 1), :].broadcast_to([P, D])).then_inc(ldb[x], 16)

                def load_rows(m, j):
                    e.dma_start(rows[j][:, :, :], S.disp[ds(m * CHUNK, CHUNK), :].rearrange("(t p) d -> p t d", p=P)).then_inc(ldr[j], 16)

                def body(e, i, last):
                    for x in range(2):
                        n = i * 2 + x
                        for ch in range(NCH):
                            m, j = n * NCH + ch, (x * NCH + ch) % 2
                            if not (last and x == 1 and ch >= NCH - 2):
                                need(e, trr, m + 1)
                                load_rows(m + 2, j)
                            if ch == NCH - 1 and not last:
                                fc.load_fc1(e, n + 2)
                                fc.load_fc2(e, n + 2)
                                load_b2(n + 2, x)

                load_rows(0, 0)
                load_rows(1, 1)
                load_b2(0, 0)
                load_b2(1, 1)
                pairs(body)(e)

            @block.tensor
            def _(e):
                def turn_rows(m, j, loads):
                    need(e, ldr[j], 16 * loads)
                    need(e, rte, 2 * m)
                    for k in range(KD):
                        for t in range(2):
                            last = e.transpose(pX[:, k, t * P:(t + 1) * P], rows[j][:, t, k * P:(k + 1) * P], S.ident[:, :])
                    last.then_inc(trr, 1)

                def body(e, i, last):
                    for x in range(2):
                        n = i * 2 + x
                        for ch in range(NCH):
                            mi = x * NCH + ch
                            m, j = n * NCH + ch, mi % 2
                            need(e, rte, 2 * m + 2)
                            if ch == 0:
                                need(e, fc.wte, (n + 1) * WG * 2)
                            for q in range(HQ):
                                need(e, act, (m - 1) * HQ + q + 1)
                                for f in (2 * q, 2 * q + 1):
                                    for k in range(KD):
                                        for n_pass, (pl, pr) in enumerate(PASSES):
                                            mm = e.matmul(pH[q][:, f % 2, :], w1T[x][pl][:, k, f * P:(f + 1) * P],
                                                          rowsT[j][pr][:, k, :], start=(k == 0 and n_pass == 0),
                                                          stop=(k == KD - 1 and n_pass == 2))
                                mm.then_inc(up, 1)
                            if not (last and mi == 2 * NCH - 1):
                                turn_rows(m + 1, (mi + 1) % 2, i * NCH + (mi + 1) // 2 + 1)
                            if ch < WG and not (last and x == 1):
                                fc.turn_fc1(e, n + 1, 1 - x, ch)
                            if ch == 0:
                                need(e, fc.w2e, (n + 1) * 2 * WG)
                            need(e, ye, m)
                            for t in range(2):
                                for f in range(KF):
                                    if t == 0 and f % 2 == 0:
                                        need(e, lo, m * HQ + f // 2 + 1)
                                    for n_pass, (pl, pr) in enumerate(PASSES):
                                        mm = e.matmul(pY[:, t, :], hid[pl][:, f, t * P:(t + 1) * P], w2[x][pr][:, f, :],
                                                      start=(f == 0 and n_pass == 0), stop=(f == KF - 1 and n_pass == 2))
                            mm.then_inc(down, 1)

                turn_rows(0, 0, 1)
                pairs(body)(e)

            @block.scalar
            def _(e):
                def body(e, i, last):
                    for x in range(2):
                        n = i * 2 + x
                        for ch in range(NCH):
                            m = n * NCH + ch
                            for q in range(HQ):
                                hq = m * HQ + q
                                need(e, up, hq + 1)
                                need(e, lo, hq - 1)
                                gate(S, e)
                                for f in (2 * q, 2 * q + 1):
                                    ins = e.activation(full[q % 2][:, f % 2, :], pH[q][:, f % 2, :], ACT.Silu,
                                                       bias=S.b1T[:, ds(n * KF + f, 1)])
                                ins.then_inc(act, 1)
                                if q == 0:
                                    need(e, down, m)
                                need(e, act, hq + 1)
                                e.activation(hid[HI][:, 2 * q:2 * q + 2, :], full[q % 2][:, :, :], ACT.Copy).then_inc(hi, 1)
                pairs(body)(e)

            @block.vector
            def _(e):
                def take_rows(m, j):
                    need(e, trr, m + 1)
                    cut(e, rowsT[j][HI][:, :, :], rowsT[j][LO][:, :, :], pX[:, :, :], rte, 2 * m)

                def body(e, i, last):
                    for x in range(2):
                        n = i * 2 + x
                        for ch in range(NCH):
                            mi = x * NCH + ch
                            m, j = n * NCH + ch, mi % 2
                            more = ch < WG and not (last and x == 1)
                            for q in range(HQ):
                                hq = m * HQ + q
                                need(e, hi, hq + 1)
                                e.tensor_tensor(hid[LO][:, 2 * q:2 * q + 2, :], full[q % 2][:, :, :],
                                                hid[HI][:, 2 * q:2 * q + 2, :], ALU.subtract).then_inc(lo, 1)
                                if q == 0 and more:
                                    fc.cut_fc2(e, n + 1, 1 - x, ch)
                            if not (last and mi == 2 * NCH - 1):
                                take_rows(m + 1, (mi + 1) % 2)
                            if more:
                                fc.take_fc1(e, n + 1, 1 - x, ch)
                            need(e, down, m + 1)
                            if ch == 0:
                                need(e, ldb[x], (i + 1) * 16)
                            need(e, yst[j], 16 * (i * NCH + mi // 2))
                            e.tensor_tensor(y[j][:, :, :], pY[:, :, :], over_tiles(b2[x], 2), ALU.add).then_inc(ye, 1)

                take_rows(0, 0)
                pairs(body)(e)

            @block.gpsimd
            def _(e):
                def body(e, i, last):
                    for mi in range(2 * NCH):
                        m = i * 2 * NCH + mi
                        need(e, ye, m + 1)
                        e.dma_start(S.ybuf[ds(m * CHUNK, CHUNK), :].rearrange("(t p) d -> p t d", p=P), y[mi % 2][:, :, :]
                                    ).then_inc(yst[mi % 2], 16)
                pairs(body)(e)
                for j in range(2):
                    need(e, yst[j], 16 * NCH * (E // 2))
    fc.ctx.close()




def combine(S):
    nc = S.nc
    ctx, sb, ps, sem = scope(S, "c")
    with ctx:
        at = [sb(f"at{j}", [P, 2, TPB], I32) for j in range(2)]
        yg = [sb(f"yg{j}", [P, 2, TPB, D]) for j in range(2)]
        acc = sb("acc", [P, 2, TPB, D])
        r = sb("r", [P, TPB, D])
        hn = sb("hn", [P, TPB, D])
        hT = sb("hT", [P, KD, SEQ])
        nb1, nb2 = Norm(S, sb, sem, "1", 1), Norm(S, sb, sem, "2", 2)
        full, rest = sb("full", [P, KD, SEQ]), sb("rest", [P, KD, SEQ])
        sb("below", [P, 2048])
        parts = sb("parts", [P, 3, KD, SEQ], BF16)
        pH, pQ = ps("pH", [P, KD, SEQ]), ps("pQ", [P, KD, SEQ])
        got = [[sem(f"got{j}{kk}", keep=True) for kk in range(2)] for j in range(2)]
        listed, added, centred, upd, trh, hte, qd, cutq, qst = (
            sem(x) for x in ("listed", "added", "centred", "upd", "trh", "hte", "qd", "cutq", "qst"))
        ADDS = 2 * TPB
        FULL, P0, REST, P1, P2 = 1, 2, 3, 4, 5

        with nc.Block() as block:
            @block.gpsimd
            def _(e):
                def list_rows(b, j, k):
                    for kk in range(2):
                        need(e, got[j][kk], 16 * TPB * k)
                    gate(S, e)
                    e.tensor_copy(at[j][:, :, :], S.row_get[:, :, tiles(b)]).then_inc(listed, 1)
                    need(e, listed, b + 1)
                    gate(S, e)
                    need(e, added, (b - 1) * ADDS)
                    gate(S, e)

                def gather(j):
                    for kk in range(2):
                        for t in range(TPB):
                            e.indirect_dma_start(yg[j][:, kk, t, :], None, S.ybuf[:, :],
                                                 bass.IndirectOffsetOnAxis(ap=at[j][:, kk, t:t + 1], axis=0)).then_inc(got[j][kk], 16)

                for b in range(2):
                    list_rows(b, b, 0)
                    gather(b)

                @rounds(e, 0, 2)
                def _(i, j, k):
                    nb1.power(e, i, 0)
                    if inside(i + 2):
                        list_rows(i + 2, j, k + 1)
                        gather(j)
                    nb2.power(e, i, j)

            @block.vector
            def _(e):
                @rounds(e, 2)
                def _(i, j, k):
                    b = i
                    if inside(b):
                        x = S.X[:, tiles(b), :]
                        need(e, centred, b * TPB)
                        for kk in range(2):
                            need(e, got[j][kk], 16 * TPB * (k + 1))
                            for t in range(TPB):
                                e.scalar_tensor_tensor(
                                    out=acc[:, kk, t, :], in0=yg[j][:, kk, t, :], scalar=S.gate[:, kk, ds(b * TPB + t, 1)],
                                    in1=acc[:, 0, t, :] if kk else S.BIG[:, ds(b * TPB + t, 1), :].rearrange("p o d -> p (o d)"),
                                    op0=ALU.mult, op1=ALU.add).then_inc(added, 1)
                            need(e, added, b * ADDS + (kk + 1) * TPB)
                        nb1.stats(e, b, 0, acc[:, 1, :, :])
                        need(e, nb1.agg, (b + 1) * TPB)
                        need(e, upd, b * TPB)
                        for t in range(TPB):
                            e.scalar_tensor_tensor(out=r[:, t, :], in0=acc[:, 1, t, :], scalar=nb1.mv[0][:, t, 0:1],
                                                   in1=S.w["gamma_b"][:, :], op0=ALU.subtract, op1=ALU.mult).then_inc(centred, 1)
                    if inside(i - 1):
                        need(e, trh, i - 1)
                        nb2.apply(e, i - 1, 1 - j, S.X[:, tiles(i - 1), :], hn)
                    if inside(b):
                        need(e, centred, (b + 1) * TPB)
                        need(e, nb1.powed, b + 1)
                        for t in range(TPB):
                            e.scalar_tensor_tensor(out=x[:, t, :], in0=r[:, t, :], scalar=nb1.rstd[0][:, t:t + 1], in1=x[:, t, :],
                                                   op0=ALU.mult, op1=ALU.add).then_inc(upd, 1)
                    if inside(i - 2):
                        need(e, cutq, (i - 2) * P2 + P0)
                        e.tensor_tensor(rest[:, :, :], full[:, :, :], parts[:, 0, :, :], ALU.subtract).then_inc(cutq, 1)
                    if inside(b):
                        need(e, upd, (b + 1) * TPB)
                        nb2.stats(e, b, j, x)
                    if inside(i - 2):
                        need(e, cutq, (i - 2) * P2 + P1)
                        e.tensor_tensor(parts[:, 2, :, :], rest[:, :, :], parts[:, 1, :, :], ALU.subtract).then_inc(cutq, 1)

            @block.tensor
            def _(e):
                @loop(e, B)
                def _(b):
                    nb2.wait(e, b)
                    need(e, hte, b)
                    turn(e, S, pH, hn).then_inc(trh, 1)
                    need(e, hte, b + 1)
                    need(e, cutq, (b - 1) * P2 + FULL)
                    for t in range(KD):
                        for k in range(KD):
                            last = e.matmul(pQ[:, t, :], S.w["wq1"][:, k, t * P:(t + 1) * P], hT[:, k, :],
                                            start=(k == 0), stop=(k == KD - 1))
                    last.then_inc(qd, 1)

            @block.scalar
            def _(e):
                @loop(e, B)
                def _(b):
                    need(e, trh, b + 1)
                    need(e, qd, b)
                    e.activation(hT[:, :, :], pH[:, :, :], ACT.Copy).then_inc(hte, 1)
                    need(e, qd, b + 1)
                    need(e, cutq, b * P2)
                    e.activation(full[:, :, :], pQ[:, :, :], ACT.Copy, scale=0.25).then_inc(cutq, 1)
                    need(e, cutq, b * P2 + FULL)
                    need(e, qst, 96 * b)
                    e.activation(parts[:, 0, :, :], full[:, :, :], ACT.Copy).then_inc(cutq, 1)
                    need(e, cutq, b * P2 + REST)
                    e.activation(parts[:, 1, :, :], rest[:, :, :], ACT.Copy).then_inc(cutq, 1)

            @block.sync
            def _(e):
                @loop(e, B)
                def _(b):
                    need(e, cutq, (b + 1) * P2)
                    for s in range(3):
                        store_part(e, S.qs[1], Q_PLACE[s], b, parts[:, s, :, :], qst)
                S.stored = [(qst, 96)]


EXP_BITS = 0x7F800000


def mask_exponent(e, out, src):
    return e.tensor_scalar(out.bitcast(I32), src.bitcast(I32), EXP_BITS, None, ALU.bitwise_and)


def make_m(e, out, src):
    return e.tensor_scalar(out, src, 2.0 ** -6, 1.5 * 2.0 ** 20, ALU.max, ALU.mult)


def quantised_weight(S):
    return S.w["wk0"][:, 0, :].bitcast(BF16).rearrange("p (k o) -> p k o", k=KD)


def merge(S):
    nc = S.nc
    ctx, sb, ps, sem = scope(S, "m")
    with ctx:
        att = sb("att", [P, TPB, D])
        attT = sb("attT", [P, KD, SEQ])
        nb = Norm(S, sb, sem)
        pA = ps("pA", [P, KD, SEQ])
        pY = ps("pY", [P, TPB, D])
        staged, tra, ate, yd, upd, maxed = (sem(x) for x in ("staged", "tra", "ate", "yd", "upd", "maxed"))

        w = S.w["wq0"]
        wmax, wmaxg, wmaxc, wrec, wscale = (sb(x, [P, 1]) for x in ("wmax", "wmaxg", "wmaxc", "wrec", "wscale"))
        wv, we, wm, wa = (sb(x, [P, KD, D]) for x in ("wv", "we", "wm", "wa"))
        wq = sb("wq", [P, KD, D], BF16)
        pW = ps("pW", [P, KD, D], BF16)
        ldw, wred, wvc, wtr, wte, biased, xb = (sem(x) for x in ("ldw", "wred", "wvc", "wtr", "wte", "biased", "xb"))
        W_STEPS = 10

        with nc.Block() as block:
            @block.sync
            def _(e):
                e.dma_start(w[:, :, :], S.a["L1_ffn_weight"].rearrange("(t p) c -> p t c", p=P)).then_inc(ldw, 16)
                need(e, ldw, 16)

            @block.tensor
            def _(e):
                def turn_attention(b):
                    need(e, staged, b + 1)
                    need(e, ate, b)
                    turn(e, S, pA, att).then_inc(tra, 1)

                turn_attention(0)

                @rounds(e, 0, 1)
                def _(b, j, k):
                    if inside(b + 1):
                        turn_attention(b + 1)
                    need(e, ate, b + 1)
                    need(e, upd, b)
                    apply_weight(e, pY, attT, S.w["wo1"]).then_inc(yd, 1)

                need(e, wvc, W_STEPS)
                for k in range(KD):
                    for t in range(KD):
                        last = e.transpose(pW[:, k, t * P:(t + 1) * P], wq[:, t, k * P:(k + 1) * P], S.identb[:, :])
                last.then_inc(wtr, 1)

            @block.scalar
            def _(e):
                def stage(b):
                    need(e, tra, b)
                    gate(S, e)
                    e.activation(att[:, :, :], S.BIG[:, tiles(b), :], ACT.Copy).then_inc(staged, 1)

                stage(0)

                @rounds(e, 0, 1)
                def _(b, j, k):
                    need(e, tra, b + 1)
                    need(e, yd, b)
                    e.activation(attT[:, :, :], pA[:, :, :], ACT.Copy).then_inc(ate, 1)
                    if inside(b + 1):
                        stage(b + 1)

                need(e, wtr, 1)
                e.activation(quantised_weight(S), pW[:, :, :], ACT.Copy).then_inc(wte, 1)

            @block.gpsimd
            def _(e):
                need(e, wvc, 1)
                e.partition_all_reduce(wmaxg[:, :], wmax[:, :], P, bass.bass_isa.ReduceOp.max).then_inc(wred, 1)

                need(e, biased, 1)

                @rounds(e, 2)
                def _(i, j, k):
                    if inside(i):
                        nb.power(e, i, j)
                    if inside(i - 2):
                        nb.wait(e, i - 2)
                        x = S.X[:, tiles(i - 2), :]
                        gate(S, e)
                        e.tensor_tensor(x, x, over_tiles(S.w["fb_b"]), ALU.add).then_inc(xb, 1)

            @block.vector
            def _(e):
                e.tensor_scalar(S.w["fb_b"][:, :], S.w["fb_b"][:, :], S.tg[:, 3:4], None, ALU.mult).then_inc(biased, 1)
                c = Chain(wvc)
                need(e, ldw, 16)
                c.did(e.tensor_reduce(wmax[:, :], w[:, :, :], AX.XY, ALU.max, apply_absolute_value=True))
                need(e, wred, 1)
                c.did(e.tensor_scalar(wmaxc[:, :], wmaxg[:, :], 1e-12, None, ALU.max))
                c.wait(e)
                c.did(e.reciprocal(wrec[:, :], wmaxc[:, :]))
                c.wait(e)
                c.did(e.tensor_scalar(wscale[:, :], wrec[:, :], FP8_MAX, None, ALU.mult))
                c.wait(e)
                c.did(e.reciprocal(S.wrscale[:, :], wscale[:, :]))
                c.did(e.tensor_scalar(wv[:, :, :], w[:, :, :], wscale[:, 0:1], None, ALU.mult))
                c.wait(e)
                c.did(mask_exponent(e, we[:, :, :], wv[:, :, :]))
                c.wait(e)
                c.did(make_m(e, wm[:, :, :], we[:, :, :]))
                c.wait(e)
                c.did(e.tensor_tensor(wa[:, :, :], wv[:, :, :], wm[:, :, :], ALU.add))
                c.wait(e)
                c.did(e.tensor_tensor(wq[:, :, :], wa[:, :, :], wm[:, :, :], ALU.subtract))
                assert c.k == W_STEPS

                @rounds(e, 1)
                def _(i, j, k):
                    if inside(i):
                        x = S.X[:, tiles(i), :]
                        need(e, yd, i + 1)
                        e.scalar_tensor_tensor(out=x, in0=pY[:, :, :], scalar=S.tg[:, 1:2], in1=x, op0=ALU.mult,
                                               op1=ALU.add).then_inc(upd, 1)
                        need(e, upd, i + 1)
                        nb.stats(e, i, j, x)
                    if inside(i - 1):
                        b = i - 1
                        need(e, staged, b + 1)
                        nb.apply(e, b, 1 - j, S.X[:, tiles(b), :], S.BIG[:, tiles(b), :])
                        nb.wait(e, b)
                        e.tensor_reduce(S.amax[:, ds(b, 1)], S.BIG[:, tiles(b), :], AX.XY, ALU.max,
                                        apply_absolute_value=True).then_inc(maxed, 1)


def quantise(S):
    nc, a = S.nc, S.a
    ctx, sb, ps, sem = scope(S, "q")
    with ctx:
        am, amg, amc, rec, scale, rscale = (sb(x, [P, 1]) for x in ("am", "amg", "amc", "rec", "scale", "rscale"))
        inv1, inv = sb("inv1", [P, 1]), sb("inv", [P, 1])
        v = [sb(f"v{j}", [P, TPB, D]) for j in range(2)]
        m = [sb(f"m{j}", [P, TPB, D]) for j in range(2)]
        big = [sb(f"big{j}", [P, TPB, D]) for j in range(2)]
        vq = [sb(f"vq{j}", [P, TPB, D], BF16) for j in range(2)]
        wqT = quantised_weight(S)
        vqT = sb("vqT", [P, KD, SEQ], BF16)
        t1 = [sb(f"t1{j}", [P, TPB, D]) for j in range(2)]
        o = [sb(f"o{j}", [P, TPB, D]) for j in range(2)]
        pV = ps("pV", [P, KD, SEQ], BF16)
        pY = [ps(f"pY{j}", [P, TPB, D]) for j in range(2)]
        vc, red, vs = sem("vc"), sem("red"), sem("vs")
        sc = [sem(f"sc{j}") for j in range(2)]
        trv, vte, yd, ye, fin = sem("trv"), sem("vte"), sem("yd"), sem("ye"), sem("fin")
        st = [sem(f"st{j}") for j in range(2)]
        MASKED, MADE, ADDED, ROUNDED = 1, 2, 3, 4

        with nc.Block() as block:
            @block.sync
            def _(e):
                @loop(e, B // 2)
                def _(i):
                    for j in range(2):
                        need(e, fin, i * 2 + j + 1)
                        e.dma_start(S.out[ds(i * 2 + j, 1), :, :].rearrange("o (t p) d -> p (o t) d", p=P),
                                    o[j][:, :, :]).then_inc(st[j], 16)
                for j in range(2):
                    need(e, st[j], 16 * (B // 2))

            @block.gpsimd
            def _(e):
                need(e, vc, 1)
                e.partition_all_reduce(amg[:, :], am[:, :], P, bass.bass_isa.ReduceOp.max).then_inc(red, 1)
                @loop(e, B // 2)
                def _(i):
                    for j in range(2):
                        need(e, sc[j], i * ROUNDED + MASKED)
                        gate(S, e)
                        make_m(e, m[j][:, :, :], m[j][:, :, :]).then_inc(sc[j], 1)

            @block.scalar
            def _(e):
                need(e, vc, 7)

                def scaled(b, i, j):
                    need(e, sc[j], (i - 1) * ROUNDED + ADDED)
                    gate(S, e)
                    e.activation(v[j][:, :, :], S.BIG[:, tiles(b), :], ACT.Copy, scale=scale[:, 0:1]).then_inc(vs, 1)

                def take_product(b, j):
                    need(e, yd, b + 1)
                    need(e, fin, b - 1)
                    e.activation(t1[j][:, :, :], pY[j][:, :, :], ACT.Copy, scale=inv[:, 0:1]).then_inc(ye, 1)

                scaled(0, 0, 0)
                scaled(1, 0, 1)

                @rounds(e, 1, 2)
                def _(b, j, i):
                    if inside(b - 1):
                        take_product(b - 1, 1 - j)
                    if inside(b + 2):
                        scaled(b + 2, i + 1, j)
                    if inside(b):
                        need(e, trv, b + 1)
                        need(e, yd, b)
                        e.activation(vqT[:, :, :], pV[:, :, :], ACT.Copy).then_inc(vte, 1)

            @block.tensor
            def _(e):
                @loop(e, B // 2)
                def _(i):
                    for j in range(2):
                        b = i * 2 + j
                        need(e, sc[j], (i + 1) * ROUNDED)
                        need(e, vte, b)
                        for k in range(KD):
                            for t in range(TPB):
                                last = e.transpose(pV[:, k, t * P:(t + 1) * P], vq[j][:, t, k * P:(k + 1) * P], S.identb[:, :])
                        last.then_inc(trv, 1)
                        need(e, vte, b + 1)
                        need(e, ye, b - 1)
                        apply_weight(e, pY[j], vqT, wqT).then_inc(yd, 1)

            @block.vector
            def _(e):
                c = Chain(vc)
                c.did(e.tensor_reduce(am[:, 0:1], S.amax[:, :], AX.X, ALU.max))
                need(e, red, 1)
                c.did(e.tensor_scalar(amc[:, :], amg[:, :], 1e-12, None, ALU.max))
                c.wait(e)
                c.did(e.reciprocal(rec[:, :], amc[:, :]))
                c.wait(e)
                c.did(e.tensor_scalar(scale[:, :], rec[:, :], FP8_MAX, None, ALU.mult))
                c.wait(e)
                c.did(e.reciprocal(rscale[:, :], scale[:, :]))
                c.wait(e)
                c.did(e.tensor_tensor(inv1[:, :], rscale[:, :], S.wrscale[:, :], ALU.mult))
                c.wait(e)
                c.did(e.tensor_tensor(inv[:, :], inv1[:, :], S.tg[:, 3:4], ALU.mult))
                c.wait(e)

                def exponents(b, i, j):
                    need(e, vs, b + 1)
                    need(e, sc[j], i * ROUNDED)
                    mask_exponent(e, m[j][:, :, :], v[j][:, :, :]).then_inc(sc[j], 1)

                def output(b, i, j):
                    need(e, ye, b + 1)
                    need(e, st[j], 16 * i)
                    e.tensor_tensor(o[j][:, :, :], t1[j][:, :, :], S.X[:, tiles(b), :], ALU.add).then_inc(fin, 1)

                exponents(0, 0, 0)

                @rounds(e, 1, 1)
                def _(b, j, i):
                    if inside(b + 1):
                        exponents(b + 1, i + j, 1 - j)
                    if inside(b):
                        need(e, sc[j], i * ROUNDED + MADE)
                        need(e, trv, b)
                        e.tensor_tensor(big[j][:, :, :], v[j][:, :, :], m[j][:, :, :], ALU.add).then_inc(sc[j], 1)
                        need(e, sc[j], i * ROUNDED + ADDED)
                        e.tensor_tensor(vq[j][:, :, :], big[j][:, :, :], m[j][:, :, :], ALU.subtract).then_inc(sc[j], 1)
                    if inside(b - 1):
                        output(b - 1, i + j - 1, 1 - j)


_INS = ['x', 'ctx_1024', 'mask_Bx1xS2_if1', 'g_xattn', 'g_ffn', 'L0_xattn_wq', 'L0_xattn_bq', 'L0_xattn_wk',
        'L0_xattn_bk', 'L0_xattn_wv', 'L0_xattn_bv', 'L0_xattn_wo', 'L0_xattn_bo', 'L0_ffn_wg', 'L0_ffn_fc1_w',
        'L0_ffn_fc1_b', 'L0_ffn_fc2_w', 'L0_ffn_fc2_b', 'L0_ffn_ln_gamma', 'L0_ffn_ln_beta', 'L1_xattn_q_map',
        'L1_xattn_k_map', 'L1_xattn_v_map', 'L1_xattn_output_map', 'L1_ffn_weight', 'L1_ffn_bias']


def kernel(**inputs):
    import numpy as _np
    import concourse.bacc as _bacc
    from concourse import mybir as _mybir
    from concourse.bass_utils import run_bass_kernel_spmd as _run

    nc = _bacc.Bacc("TRN2", target_bir_lowering=False, num_devices=1)
    arrays, args = {}, {}
    for name in _INS:
        v = _np.ascontiguousarray(inputs[name])
        arrays[f"in_{name}"] = v
        args[name] = nc.dram_tensor(f"in_{name}", v.shape, _mybir.dt.from_np(v.dtype), kind="ExternalInput").ap()
    out = nc.dram_tensor("out_x", (B, SEQ, D), _mybir.dt.float32, kind="ExternalOutput").ap()
    build(nc, args, out)
    r = _run(nc, [arrays], core_ids=[0])
    return r.results[0]["out_x"]
```
